# Optimizing a Trainium2 kernel written in Bass

```python
import numpy as np
import jax
import jax.numpy as jnp

def _softmax(x, axis=-1):
    return jax.nn.softmax(x, axis=axis)

def _gelu(x):
    return jax.nn.gelu(x, approximate=True)

def _silu(x):
    return jax.nn.silu(x)

def _sigmoid(x):
    return jax.nn.sigmoid(x)

def _layernorm(x, axis=-1, eps=1e-05):
    m = jnp.mean(x, axis=axis, keepdims=True)
    v = jnp.var(x, axis=axis, keepdims=True)
    return (x - m) / jnp.sqrt(v + eps)

def _scatter_add(tgt, idx, src, axis=0):
    return tgt.at[idx].add(src)

def _segment_sum(src, seg, n):
    return jax.ops.segment_sum(src, seg, n)
kernel_name = 'mk_lm_tower_d2_tok_ids768_r4_847d4d'

def setup_inputs(seed: int=0):
    np.random.seed(seed)
    _w = jnp.asarray

    def _rec_inputs():
        import jax
        import jax.numpy as jnp
        _rk = jax.random.key(seed)
        x = jax.random.randint(jax.random.fold_in(_rk, 1), (64, 128), 0, 7500, jnp.int32)
        itok_BS_0_255 = jax.random.randint(jax.random.fold_in(_rk, 21), (64, 128), 0, 64, jnp.int32)
        mask_BS_i1_0 = jnp.where(jnp.ones((64, 128), dtype=bool), 1, 0).astype(jnp.int32)
        itok_BS_0_511 = jax.random.randint(jax.random.fold_in(_rk, 23), (64, 128), 0, 128, jnp.int32)
        return (x, itok_BS_0_255, mask_BS_i1_0, itok_BS_0_511)
    x, itok_BS_0_255, mask_BS_i1_0, itok_BS_0_511 = _rec_inputs()

    def _L0_tok_setup():
        import jax, jax.numpy as jnp
        import numpy as np
        VOCAB = 7500
        DEMO_VOCAB = 64
        MAX_POS = 128
        SEG_VOCAB = 2
        HIDDEN = 192
        B, S = (64, 128)
        EPS = 1e-12
        key = jax.random.key(seed)
        ks = jax.random.split(key, 12)
        word_ids = jax.random.randint(ks[0], (B, S), 0, VOCAB, dtype=jnp.int32)
        age_ids = jax.random.randint(ks[1], (B, S), 0, DEMO_VOCAB, dtype=jnp.int32)
        bmi_ids = jax.random.randint(ks[2], (B, S), 0, DEMO_VOCAB, dtype=jnp.int32)
        cycle_len_ids = jax.random.randint(ks[3], (B, S), 0, DEMO_VOCAB, dtype=jnp.int32)
        seg_ids = jax.random.randint(ks[4], (B, S), 0, SEG_VOCAB, dtype=jnp.int32)
        posi_ids = jnp.sort(jax.random.randint(ks[5], (B, S), 0, MAX_POS, dtype=jnp.int32), axis=-1)
        word_table = jax.random.normal(ks[6], (VOCAB, HIDDEN), dtype=jnp.float32) * 0.02
        demo_table = jax.random.normal(ks[7], (DEMO_VOCAB, HIDDEN), dtype=jnp.float32) * 0.02
        posi_table = jax.random.normal(ks[8], (MAX_POS, HIDDEN), dtype=jnp.float32) * 0.02
        seg_table = jax.random.normal(ks[9], (SEG_VOCAB, HIDDEN), dtype=jnp.float32) * 0.02
        ln_gamma = jnp.ones((HIDDEN,), dtype=jnp.float32)
        ln_beta = jnp.zeros((HIDDEN,), dtype=jnp.float32)
        return {'word_ids': word_ids, 'age_ids': age_ids, 'bmi_ids': bmi_ids, 'cycle_len_ids': cycle_len_ids, 'seg_ids': seg_ids, 'posi_ids': posi_ids, 'word_table': word_table, 'demo_table': demo_table, 'posi_table': posi_table, 'seg_table': seg_table, 'ln_gamma': ln_gamma, 'ln_beta': ln_beta}
    _L0_tok_all = _L0_tok_setup()
    _L0_tok_in = {k: v for k, v in _L0_tok_all.items() if k in ('word_table', 'demo_table', 'posi_table', 'seg_table', 'ln_gamma', 'ln_beta')}
    del _L0_tok_all

    def _L0_attn_setup():
        import jax, jax.numpy as jnp
        import numpy as np
        N_HEADS = 12
        NEG_BIG = 10000000000.0
        key = jax.random.key(seed)
        ks = jax.random.split(key, 5)
        nb, ns, nf = (4, 512, 192)
        return {'x': jax.random.normal(ks[0], (nb, ns, nf), dtype=jnp.float32), 'Wqkv_w': jax.random.normal(ks[1], (3 * nf, nf), dtype=jnp.float32) * 0.02, 'Wqkv_b': jax.random.normal(ks[2], (3 * nf,), dtype=jnp.float32) * 0.02, 'Wproj_w': jax.random.normal(ks[3], (nf, nf), dtype=jnp.float32) * 0.02, 'Wproj_b': jax.random.normal(ks[4], (nf,), dtype=jnp.float32) * 0.02}
    _L0_attn_all = _L0_attn_setup()
    _L0_attn_in = {k: v for k, v in _L0_attn_all.items() if k in ('Wqkv_w', 'Wqkv_b', 'Wproj_w', 'Wproj_b')}
    del _L0_attn_all

    def _L0_ffn_setup():
        import jax, jax.numpy as jnp
        import numpy as np
        B, N, C, H, E = (8, 256, 192, 768, 4)
        key = jax.random.key(seed)
        ks = jax.random.split(key, 8)
        s_in = 1.0 / np.sqrt(C)
        s_h = 1.0 / np.sqrt(H)
        return {'x': jax.random.normal(ks[0], (B, N, C), dtype=jnp.float32), 'gate_w': jax.random.normal(ks[1], (C, E), dtype=jnp.float32) * 0.01, 'gate_b': jnp.zeros((E,), dtype=jnp.float32), 'gate_center': jnp.zeros((E,), dtype=jnp.float32), 'w1': jax.random.uniform(ks[2], (E, C, H), jnp.float32, -s_in, s_in), 'b1': jax.random.uniform(ks[3], (E, H), jnp.float32, -s_in, s_in), 'w2': jax.random.uniform(ks[4], (E, H, C), jnp.float32, -s_h, s_h), 'b2': jax.random.uniform(ks[5], (E, C), jnp.float32, -s_h, s_h)}
    _L0_ffn_all = _L0_ffn_setup()
    _L0_ffn_in = {k: v for k, v in _L0_ffn_all.items() if k in ('gate_w', 'gate_b', 'gate_center', 'w1', 'b1', 'w2', 'b2')}
    del _L0_ffn_all

    def _L1_attn_setup():
        import jax, jax.numpy as jnp
        import numpy as np
        D_MODEL = 192
        EXPAND = 2
        D_INNER = EXPAND * D_MODEL
        D_STATE = 16
        D_CONV = 4
        DT_RANK = (D_MODEL + 15) // 16
        BATCH, SEQ = (2, 512)

        def _mamba(x, W_in, conv_w, conv_b, W_xproj, W_dt, b_dt, A_log, D_param, W_out):
            Bsz = x.shape[0]
            xz = x @ W_in.T
            xp, z = jnp.split(xz, 2, axis=-1)
            kern = conv_w.T[:, None, :]
            xc = jax.lax.conv_general_dilated(xp, kern, window_strides=(1,), padding=[(D_CONV - 1, 0)], dimension_numbers=('NWC', 'WIO', 'NWC'), feature_group_count=D_INNER) + conv_b
            xc = jax.nn.silu(xc)
            proj = xc @ W_xproj.T
            dt, Bt, Ct = jnp.split(proj, [DT_RANK, DT_RANK + D_STATE], axis=-1)
            dt = jax.nn.softplus(dt @ W_dt.T + b_dt)
            A = -jnp.exp(A_log)

            def step(h, inp):
                dt_t, B_t, C_t, x_t = inp
                dA = jnp.exp(dt_t[..., None] * A)
                h = dA * h + (dt_t * x_t)[..., None] * B_t[:, None, :]
                y = jnp.einsum('bdn,bn->bd', h, C_t)
                return (h, y)
            h0 = jnp.zeros((Bsz, D_INNER, D_STATE), x.dtype)
            inputs = (jnp.swapaxes(dt, 0, 1), jnp.swapaxes(Bt, 0, 1), jnp.swapaxes(Ct, 0, 1), jnp.swapaxes(xc, 0, 1))
            _, ys = jax.lax.scan(step, h0, inputs)
            y = jnp.swapaxes(ys, 0, 1) + xc * D_param
            y = y * jax.nn.silu(z)
            return y @ W_out.T
        key = jax.random.key(seed)
        ks = jax.random.split(key, 10)
        s = lambda k, shape, scale: jax.random.normal(k, shape, dtype=jnp.float32) * scale
        x = s(ks[0], (BATCH, SEQ, D_MODEL), 1.0)
        W_in = s(ks[1], (2 * D_INNER, D_MODEL), D_MODEL ** (-0.5))
        conv_w = s(ks[2], (D_INNER, D_CONV), D_CONV ** (-0.5))
        conv_b = jnp.zeros((D_INNER,), jnp.float32)
        W_xproj = s(ks[3], (DT_RANK + 2 * D_STATE, D_INNER), D_INNER ** (-0.5))
        W_dt = s(ks[4], (D_INNER, DT_RANK), DT_RANK ** (-0.5))
        b_dt = jnp.full((D_INNER,), -4.6, jnp.float32)
        A_log = jnp.log(jnp.broadcast_to(jnp.arange(1, D_STATE + 1, dtype=jnp.float32), (D_INNER, D_STATE)))
        D_param = jnp.ones((D_INNER,), jnp.float32)
        W_out = s(ks[5], (D_MODEL, D_INNER), D_INNER ** (-0.5))
        return {'x': x, 'W_in': W_in, 'conv_w': conv_w, 'conv_b': conv_b, 'W_xproj': W_xproj, 'W_dt': W_dt, 'b_dt': b_dt, 'A_log': A_log, 'D_param': D_param, 'W_out': W_out}
    _L1_attn_all = _L1_attn_setup()
    _L1_attn_in = {k: v for k, v in _L1_attn_all.items() if k in ('W_in', 'conv_w', 'conv_b', 'W_xproj', 'W_dt', 'b_dt', 'A_log', 'D_param', 'W_out')}
    del _L1_attn_all

    def _L1_ffn_setup():
        import jax, jax.numpy as jnp
        import numpy as np
        TOP_K = 2
        key = jax.random.key(seed)
        ks = jax.random.split(key, 8)
        B, S, D, E = (4, 512, 192, 8)
        F = 4 * D
        scale = 0.02
        x = jax.random.normal(ks[0], (B, S, D), dtype=jnp.float32)
        router_w = jax.random.normal(ks[1], (D, E), dtype=jnp.float32) * scale
        router_b = jnp.zeros((E,), dtype=jnp.float32)
        w1 = jax.random.normal(ks[2], (E, D, F), dtype=jnp.float32) * scale
        b1 = jnp.zeros((E, F), dtype=jnp.float32)
        w2 = jax.random.normal(ks[3], (E, F, D), dtype=jnp.float32) * scale
        b2 = jnp.zeros((E, D), dtype=jnp.float32)
        return {'x': x, 'router_w': router_w, 'router_b': router_b, 'w1': w1, 'b1': b1, 'w2': w2, 'b2': b2}
    _L1_ffn_all = _L1_ffn_setup()
    _L1_ffn_in = {k: v for k, v in _L1_ffn_all.items() if k in ('router_w', 'router_b', 'w1', 'b1', 'w2', 'b2')}
    del _L1_ffn_all
    return {'x': x, 'itok_BS_0_255': itok_BS_0_255, 'mask_BS_i1_0': mask_BS_i1_0, 'itok_BS_0_511': itok_BS_0_511, 'L0_tok_word_table': _L0_tok_in['word_table'], 'L0_tok_demo_table': _L0_tok_in['demo_table'], 'L0_tok_posi_table': _L0_tok_in['posi_table'], 'L0_tok_seg_table': _L0_tok_in['seg_table'], 'L0_tok_ln_gamma': _L0_tok_in['ln_gamma'], 'L0_tok_ln_beta': _L0_tok_in['ln_beta'], 'L0_attn_Wqkv_w': _L0_attn_in['Wqkv_w'], 'L0_attn_Wqkv_b': _L0_attn_in['Wqkv_b'], 'L0_attn_Wproj_w': _L0_attn_in['Wproj_w'], 'L0_attn_Wproj_b': _L0_attn_in['Wproj_b'], 'L0_ffn_gate_w': _L0_ffn_in['gate_w'], 'L0_ffn_gate_b': _L0_ffn_in['gate_b'], 'L0_ffn_gate_center': _L0_ffn_in['gate_center'], 'L0_ffn_w1': _L0_ffn_in['w1'], 'L0_ffn_b1': _L0_ffn_in['b1'], 'L0_ffn_w2': _L0_ffn_in['w2'], 'L0_ffn_b2': _L0_ffn_in['b2'], 'L1_attn_W_in': _L1_attn_in['W_in'], 'L1_attn_conv_w': _L1_attn_in['conv_w'], 'L1_attn_conv_b': _L1_attn_in['conv_b'], 'L1_attn_W_xproj': _L1_attn_in['W_xproj'], 'L1_attn_W_dt': _L1_attn_in['W_dt'], 'L1_attn_b_dt': _L1_attn_in['b_dt'], 'L1_attn_A_log': _L1_attn_in['A_log'], 'L1_attn_D_param': _L1_attn_in['D_param'], 'L1_attn_W_out': _L1_attn_in['W_out'], 'L1_ffn_router_w': _L1_ffn_in['router_w'], 'L1_ffn_router_b': _L1_ffn_in['router_b'], 'L1_ffn_w1': _L1_ffn_in['w1'], 'L1_ffn_b1': _L1_ffn_in['b1'], 'L1_ffn_w2': _L1_ffn_in['w2'], 'L1_ffn_b2': _L1_ffn_in['b2']}

def reference(x, itok_BS_0_255, mask_BS_i1_0, itok_BS_0_511, L0_tok_word_table, L0_tok_demo_table, L0_tok_posi_table, L0_tok_seg_table, L0_tok_ln_gamma, L0_tok_ln_beta, L0_attn_Wqkv_w, L0_attn_Wqkv_b, L0_attn_Wproj_w, L0_attn_Wproj_b, L0_ffn_gate_w, L0_ffn_gate_b, L0_ffn_gate_center, L0_ffn_w1, L0_ffn_b1, L0_ffn_w2, L0_ffn_b2, L1_attn_W_in, L1_attn_conv_w, L1_attn_conv_b, L1_attn_W_xproj, L1_attn_W_dt, L1_attn_b_dt, L1_attn_A_log, L1_attn_D_param, L1_attn_W_out, L1_ffn_router_w, L1_ffn_router_b, L1_ffn_w1, L1_ffn_b1, L1_ffn_w2, L1_ffn_b2):
    import jax
    import jax.numpy as jnp

    def _L0_tok_ref(word_ids, age_ids, bmi_ids, cycle_len_ids, seg_ids, posi_ids, word_table, demo_table, posi_table, seg_table, ln_gamma, ln_beta):
        import jax, jax.numpy as jnp
        import numpy as np
        VOCAB = 7500
        DEMO_VOCAB = 64
        MAX_POS = 128
        SEG_VOCAB = 2
        HIDDEN = 192
        B, S = (64, 128)
        EPS = 1e-12
        emb = word_table[word_ids] + seg_table[seg_ids] + posi_table[posi_ids] + demo_table[age_ids] + demo_table[bmi_ids] + demo_table[cycle_len_ids]
        mean = jnp.mean(emb, axis=-1, keepdims=True)
        var = jnp.mean(jnp.square(emb - mean), axis=-1, keepdims=True)
        normed = (emb - mean) * jax.lax.rsqrt(var + EPS)
        out = normed * ln_gamma + ln_beta
        return out

    def _L0_attn_ref(x, Wqkv_w, Wqkv_b, Wproj_w, Wproj_b):
        import jax, jax.numpy as jnp
        import numpy as np
        N_HEADS = 12
        NEG_BIG = 10000000000.0
        nb, ns, nf = x.shape
        hd = nf // N_HEADS
        qkv = x @ Wqkv_w.T + Wqkv_b
        q = qkv[..., :nf]
        q = q.reshape(nb, ns, N_HEADS, hd).transpose(0, 2, 1, 3)
        k = q
        v = q
        w = jnp.einsum('bhqd,bhkd->bhqk', q, k) * (1.0 / jnp.sqrt(jnp.float32(hd)))
        mask = jnp.tril(jnp.ones((ns, ns), dtype=x.dtype))
        w = jax.nn.softmax(w * mask - NEG_BIG * (1.0 - mask), axis=-1)
        a = jnp.einsum('bhqk,bhkd->bhqd', w, v)
        a = a.transpose(0, 2, 1, 3).reshape(nb, ns, nf)
        return a @ Wproj_w.T + Wproj_b

    def _L0_ffn_ref(x, gate_w, gate_b, gate_center, w1, b1, w2, b2):
        import jax, jax.numpy as jnp
        import numpy as np
        B, N, C, H, E = (8, 256, 192, 768, 4)
        b, n, c = x.shape
        scores = jnp.einsum('bnc,ce->bne', x, gate_w) + gate_b
        p_experts = jax.nn.softmax(scores - gate_center, axis=-1)
        expert = jnp.argmax(p_experts, axis=-1).reshape(-1)
        xt = x.reshape(-1, c)
        h = jax.nn.gelu(jnp.einsum('tc,ech->eth', xt, w1) + b1[:, None, :], approximate=False)
        out_all = jnp.einsum('eth,ehc->etc', h, w2) + b2[:, None, :]
        out = jnp.take_along_axis(out_all, expert[None, :, None], axis=0)[0]
        return out.reshape(b, n, c)

    def _L1_attn_ref(x, W_in, conv_w, conv_b, W_xproj, W_dt, b_dt, A_log, D_param, W_out):
        import jax, jax.numpy as jnp
        import numpy as np
        D_MODEL = 192
        EXPAND = 2
        D_INNER = EXPAND * D_MODEL
        D_STATE = 16
        D_CONV = 4
        DT_RANK = (D_MODEL + 15) // 16
        BATCH, SEQ = (2, 512)

        def _mamba(x, W_in, conv_w, conv_b, W_xproj, W_dt, b_dt, A_log, D_param, W_out):
            Bsz = x.shape[0]
            xz = x @ W_in.T
            xp, z = jnp.split(xz, 2, axis=-1)
            kern = conv_w.T[:, None, :]
            xc = jax.lax.conv_general_dilated(xp, kern, window_strides=(1,), padding=[(D_CONV - 1, 0)], dimension_numbers=('NWC', 'WIO', 'NWC'), feature_group_count=D_INNER) + conv_b
            xc = jax.nn.silu(xc)
            proj = xc @ W_xproj.T
            dt, Bt, Ct = jnp.split(proj, [DT_RANK, DT_RANK + D_STATE], axis=-1)
            dt = jax.nn.softplus(dt @ W_dt.T + b_dt)
            A = -jnp.exp(A_log)

            def step(h, inp):
                dt_t, B_t, C_t, x_t = inp
                dA = jnp.exp(dt_t[..., None] * A)
                h = dA * h + (dt_t * x_t)[..., None] * B_t[:, None, :]
                y = jnp.einsum('bdn,bn->bd', h, C_t)
                return (h, y)
            h0 = jnp.zeros((Bsz, D_INNER, D_STATE), x.dtype)
            inputs = (jnp.swapaxes(dt, 0, 1), jnp.swapaxes(Bt, 0, 1), jnp.swapaxes(Ct, 0, 1), jnp.swapaxes(xc, 0, 1))
            _, ys = jax.lax.scan(step, h0, inputs)
            y = jnp.swapaxes(ys, 0, 1) + xc * D_param
            y = y * jax.nn.silu(z)
            return y @ W_out.T
        params = (W_in, conv_w, conv_b, W_xproj, W_dt, b_dt, A_log, D_param, W_out)
        y_fwd = _mamba(x, *params)
        y_bwd = _mamba(x[:, ::-1], *params)[:, ::-1]
        return 0.5 * (y_fwd + y_bwd)

    def _L1_ffn_ref(x, router_w, router_b, w1, b1, w2, b2):
        import jax, jax.numpy as jnp
        import numpy as np
        TOP_K = 2
        E = w1.shape[0]
        logits = jnp.einsum('bsd,de->bse', x, router_w) + router_b
        probs = jax.nn.softmax(logits, axis=-1)
        top_p, top_i = jax.lax.top_k(probs, TOP_K)
        top_p = top_p / jnp.sum(top_p, axis=-1, keepdims=True)
        combine = jnp.sum(jax.nn.one_hot(top_i, E, dtype=x.dtype) * top_p[..., None], axis=-2)
        out = jnp.zeros_like(x)
        for e in range(E):
            h = jax.nn.gelu(jnp.einsum('bsd,df->bsf', x, w1[e]) + b1[e], approximate=False)
            y = jnp.einsum('bsf,fd->bsd', h, w2[e]) + b2[e]
            out = out + combine[..., e:e + 1] * y
        return out
    h = _L0_tok_ref(x, itok_BS_0_255, itok_BS_0_255, itok_BS_0_255, mask_BS_i1_0, itok_BS_0_511, L0_tok_word_table, L0_tok_demo_table, L0_tok_posi_table, L0_tok_seg_table, L0_tok_ln_gamma, L0_tok_ln_beta)
    h = h + _L0_attn_ref(_layernorm(h, axis=-1), L0_attn_Wqkv_w, L0_attn_Wqkv_b, L0_attn_Wproj_w, L0_attn_Wproj_b)
    h = h + _L0_ffn_ref(_layernorm(h, axis=-1), L0_ffn_gate_w, L0_ffn_gate_b, L0_ffn_gate_center, L0_ffn_w1, L0_ffn_b1, L0_ffn_w2, L0_ffn_b2)
    h = h + _L1_attn_ref(_layernorm(h, axis=-1), L1_attn_W_in, L1_attn_conv_w, L1_attn_conv_b, L1_attn_W_xproj, L1_attn_W_dt, L1_attn_b_dt, L1_attn_A_log, L1_attn_D_param, L1_attn_W_out)
    h = h + _L1_ffn_ref(_layernorm(h, axis=-1), L1_ffn_router_w, L1_ffn_router_b, L1_ffn_w1, L1_ffn_b1, L1_ffn_w2, L1_ffn_b2)
    return h

_drawn_inputs = setup_inputs


def setup_inputs(seed=0):
    import zlib

    import numpy as np

    out = dict(_drawn_inputs(seed))
    spreads = {'L0_tok_ln_gamma': (1.0, 0.2),
     'L0_tok_ln_beta': (0.0, 0.1),
     'L0_ffn_gate_b': (0.0, 0.1),
     'L0_ffn_gate_center': (0.0, 0.1),
     'L1_attn_conv_b': (0.0, 0.1),
     'L1_attn_b_dt': (-4.599999904632568, 0.6),
     'L1_attn_D_param': (1.0, 0.2),
     'L1_ffn_router_b': (0.0, 0.1),
     'L1_ffn_b1': (0.0, 0.414),
     'L1_ffn_b2': (0.0, 0.1)}
    factors = {'L0_attn_Wqkv_b': 5.566, 'L0_ffn_b1': 3.348, 'L1_attn_W_dt': 4.509, 'L1_attn_A_log': 4.065}
    for name, (base, spread) in spreads.items():
        noise = np.random.default_rng([zlib.crc32(name.encode()), seed]).standard_normal(out[name].shape)
        drawn = base * np.exp(spread * noise) if base else spread * noise
        out[name] = jnp.asarray(drawn.astype(out[name].dtype))
    for name, factor in factors.items():
        out[name] = (out[name] * factor).astype(out[name].dtype)
    return out
```

```python
from contextlib import ExitStack

import concourse.bass as bass
from concourse import mybir

ALU = mybir.AluOpType
ACT = mybir.ActivationFunctionType
AX = mybir.AxisListType.X
F32 = mybir.dt.float32
BF16 = mybir.dt.bfloat16
I32 = mybir.dt.int32
U32 = mybir.dt.uint32

P = 128
B = 64
C = 192
CR = C - P
G = 4
NG = B // G
TOK = G * P
HEADS, HD = 12, 16
RG = 4
HC = HEADS // RG
HID = 768
HK = HID // P
E0, E1 = 4, 8
BIG = 1.0e10


class Phase(ExitStack):

    def __init__(self, nc):
        super().__init__()
        self.nc, self.sems = nc, []

    def sem(self, name):
        self.sems.append(self.enter_context(self.nc.semaphore(name)))
        return self.sems[-1]

    def __exit__(self, *exc):
        if exc[0] is None and self.sems:
            nums = sorted(s.num for s in self.sems)
            starts = [n for n in nums if n - 1 not in nums]
            ends = [n + 1 for n in nums if n + 1 not in nums]
            with self.nc.Block() as block:
                @block.gpsimd
                def _(pool):
                    for a, b in zip(starts, ends):
                        pool.sem_clear(range(a, b))
        return super().__exit__(*exc)


def stand_alone(eng, go):
    eng.sem_inc(go, 1)


class LayerNorm:

    def __init__(self, nc, ctx, name, eps, K):
        self.nc, self.eps, self.const, self.go = nc, eps, K.mhalf, K.go
        sb = lambda n, s: ctx.enter_context(nc.sbuf_tensor(f"{name}_{n}", s, F32))
        sem = lambda n: ctx.sem(f"{name}_{n}")
        self.bn = sb("bn", [P, G, 6])
        self.mv = sb("mv", [P, G, 2])
        self.ve = sb("ve", [P, G])
        self.rs = sb("rs", [P, G])
        self.bn_done, self.mv_done = sem("bn_done"), sem("mv_done")
        self.eps_done, self.rs_done = sem("eps_done"), sem("rs_done")

    def stats(self, dve, g, src):
        for j in range(G):
            dve.bn_stats(self.bn[:, j, :], src(j)).then_inc(self.bn_done, 1)
        for j in range(G):
            dve.wait_ge(self.bn_done, g * G + j + 1)
            stand_alone(dve, self.go)
            dve.bn_aggr(self.mv[:, j, :], self.bn[:, j, :]).then_inc(self.mv_done, 1)

    def rstd(self, pool, g):
        pool.wait_ge(self.mv_done, g * G + G)
        stand_alone(pool, self.go)
        pool.tensor_scalar(self.ve[:, :], self.mv[:, :, 1], self.eps, None, ALU.add).then_inc(self.eps_done, 1)
        pool.wait_ge(self.eps_done, g + 1)
        pool.tensor_tensor(self.rs[:, :], self.ve[:, :], self.const[:, 0:G], ALU.pow).then_inc(self.rs_done, 1)

    def normalise(self, dve, g, src, dst, done):
        dve.wait_ge(self.rs_done, g + 1)
        for j in range(G):
            dve.tensor_scalar(dst(j), src(j), self.mv[:, j, 0:1], self.rs[:, j:j + 1],
                              ALU.subtract, ALU.mult).then_inc(done, 1)


def constants(nc, ctx, A):
    sb = lambda n, s, dt=F32: ctx.enter_context(nc.sbuf_tensor(n, s, dt))
    sem = lambda n: ctx.sem(n)
    K = type("Constants", (), {})()
    K.ident = sb("ident", [P, P])
    K.identb = sb("identb", [P, P], BF16)
    K.mhalf = sb("mhalf", [P, G])
    K.ones = sb("ones", [P, P])
    K.go = sem("stand_alone")
    zeroed, made = sem("const_zeroed"), sem("const_made")
    with nc.Block() as block:
        @block.gpsimd
        def _(pool):
            pool.memset(K.ident[:, :], 0.0).then_inc(zeroed, 1)
            pool.memset(K.identb[:, :], 0.0).then_inc(zeroed, 1)
            pool.memset(K.mhalf[:, :], -0.5)
            pool.memset(K.ones[:, :], 1.0)
            pool.wait_ge(zeroed, 2)
            for t in (K.ident, K.identb):
                pool.affine_select(out=t[:, :], in_=t[:, :], compare_op=ALU.not_equal, fill=1.0, base=0,
                                   pattern=[[-1, P]], channel_multiplier=1)
    return K


def attention_phase(nc, A, H, bank, K):
    with Phase(nc) as ctx:
        sb = lambda n, s, dt=F32: ctx.enter_context(nc.sbuf_tensor(n, s, dt))
        sem = lambda n: ctx.sem(n)
        posi_t = sb("posi_t", [P, C])
        ds_t = sb("ds_t", [66, C])
        gam, bet = sb("gam", [P, C]), sb("bet", [P, C])
        wqp_a, wqp_b = sb("wqp_a", [P, HC * P]), sb("wqp_b", [CR + 1, HC * P])
        wq_a, wq_b = sb("wq_a", [P, C]), sb("wq_b", [CR + 1, C])
        wo_a, wo_b = sb("wo_a", [P, C]), sb("wo_b", [CR + 1, C])
        mask = sb("mask", [P, HC, P], BF16)
        col_i = sb("col_i", [P, 2], I32)
        col = sb("col", [P, 2])
        mul3 = sb("mul3", [66, 1])
        ids_w = sb("ids_w", [P, B], I32)
        idx = sb("idx", [P, G], I32)
        pid = sb("pid", [P, TOK], I32)
        did = sb("did", [66, TOK], I32)
        oh_p, oh_d = sb("oh_p", [P, TOK]), sb("oh_d", [66, TOK])
        word = sb("word", [P, G, C])
        emb = sb("emb", [P, G, C])
        xn = sb("xn", [P, G, C])
        h1 = sb("h1", [P, G, C])
        z = sb("z", [P, G, C])
        zTa, zTb = sb("zTa", [P, TOK]), sb("zTb", [CR + 1, TOK])
        V = sb("V", [P, G, HEADS, HD + 1])
        qT = sb("qT", [P, HC, TOK])
        NE = 3
        mx = sb("mx", [P, NE, HC])
        S = sb("S", [P, NE, HC, P])
        ST = sb("ST", [P, 2, HC, P])
        ri = sb("ri", [P, 2, HEADS])
        at = sb("at", [P, 2, C])
        aTa, aTb = sb("aTa", [P, 2, P]), sb("aTb", [CR + 1, 2, P])
        ln_e = LayerNorm(nc, ctx, "ln_e", 1e-12, K)
        ln_a = LayerNorm(nc, ctx, "ln_a", 1e-5, K)

        loaded, cleared, mul3_set = sem("a_loaded"), sem("a_cleared"), sem("mul3_set")
        s_ids, s_idx, s_word = sem("ids_in"), sem("idx_ready"), sem("word_in")
        s_onehot, s_embps, s_emb = sem("onehot_ready"), sem("embps_ready"), sem("emb_ready")
        s_xn, s_gam, s_h1, s_h1kept = sem("xn_ready"), sem("gamma_done"), sem("h1_ready"), sem("h1_kept")
        s_z, s_zTps, s_zT = sem("z_ready"), sem("zTps_ready"), sem("zT_ready")
        s_qps, s_q = sem("qps_ready"), sem("q_ready")
        s_sc, s_mx, s_sub, s_exp = sem("scores_ready"), sem("max_ready"), sem("sub_ready"), sem("exp_ready")
        s_pT, s_pTc, s_pv = sem("probsT_ready"), sem("probsT_copied"), sem("pv_ready")
        s_ri, s_at, s_aT, s_aTc = sem("rowsum_inv"), sem("att_ready"), sem("attT_ready"), sem("attT_copied")
        s_pr, s_out = sem("proj_ready"), sem("res_ready")

        OB = (5, 2)
        UN = G * RG

        with nc.Block() as block:
            @block.gpsimd
            def _(pool):
                pool.memset(wqp_a[:, :], 0.0).then_inc(cleared, 1)
                pool.memset(wqp_b[:, :], 0.0).then_inc(cleared, 1)
                pool.memset(mask[:, :, :], 0.0).then_inc(cleared, 1)
                pool.iota(col_i[:, :], pattern=[[0, 2]], base=0, channel_multiplier=1).then_inc(cleared, 1)
                pool.wait_ge(cleared, 4)
                pool.affine_select(out=mask[:, :, :], in_=mask[:, :, :], compare_op=ALU.is_ge,
                                   fill=-4.0 * BIG, base=0, pattern=[[0, HC], [-1, P]], channel_multiplier=1).then_inc(cleared, 1)
                pool.wait_ge(cleared, 5)
                pool.iota(col_i[64:128, 1:2], pattern=[[0, 1]], base=0, channel_multiplier=1).then_inc(cleared, 1)
                pool.wait_ge(cleared, 6)
                pool.tensor_copy(col[:, :], col_i[:, :])
                pool.memset(V[:, :, :, HD:HD + 1], 1.0)

            @block.vector
            def _(dve):
                dve.memset(mul3[:, :], 3.0).then_inc(mul3_set, 1)
                dve.memset(zTb[CR:CR + 1, :], 1.0)
                dve.memset(aTb[CR:CR + 1, :, :], 1.0)
                dve.wait_ge(mul3_set, 1)
                dve.memset(mul3[64:66, :], 1.0)

            @block.sync
            def _(sp):
                n = 0
                sp.wait_ge(cleared, 4)
                for dst, src in (
                    (posi_t[:, :], A["posi_table"]), (ds_t[0:64, :], A["demo_table"]), (ds_t[64:66, :], A["seg_table"]),
                    (gam[:, :], A["ln_gamma"].partition_broadcast(P)), (bet[:, :], A["ln_beta"].partition_broadcast(P)),
                    (wq_a[:, :], A["WqkvT"][0:P, 0:C]), (wq_b[0:CR, :], A["WqkvT"][P:C, 0:C]),
                    (wq_b[CR:CR + 1, :], A["bqkv"][0:1, 0:C]),
                    (wqp_a[:, :].rearrange("p (h x) -> p h x", x=32)[:, :, 0:HD],
                     A["WqkvT"][0:P, 0:C].rearrange("k (h d) -> k h d", d=HD)),
                    (wqp_b[0:CR, :].rearrange("p (h x) -> p h x", x=32)[:, :, 0:HD],
                     A["WqkvT"][P:C, 0:C].rearrange("k (h d) -> k h d", d=HD)),
                    (wqp_b[CR:CR + 1, :].rearrange("p (h x) -> p h x", x=32)[:, :, 0:HD],
                     A["bqkv"][0:1, 0:C].rearrange("k (h d) -> k h d", d=HD)),
                    (wo_a[:, :], A["WprojT"][0:P, :]), (wo_b[0:CR, :], A["WprojT"][P:C, :]),
                    (wo_b[CR:CR + 1, :], A["bproj"]), (ids_w[:, :], A["ids_wordT"]),
                ):
                    sp.dma_start(dst, src).then_inc(loaded, 16)
                    n += 1
                sp.wait_ge(loaded, 16 * n)

        with nc.Block() as block:
            def ids_front(sp, g):
                if not isinstance(g, int) or g > 0:
                    sp.wait_ge(s_onehot, g * 2)
                sl = bass.ds(g * TOK, TOK)
                sp.dma_start(pid[:, :], A["ids_posi"][sl].partition_broadcast(P)).then_inc(s_ids, 16)
                sp.dma_start(did[0:64, :], A["ids_demo"][sl].partition_broadcast(64)).then_inc(s_ids, 16)
                sp.dma_start(did[64:66, :], A["ids_seg"][sl].partition_broadcast(2)).then_inc(s_ids, 16)

            @block.sync
            def _(sp):
                ids_front(sp, 0)
                with sp.Fori(1, NG) as g:
                    ids_front(sp, g)

            def pool_front(pool, g):
                if not isinstance(g, int) or g > 0:
                    pool.wait_ge(s_emb, g * 2)
                pool.tensor_copy(idx[:, :], ids_w[:, bass.ds(g * G, G)]).then_inc(s_idx, 1)
                pool.wait_ge(s_idx, g + 1)
                stand_alone(pool, K.go)
                for j in range(G):
                    pool.indirect_dma_start(word[:, j, :], None, A["word_table"],
                                            bass.IndirectOffsetOnAxis(idx[:, j:j + 1].bitcast(U32), 0)).then_inc(s_word, 16)
                ln_e.rstd(pool, g)
                ln_a.rstd(pool, g)

            @block.gpsimd
            def _(pool):
                pool_front(pool, 0)
                with pool.Fori(1, NG) as g:
                    pool_front(pool, g)

            def dve_front(dve, g):
                later = not isinstance(g, int) or g > 0

                def onehots():
                    dve.wait_ge(s_ids, g * 48 + 48)
                    if later:
                        dve.wait_ge(s_embps, g * 2)
                    dve.tensor_scalar(oh_p[:, :], pid[:, :], col[:, 0:1], None, ALU.is_equal).then_inc(s_onehot, 1)
                    dve.tensor_scalar(oh_d[:, :], did[:, :], col[0:66, 1:2], mul3[:, :], ALU.is_equal,
                                      ALU.mult).then_inc(s_onehot, 1)

                def embed():
                    dve.wait_ge(s_word, g * 64 + 64)
                    for b in range(2):
                        dve.wait_ge(s_embps, g * 2 + b + 1)
                        dve.tensor_tensor(emb[:, 2 * b:2 * b + 2, :],
                                          bank[:, 6 + b, 0:2 * C].rearrange("p (j c) -> p j c", j=2),
                                          word[:, 2 * b:2 * b + 2, :], ALU.add).then_inc(s_emb, 1)
                    dve.wait_ge(s_emb, g * 2 + 2)
                    ln_e.stats(dve, g, lambda j: emb[:, j, :])

                def norm1():
                    ln_e.normalise(dve, g, lambda j: emb[:, j, :], lambda j: xn[:, j, :], s_xn)
                    dve.wait_ge(s_xn, g * G + G)
                    dve.tensor_tensor(xn[:, :, :], xn[:, :, :], gam[:, :].unsqueeze(1).to_broadcast([P, G, C]),
                                      ALU.mult).then_inc(s_gam, 1)
                    dve.wait_ge(s_gam, g + 1)
                    if later:
                        dve.wait_ge(s_h1kept, g)
                    dve.tensor_tensor(h1[:, :, :], xn[:, :, :], bet[:, :].unsqueeze(1).to_broadcast([P, G, C]),
                                      ALU.add).then_inc(s_h1, 1)
                    dve.wait_ge(s_h1, g + 1)
                    ln_a.stats(dve, g, lambda j: h1[:, j, :])

                def norm2():
                    if later:
                        dve.wait_ge(s_zTps, g * 2)
                    ln_a.normalise(dve, g, lambda j: h1[:, j, :], lambda j: z[:, j, :], s_z)

                return [onehots, embed, norm1, norm2]

            def dve_unit(dve, g, u):
                n = g * UN + u
                dve.wait_ge(s_sc, n + 1)
                s_ps = bank[:, u % 2, 0:HC * P].rearrange("p (c k) -> p c k", c=HC)
                if u >= NE or not isinstance(g, int) or g > 0:
                    dve.wait_ge(s_pT, n - NE + 1)
                dve.reduce_max(mx[:, u % NE, :], s_ps, AX).then_inc(s_mx, 1)
                dve.wait_ge(s_mx, n + 1)
                dve.tensor_tensor(S[:, u % NE, :, :], s_ps,
                                  mx[:, u % NE, :].unsqueeze(2).to_broadcast([P, HC, P]),
                                  ALU.subtract).then_inc(s_sub, 1)

            def dve_norm_att(dve, g, j):
                n = g * G + j
                O = bank[:, OB[j % 2], 0:HEADS * (HD + 1)].rearrange("p (h d) -> p h d", h=HEADS)
                dve.wait_ge(s_pv, n + 1)
                dve.reciprocal(ri[:, j % 2, :], O[:, :, HD]).then_inc(s_ri, 1)
                dve.wait_ge(s_ri, n + 1)
                if j >= 2 or not isinstance(g, int) or g > 0:
                    dve.wait_ge(s_aT, n - 1)
                dve.tensor_tensor(at[:, j % 2, :].rearrange("p (h d) -> p h d", h=HEADS), O[:, :, 0:HD],
                                  ri[:, j % 2, :].unsqueeze(2).to_broadcast([P, HEADS, HD]),
                                  ALU.mult).then_inc(s_at, 1)

            def dve_residual(dve, g, j):
                n = g * G + j
                if j == 0:
                    dve.wait_ge(s_h1kept, g + 1)
                dve.wait_ge(s_pr, n + 1)
                hs = H[:, bass.ds(g * G + j, 1), :]
                dve.tensor_tensor(hs, hs, bank[:, OB[j % 2], 256:256 + C].unsqueeze(1), ALU.add).then_inc(s_out, 1)

            def dve_body(dve, g, nxt):
                front = dve_front(dve, nxt) if nxt is not None else []
                for u in range(UN):
                    dve_unit(dve, g, u)
                    if u % RG == 1 and front:
                        front.pop(0)()
                    if u >= 5 and (u - 5) % RG == 0:
                        dve_norm_att(dve, g, (u - 5) // RG)
                    if u >= 7 and (u - 7) % RG == 0:
                        dve_residual(dve, g, (u - 7) // RG)
                dve_norm_att(dve, g, G - 1)
                dve_residual(dve, g, G - 1)

            @block.vector
            def _(dve):
                for step in dve_front(dve, 0):
                    step()
                dve_body(dve, 0, 1)
                with dve.Fori(1, NG - 1) as g:
                    dve_body(dve, g, g + 1)
                dve_body(dve, NG - 1, None)

            def act_keep(act, g):
                act.wait_ge(s_h1, g + 1)
                act.copy(H[:, bass.ds(g * G, G), :], h1[:, :, :]).then_inc(s_h1kept, 1)

            def act_zT(act, g):
                if not isinstance(g, int) or g > 0:
                    act.wait_ge(s_qps, g * 5)
                act.wait_ge(s_zTps, g * 2 + 1)
                act.copy(zTa[:, :], bank[:, 6, :]).then_inc(s_zT, 1)
                act.wait_ge(s_zTps, g * 2 + 2)
                act.copy(zTb[0:CR, :], bank[0:CR, 7, :]).then_inc(s_zT, 1)

            def act_q(act, g):
                for c in range(HC):
                    act.wait_ge(s_qps, g * 5 + c + 1)
                    act.copy(qT[:, c, :], bank[:, 6 + c % 2, :]).then_inc(s_q, 1)
                for b in range(2):
                    act.wait_ge(s_qps, g * 5 + HC + b + 1)
                    act.copy(V[:, 2 * b:2 * b + 2, :, 0:HD],
                             bank[:, 6 + (HC + b) % 2, 0:2 * C].rearrange("p (j h d) -> p j h d", j=2, h=HEADS)).then_inc(s_q, 1)

            def act_exp(act, g, u):
                act.wait_ge(s_sub, g * UN + u + 1)
                act.activation(S[:, u % NE, :, :], S[:, u % NE, :, :], ACT.Exp, scale=HD ** -0.5).then_inc(s_exp, 1)

            def act_pT(act, g, u):
                n = g * UN + u
                act.wait_ge(s_pT, n + 1)
                act.copy(ST[:, u % 2, :, :], bank[:, 3 + u % 2, 0:HC * P].rearrange("p (c k) -> p c k", c=HC)).then_inc(s_pTc, 1)

            def act_aT(act, g, j):
                n = g * G + j
                act.wait_ge(s_aT, n + 1)
                act.copy(aTa[:, j % 2, :], bank[:, 7, 0:P]).then_inc(s_aTc, 1)
                act.copy(aTb[0:CR, j % 2, :], bank[0:CR, 7, P:2 * P]).then_inc(s_aTc, 1)

            def act_body(act, g, nxt):
                act_q(act, g)
                for u in range(UN):
                    act_exp(act, g, u)
                    if u >= 1:
                        act_pT(act, g, u - 1)
                    if u >= 6 and (u - 6) % RG == 0:
                        act_aT(act, g, (u - 6) // RG)
                    if u == 12 and nxt is not None:
                        act_keep(act, nxt)
                act_pT(act, g, UN - 1)
                act_aT(act, g, G - 1)
                if nxt is not None:
                    act_zT(act, nxt)

            @block.scalar
            def _(act):
                act_keep(act, 0)
                act_zT(act, 0)
                act_body(act, 0, 1)
                with act.Fori(1, NG - 1) as g:
                    act_body(act, g, g + 1)
                act_body(act, NG - 1, None)

            def pe_embed(pe, g):
                later = not isinstance(g, int) or g > 0
                pe.wait_ge(s_onehot, g * 2 + 2)
                if later:
                    pe.wait_ge(s_q, g * 5)
                for b in range(2):
                    for j in (2 * b, 2 * b + 1):
                        o = bank[:, 6 + b, (j % 2) * C:(j % 2 + 1) * C]
                        sl = slice(j * P, (j + 1) * P)
                        pe.matmul(o, oh_p[:, sl], posi_t[:, :], start=True, stop=False)
                        mm = pe.matmul(o, oh_d[:, sl], ds_t[:, :], start=False, stop=True)
                    mm.then_inc(s_embps, 1)

            def pe_zT(pe, g):
                pe.wait_ge(s_z, g * G + G)
                pe.wait_ge(s_emb, g * 2 + 2)
                if not isinstance(g, int) or g > 0:
                    pe.wait_ge(s_aTc, g * 2 * G)
                for j in range(G):
                    mm = pe.transpose(bank[:, 6, j * P:(j + 1) * P], z[:, j, 0:P], K.ident[:, :])
                mm.then_inc(s_zTps, 1)
                for j in range(G):
                    mm = pe.transpose(bank[0:CR, 7, j * P:(j + 1) * P], z[:, j, P:C], K.ident[:, :])
                mm.then_inc(s_zTps, 1)

            def pe_q(pe, g):
                pe.wait_ge(s_zT, g * 2 + 2)
                for c in range(HC):
                    if c == 2:
                        pe.wait_ge(s_q, g * 5 + 1)
                    o = bank[:, 6 + c % 2, :]
                    pe.matmul(o, wqp_a[:, c * P:(c + 1) * P], zTa[:, :], start=True, stop=False)
                    pe.matmul(o, wqp_b[:, c * P:(c + 1) * P], zTb[:, :], start=False, stop=True).then_inc(s_qps, 1)
                for b in range(2):
                    pe.wait_ge(s_q, g * 5 + 2 + b)
                    for j in (2 * b, 2 * b + 1):
                        o = bank[:, 6 + (HC + b) % 2, (j % 2) * C:(j % 2 + 1) * C]
                        sl = slice(j * P, (j + 1) * P)
                        pe.matmul(o, zTa[:, sl], wq_a[:, :], start=True, stop=False)
                        mm = pe.matmul(o, zTb[:, sl], wq_b[:, :], start=False, stop=True)
                    mm.then_inc(s_qps, 1)

            def pe_scores(pe, g, u):
                j, r = u // RG, u % RG
                n = g * UN + u
                if u == 0:
                    pe.wait_ge(s_q, g * 5 + 5)
                if u >= 2 or not isinstance(g, int) or g > 0:
                    pe.wait_ge(s_sub, n - 1)
                pe.matmul(bank[:, u % 2, 0:HC * P], K.identb[:, :], mask[:, :, :], start=True, stop=False)
                for c in range(HC):
                    q = qT[32 * r:32 * r + HD, c, j * P:(j + 1) * P]
                    mm = pe.matmul(bank[:, u % 2, c * P:(c + 1) * P], q, q, start=False, stop=(c == HC - 1))
                mm.then_inc(s_sc, 1)

            def pe_probsT(pe, g, u):
                n = g * UN + u
                pe.wait_ge(s_exp, n + 1)
                if u >= 2 or not isinstance(g, int) or g > 0:
                    pe.wait_ge(s_pTc, n - 1)
                for c in range(HC):
                    mm = pe.transpose(bank[:, 3 + u % 2, c * P:(c + 1) * P], S[:, u % NE, c, :], K.ident[:, :])
                mm.then_inc(s_pT, 1)

            def pe_pv(pe, g, u):
                j, r = u // RG, u % RG
                n = g * UN + u
                pe.wait_ge(s_pTc, n + 1)
                if r == 0 and (j >= 2 or not isinstance(g, int) or g > 0):
                    pe.wait_ge(s_out, g * G + j - 1)
                for c in range(HC):
                    h = RG * c + r
                    o = h * (HD + 1)
                    mm = pe.matmul(bank[:, OB[j % 2], o:o + HD + 1], ST[:, u % 2, c, :], V[:, j, h, :], start=True, stop=True)
                if r == RG - 1:
                    mm.then_inc(s_pv, 1)

            def pe_aT(pe, g, j, embedded):
                n = g * G + j
                pe.wait_ge(s_emb, (embedded + 1) * 2)
                pe.wait_ge(s_at, n + 1)
                if j >= 1 or not isinstance(g, int) or g > 0:
                    pe.wait_ge(s_aTc, 2 * n)
                pe.transpose(bank[:, 7, 0:P], at[:, j % 2, 0:P], K.ident[:, :])
                pe.transpose(bank[0:CR, 7, P:2 * P], at[:, j % 2, P:C], K.ident[:, :]).then_inc(s_aT, 1)

            def pe_proj(pe, g, j):
                n = g * G + j
                pe.wait_ge(s_aTc, 2 * n + 2)
                o = bank[:, OB[j % 2], 256:256 + C]
                pe.matmul(o, aTa[:, j % 2, :], wo_a[:, :], start=True, stop=False)
                pe.matmul(o, aTb[:, j % 2, :], wo_b[:, :], start=False, stop=True).then_inc(s_pr, 1)

            def pe_body(pe, g, nxt):
                pe_q(pe, g)
                for u in range(UN):
                    pe_scores(pe, g, u)
                    if u >= 1:
                        pe_probsT(pe, g, u - 1)
                    if u >= 2:
                        pe_pv(pe, g, u - 2)
                    if u >= 6 and (u - 6) % RG == 0:
                        pe_aT(pe, g, (u - 6) // RG, g if nxt is None else nxt)
                    if u >= 7 and (u - 7) % RG == 0:
                        pe_proj(pe, g, (u - 7) // RG)
                    if u == 3 and nxt is not None:
                        pe_embed(pe, nxt)
                pe_probsT(pe, g, UN - 1)
                pe_pv(pe, g, UN - 2)
                pe_pv(pe, g, UN - 1)
                pe_aT(pe, g, G - 1, g if nxt is None else nxt)
                pe_proj(pe, g, G - 1)
                if nxt is not None:
                    pe_zT(pe, nxt)

            @block.tensor
            def _(pe):
                pe_embed(pe, 0)
                pe_zT(pe, 0)
                pe_body(pe, 0, 1)
                with pe.Fori(1, NG - 1) as g:
                    pe_body(pe, g, g + 1)
                pe_body(pe, NG - 1, None)


def expert_phase(nc, name, A, H, bank, K, E, top, center, X, Y):
    NT = top * B * P // TOK + E - 1
    NJ = B * P // TOK
    with Phase(nc) as ctx:
        sb = lambda n, s, dt=F32: ctx.enter_context(nc.sbuf_tensor(f"{name}_{n}", s, dt))
        sem = lambda n: ctx.sem(f"{name}_{n}")
        pos_i = sb("pos_i", [P, top, B], I32)
        wgt = sb("wgt", [P, top, B])
        ex_i = sb("ex_i", [1, NT], I32)

        with Phase(nc) as c2:
            sb2 = lambda n, s, dt=F32: c2.enter_context(nc.sbuf_tensor(f"{name}_{n}", s, dt))
            Z = sb2("Z", [P, B, C])
            L = sb2("L", [P, E, B])
            router_pass(nc, name, A, H, bank, K, E, Z, L)
            routing(nc, name, A, bank, K, E, top, center, NT, NJ, L, pos_i, wgt, ex_i)
            scatter_rows(nc, name, top, Z, pos_i, X)
        X, Y = X[0:NT * TOK, :], Y[0:NT * TOK, :]
        expert_tiles(nc, name, A, bank, K, NT, ex_i, X, Y)
        combine(nc, name, H, top, pos_i, wgt, Y)


def router_pass(nc, name, A, H, bank, K, E, Z, L):
    with Phase(nc) as ctx:
        sb = lambda n, s, dt=F32: ctx.enter_context(nc.sbuf_tensor(f"{name}r_{n}", s, dt))
        sem = lambda n: ctx.sem(f"{name}r_{n}")
        gw_a, gw_b = sb("gw_a", [P, E]), sb("gw_b", [CR + 1, E])
        z = sb("z", [P, G, C])
        zTa, zTb = sb("zTa", [P, TOK]), sb("zTb", [CR + 1, TOK])
        ln = LayerNorm(nc, ctx, name + "_ln", 1e-5, K)
        loaded, ones = sem("loaded"), sem("ones")
        s_z, s_kept, s_zTps, s_zT, s_lg, s_L = (sem(n) for n in ("z_ready", "z_kept", "zTps_ready", "zT_ready", "logits_ready", "logits_kept"))

        with nc.Block() as block:
            @block.sync
            def _(sp):
                for dst, src in ((gw_a[:, :], A[name + "_gate"][0:P, :]), (gw_b[0:CR, :], A[name + "_gate"][P:C, :]),
                                 (gw_b[CR:CR + 1, :], A[name + "_gate_b"])):
                    sp.dma_start(dst, src).then_inc(loaded, 16)

            @block.gpsimd
            def _(pool):
                ln.rstd(pool, 0)
                with pool.Fori(1, NG) as g:
                    ln.rstd(pool, g)

            def dve_step(dve, g):
                later = not isinstance(g, int) or g > 0
                h = lambda j: H[:, bass.ds(g * G + j, 1), :].rearrange("p a c -> p (a c)")
                ln.stats(dve, g, h)
                if later:
                    dve.wait_ge(s_zTps, g * 2)
                    dve.wait_ge(s_kept, g)
                ln.normalise(dve, g, h, lambda j: z[:, j, :], s_z)

            @block.vector
            def _(dve):
                dve.memset(zTb[CR:CR + 1, :], 1.0).then_inc(ones, 1)
                dve_step(dve, 0)
                with dve.Fori(1, NG) as g:
                    dve_step(dve, g)

            def act_step(act, g):
                act.wait_ge(s_z, g * G + G)
                act.copy(Z[:, bass.ds(g * G, G), :], z[:, :, :]).then_inc(s_kept, 1)
                if not isinstance(g, int) or g > 0:
                    act.wait_ge(s_lg, g)
                act.wait_ge(s_zTps, g * 2 + 1)
                act.copy(zTa[:, :], bank[:, 0, :]).then_inc(s_zT, 1)
                act.wait_ge(s_zTps, g * 2 + 2)
                act.copy(zTb[0:CR, :], bank[0:CR, 1, :]).then_inc(s_zT, 1)
                act.wait_ge(s_lg, g + 1)
                act.copy(L[:, :, bass.ds(g * G, G)], bank[:, 2, 0:G * E].rearrange("p (j e) -> p e j", j=G)).then_inc(s_L, 1)

            @block.scalar
            def _(act):
                act_step(act, 0)
                with act.Fori(1, NG) as g:
                    act_step(act, g)

            def pe_step(pe, g):
                later = not isinstance(g, int) or g > 0
                pe.wait_ge(s_z, g * G + G)
                if later:
                    pe.wait_ge(s_zT, g * 2)
                for j in range(G):
                    mm = pe.transpose(bank[:, 0, j * P:(j + 1) * P], z[:, j, 0:P], K.ident[:, :])
                mm.then_inc(s_zTps, 1)
                for j in range(G):
                    mm = pe.transpose(bank[0:CR, 1, j * P:(j + 1) * P], z[:, j, P:C], K.ident[:, :])
                mm.then_inc(s_zTps, 1)
                pe.wait_ge(s_zT, g * 2 + 2)
                if later:
                    pe.wait_ge(s_L, g)
                for j in range(G):
                    sl = slice(j * P, (j + 1) * P)
                    o = bank[:, 2, j * E:(j + 1) * E]
                    pe.matmul(o, zTa[:, sl], gw_a[:, :], start=True, stop=False)
                    mm = pe.matmul(o, zTb[:, sl], gw_b[:, :], start=False, stop=True)
                mm.then_inc(s_lg, 1)

            @block.tensor
            def _(pe):
                pe.wait_ge(loaded, 48)
                pe.wait_ge(ones, 1)
                pe_step(pe, 0)
                with pe.Fori(1, NG) as g:
                    pe_step(pe, g)


def routing(nc, name, A, bank, K, E, top, center, NT, NJ, L, pos_i, wgt, ex_i):
    with Phase(nc) as ctx:
        sb = lambda n, s, dt=F32: ctx.enter_context(nc.sbuf_tensor(f"{name}q_{n}", s, dt))
        sem = lambda n: ctx.sem(f"{name}q_{n}")
        tri = sb("tri", [P, P])
        irow = sb("irow", [P, 64], I32)
        row = sb("row", [P, 64])
        prio, lim, cen = sb("prio", [P, E]), sb("lim", [P, NJ]), sb("cen", [P, E])
        keep = sb("keep", [P, E, B])
        m = sb("m", [P, 2, B])
        pm = sb("pm", [P, B])
        oh = sb("oh", [P, 2, E, B])
        tmp = sb("tmp", [P, E, B])
        Aall = sb("Aall", [P, E, B])
        cnt, incl, pos = sb("cnt", [P, E, B]), sb("incl", [P, E, B]), sb("pos", [P, E, B])
        gt = sb("gt", [P, E, NJ])
        tiles, tincl, tbase, one = sb("tiles", [P, E]), sb("tincl", [P, E]), sb("tbase", [P, E]), sb("one", [P, E])
        exc = sb("exc", [1, NT, E])
        exf = sb("exf", [1, NT])
        posf = sb("posf", [P, B])
        ew, den = sb("ew", [P, B]), sb("den", [P, B])
        s_tri, s_row, s_cen = sem("tri_zeroed"), sem("rows_ready"), sem("center_in")
        s_dif, s_exp, s_all, s_rank, s_step = sem("margin_ready"), sem("exp_ready"), sem("choice_ready"), sem("ranks_ready"), sem("dve_step")

        def over_e(x):
            return x.rearrange("p e t -> p t e")

        with nc.Block() as block:
            @block.gpsimd
            def _(pool):
                pool.memset(tri[:, :], 1.0).then_inc(s_tri, 1)
                pool.iota(irow[:, :], pattern=[[1, 64]], base=0, channel_multiplier=0).then_inc(s_tri, 1)
                pool.wait_ge(s_tri, 2)
                pool.affine_select(out=tri[:, :], in_=tri[:, :], compare_op=ALU.is_gt, fill=0.0, base=0,
                                   pattern=[[1, P]], channel_multiplier=-1).then_inc(s_row, 1)
                pool.tensor_copy(row[:, :], irow[:, :]).then_inc(s_row, 1)

            if center:
                @block.sync
                def _(sp):
                    sp.dma_start(cen[:, :], A[center].partition_broadcast(P)).then_inc(s_cen, 16)

            @block.scalar
            def _(act):
                if top == 2:
                    act.wait_ge(s_dif, 1)
                    act.activation(ew[:, :], posf[:, :], ACT.Exp).then_inc(s_exp, 1)

            @block.tensor
            def _(pe):
                pe.wait_ge(s_all, 1)
                pe.wait_ge(s_row, 2)
                a = Aall[:, :, :].rearrange("p e t -> p (e t)")
                pe.matmul(bank[:, 0, 0:E * B], tri[:, :], a, start=True, stop=True)
                pe.matmul(bank[:, 1, 0:E * B], K.ones[:, :], a, start=True, stop=True).then_inc(s_rank, 1)

            @block.vector
            def _(dve):
                done = [0]

                def step(ins):
                    done[0] += 1
                    ins.then_inc(s_step, 1)
                    dve.wait_ge(s_step, done[0])

                dve.wait_ge(s_row, 2)
                step(dve.tensor_scalar(prio[:, :], row[:, 0:E], -1.0, float(E), ALU.mult, ALU.add))
                step(dve.tensor_scalar(lim[:, :], row[:, 0:NJ], float(TOK), None, ALU.mult))
                step(dve.memset(one[:, :], 1.0))
                step(dve.memset(keep[:, :, :], 1.0))
                step(dve.memset(keep[:, :, 0:1], 0.0))
                if center:
                    dve.wait_ge(s_cen, 16)
                    step(dve.tensor_tensor(L[:, :, :], L[:, :, :], cen[:, :].unsqueeze(2).to_broadcast([P, E, B]), ALU.subtract))
                for k in range(top):
                    step(dve.reduce_max(m[:, k, :], over_e(L[:, :, :]), AX))
                    mk = m[:, k, :].unsqueeze(1).to_broadcast([P, E, B])
                    pb = prio[:, :].unsqueeze(2).to_broadcast([P, E, B])
                    step(dve.tensor_tensor(tmp[:, :, :], L[:, :, :], mk, ALU.is_equal))
                    step(dve.tensor_tensor(tmp[:, :, :], tmp[:, :, :], pb, ALU.mult))
                    step(dve.reduce_max(pm[:, :], over_e(tmp[:, :, :]), AX))
                    step(dve.tensor_tensor(oh[:, k, :, :], pb, pm[:, :].unsqueeze(1).to_broadcast([P, E, B]), ALU.is_equal))
                    if k == 0 and top == 2:
                        step(dve.scalar_tensor_tensor(L[:, :, :], oh[:, 0, :, :], -1.0e30, L[:, :, :], ALU.mult, ALU.add))
                if top == 2:
                    step(dve.tensor_tensor(posf[:, :], m[:, 1, :], m[:, 0, :], ALU.subtract))
                    dve.sem_inc(s_dif, 1)
                    step(dve.tensor_tensor(Aall[:, :, :], oh[:, 0, :, :], oh[:, 1, :, :], ALU.add))
                else:
                    step(dve.tensor_copy(Aall[:, :, :], oh[:, 0, :, :]))
                dve.sem_inc(s_all, 1)
                if top == 2:
                    dve.wait_ge(s_exp, 1)
                    step(dve.tensor_scalar(den[:, :], ew[:, :], 1.0, None, ALU.add))
                    step(dve.reciprocal(wgt[:, 0, :], den[:, :]))
                    step(dve.tensor_tensor(wgt[:, 1, :], ew[:, :], wgt[:, 0, :], ALU.mult))
                dve.wait_ge(s_rank, 1)
                flat = lambda x: x[:, :, :].rearrange("p e t -> p (e t)")
                step(dve.tensor_copy(flat(cnt), bank[:, 1, 0:E * B]))
                step(dve.tensor_tensor_scan(flat(incl), flat(keep), flat(cnt), 0.0, ALU.mult, ALU.add))
                step(dve.tensor_tensor(flat(pos), bank[:, 0, 0:E * B], flat(incl), ALU.add))
                step(dve.tensor_tensor(flat(pos), flat(pos), flat(cnt), ALU.subtract))
                total = incl[:, :, B - 1:B]
                step(dve.tensor_tensor(gt[:, :, :], total.to_broadcast([P, E, NJ]),
                                       lim[:, :].unsqueeze(1).to_broadcast([P, E, NJ]), ALU.is_gt))
                step(dve.reduce_sum(tiles[:, :], gt[:, :, :], AX))
                step(dve.tensor_tensor_scan(tincl[:, :], one[:, :], tiles[:, :], 0.0, ALU.mult, ALU.add))
                step(dve.tensor_tensor(tbase[:, :], tincl[:, :], tiles[:, :], ALU.subtract))
                step(dve.scalar_tensor_tensor(pos[:, :, :], tbase[:, :].unsqueeze(2).to_broadcast([P, E, B]), float(TOK),
                                              pos[:, :, :], ALU.mult, ALU.add))
                for k in range(top):
                    step(dve.tensor_tensor(tmp[:, :, :], oh[:, k, :, :], pos[:, :, :], ALU.mult))
                    step(dve.reduce_sum(posf[:, :], over_e(tmp[:, :, :]), AX))
                    step(dve.tensor_copy(pos_i[:, k, :], posf[:, :]))
                step(dve.tensor_tensor(exc[:, :, :], row[0:1, 0:NT].unsqueeze(2).to_broadcast([1, NT, E]),
                                       tincl[0:1, :].unsqueeze(1).to_broadcast([1, NT, E]), ALU.is_ge))
                step(dve.reduce_sum(exf[:, :], exc[:, :, :], AX))
                step(dve.tensor_scalar(ex_i[:, :], exf[:, :], float(E - 1), None, ALU.min))


def scatter_rows(nc, name, top, Z, pos_i, X):
    with Phase(nc) as ctx:
        sb = lambda n, s, dt=F32: ctx.enter_context(nc.sbuf_tensor(f"{name}s_{n}", s, dt))
        sem = lambda n: ctx.sem(f"{name}s_{n}")
        st = [sb(f"st{b}", [P, G, C]) for b in range(2)]
        idx = [sb(f"idx{b}", [P, top, G], I32) for b in range(2)]
        s_st, s_idx = sem("staged"), sem("idx_ready")
        s_sc = [sem(f"scattered{b}") for b in range(2)]
        n_dma = 16 * top * G

        def scatter(pool, i, b):
            g = i * 2 + b
            if not isinstance(i, int) or i > 0:
                pool.wait_ge(s_sc[b], i * n_dma)
            pool.tensor_copy(idx[b][:, :, :], pos_i[:, :, bass.ds(g * G, G)]).then_inc(s_idx, 1)
            pool.wait_ge(s_idx, g + 1)
            pool.wait_ge(s_st, g + 1)
            pool.sem_inc(s_alone, 1)
            for j in range(G):
                for k in range(top):
                    pool.indirect_dma_start(X, bass.IndirectOffsetOnAxis(idx[b][:, k, j:j + 1].bitcast(U32), 0),
                                            st[b][:, j, :], None).then_inc(s_sc[b], 16)

        s_alone = sem("stand_alone")
        with nc.Block() as block:
            @block.scalar
            def _(act):
                def pair(i):
                    for b in range(2):
                        if not isinstance(i, int) or i > 0:
                            act.wait_ge(s_sc[b], i * n_dma)
                            act.sem_inc(s_alone, 1)
                        act.copy(st[b][:, :, :], Z[:, bass.ds(i * (2 * G) + b * G, G), :]).then_inc(s_st, 1)
                pair(0)
                with act.Fori(1, NG // 2) as i:
                    pair(i)

            @block.gpsimd
            def _(pool):
                for b in range(2):
                    scatter(pool, 0, b)
                with pool.Fori(1, NG // 2) as i:
                    for b in range(2):
                        scatter(pool, i, b)
                for b in range(2):
                    pool.wait_ge(s_sc[b], NG // 2 * n_dma)


def expert_tiles(nc, name, A, bank, K, NT, ex_i, X, Y):
    with Phase(nc) as ctx:
        sb = lambda n, s, dt=F32: ctx.enter_context(nc.sbuf_tensor(f"{name}t_{n}", s, dt))
        sem = lambda n: ctx.sem(f"{name}t_{n}")
        two = range(2)
        w1a, w1b = [sb(f"w1a{b}", [P, HID]) for b in two], [sb(f"w1b{b}", [CR + 1, HID]) for b in two]
        w2, b2 = [sb(f"w2{b}", [P, HK, C]) for b in two], [sb(f"b2{b}", [P, C]) for b in two]
        x = [sb(f"x{b}", [P, G, C]) for b in two]
        y = [sb(f"y{b}", [P, G, C]) for b in two]
        xTa, xTb = [sb(f"xTa{b}", [P, TOK]) for b in two], [sb(f"xTb{b}", [CR + 1, TOK]) for b in two]
        h = [sb(f"h{b}", [P, HK, TOK]) for b in two]
        s_w, s_x, s_yout = ([sem(f"{n}{b}") for b in two] for n in ("w_in", "x_in", "y_stored"))
        s_ones, s_xTps, s_xT, s_h, s_gelu, s_yps, s_y = (
            sem(n) for n in ("ones", "xTps_ready", "xT_ready", "hidden_ready", "gelu_ready", "yps_ready", "y_ready"))
        Xv = X.rearrange("(s p j) c -> p s (j c)", p=P, j=G)
        Yv = Y.rearrange("(s p j) c -> p s (j c)", p=P, j=G)
        W1, B1, W2, B2 = (A[f"{name}_{n}"] for n in ("w1", "b1", "w2", "b2"))
        YB = (5, 6)

        def tiles(step):
            step(0, 0)
            step(0, 1)
            yield 1, NT // 2
            if NT % 2:
                step(NT // 2, 0)

        def run(eng, step):
            for lo, hi in tiles(step):
                with eng.Fori(lo, hi) as i:
                    step(i, 0)
                    step(i, 1)

        with nc.Block() as block:
            @block.sync
            def _(sp):
                def load(i, b):
                    s = i * 2 + b
                    e = sp.value_load(ex_i[0:1, bass.ds(s, 1)], min_val=0, max_val=A[f"{name}_w1"].shape[0] - 1)
                    if not isinstance(i, int) or i > 0:
                        sp.wait_ge(s_xTps, s * 2 - 2)
                    sp.dma_start(x[b][:, :, :].rearrange("p j c -> p (j c)"),
                                 Xv[:, bass.ds(s, 1), :].rearrange("p s n -> p (s n)")).then_inc(s_x[b], 16)
                    if not isinstance(i, int) or i > 0:
                        sp.wait_ge(s_y, (s - 1) * G)
                    sp.dma_start(w1a[b][:, :], W1[bass.ds(e, 1), 0:P, :].rearrange("a k n -> k (a n)")).then_inc(s_w[b], 16)
                    sp.dma_start(w1b[b][0:CR, :], W1[bass.ds(e, 1), P:C, :].rearrange("a k n -> k (a n)")).then_inc(s_w[b], 16)
                    sp.dma_start(w1b[b][CR:CR + 1, :], B1[bass.ds(e, 1), :]).then_inc(s_w[b], 16)
                    sp.dma_start(w2[b][:, :, :], W2[bass.ds(e, 1), :, :].rearrange("a (m p) c -> p (a m) c", p=P)).then_inc(s_w[b], 16)
                    sp.dma_start(b2[b][:, :], B2[bass.ds(e, 1), :].rearrange("a c -> (a c)").partition_broadcast(P)).then_inc(s_w[b], 16)
                run(sp, load)

            @block.gpsimd
            def _(pool):
                def store(i, b):
                    s = i * 2 + b
                    pool.wait_ge(s_y, s * G + G)
                    pool.dma_start(Yv[:, bass.ds(s, 1), :].rearrange("p s n -> p (s n)"),
                                   y[b][:, :, :].rearrange("p j c -> p (j c)")).then_inc(s_yout[b], 16)
                run(pool, store)
                for b in two:
                    pool.wait_ge(s_yout[b], 16 * ((NT + 1 - b) // 2))

            @block.vector
            def _(dve):
                def xT(i, b):
                    s = i * 2 + b
                    dve.wait_ge(s_xTps, s * 2 + 1)
                    if not isinstance(i, int) or i > 0:
                        dve.wait_ge(s_h, s * HK - HK)
                    dve.tensor_copy(xTa[b][:, :], bank[:, 0, :]).then_inc(s_xT, 1)
                    dve.wait_ge(s_xTps, s * 2 + 2)
                    dve.tensor_copy(xTb[b][0:CR, :], bank[0:CR, 1, :]).then_inc(s_xT, 1)

                def out(i, b):
                    s = i * 2 + b
                    if not isinstance(i, int) or i > 0:
                        dve.wait_ge(s_yout[b], i * 16)
                    for j in range(G):
                        dve.wait_ge(s_yps, s * G + j + 1)
                        dve.tensor_tensor(y[b][:, j, :], bank[:, YB[j % 2], 0:C], b2[b][:, :], ALU.add).then_inc(s_y, 1)

                for b in two:
                    dve.memset(xTb[b][CR:CR + 1, :], 1.0).then_inc(s_ones, 1)
                xT(0, 0)
                xT(0, 1)
                out(0, 0)
                def pair(i):
                    xT(i, 0)
                    out(i - 1, 1)
                    xT(i, 1)
                    out(i, 0)

                pair(1)
                with dve.Fori(2, NT // 2) as i:
                    pair(i)
                if NT % 2:
                    xT(NT // 2, 0)
                out(NT // 2 - 1, 1)
                if NT % 2:
                    out(NT // 2, 0)

            @block.scalar
            def _(act):
                def gelus(i, b):
                    s = i * 2 + b
                    if not isinstance(i, int) or i > 0:
                        act.wait_ge(s_yps, s * G - G)
                    for m in range(HK):
                        act.wait_ge(s_h, s * HK + m + 1)
                        act.activation(h[b][:, m, :], bank[:, 2 + m % 3, :], ACT.Gelu).then_inc(s_gelu, 1)
                run(act, gelus)

            @block.tensor
            def _(pe):
                def transposes(i, b):
                    s = i * 2 + b
                    pe.wait_ge(s_x[b], i * 16 + 16)
                    if not (isinstance(i, int) and i == 0 and b == 0):
                        pe.wait_ge(s_xT, s * 2)
                    for j in range(G):
                        mm = pe.transpose(bank[:, 0, j * P:(j + 1) * P], x[b][:, j, 0:P], K.ident[:, :])
                    mm.then_inc(s_xTps, 1)
                    for j in range(G):
                        mm = pe.transpose(bank[0:CR, 1, j * P:(j + 1) * P], x[b][:, j, P:C], K.ident[:, :])
                    mm.then_inc(s_xTps, 1)

                def first(i, b):
                    s = i * 2 + b
                    pe.wait_ge(s_w[b], i * 80 + 80)
                    pe.wait_ge(s_xT, s * 2 + 2)
                    for m in range(HK):
                        if m >= 3 or not (isinstance(i, int) and i == 0 and b == 0):
                            pe.wait_ge(s_gelu, s * HK + m - 2)
                        o = bank[:, 2 + m % 3, :]
                        ms = slice(m * P, (m + 1) * P)
                        pe.matmul(o, w1a[b][:, ms], xTa[b][:, :], start=True, stop=False)
                        pe.matmul(o, w1b[b][:, ms], xTb[b][:, :], start=False, stop=True).then_inc(s_h, 1)

                def second(i, b):
                    s = i * 2 + b
                    pe.wait_ge(s_gelu, s * HK + HK)
                    for j in range(G):
                        if j >= 2 or not (isinstance(i, int) and i == 0 and b == 0):
                            pe.wait_ge(s_y, s * G + j - 1)
                        for m in range(HK):
                            mm = pe.matmul(bank[:, YB[j % 2], 0:C], h[b][:, m, j * P:(j + 1) * P], w2[b][:, m, :],
                                           start=(m == 0), stop=(m == HK - 1))
                        mm.then_inc(s_yps, 1)

                pe.wait_ge(s_ones, 2)
                transposes(0, 0)
                first(0, 0)
                transposes(0, 1)
                second(0, 0)
                with pe.Fori(1, NT // 2) as i:
                    first(i - 1, 1)
                    transposes(i, 0)
                    second(i - 1, 1)
                    first(i, 0)
                    transposes(i, 1)
                    second(i, 0)
                first(NT // 2 - 1, 1)
                if NT % 2:
                    transposes(NT // 2, 0)
                second(NT // 2 - 1, 1)
                if NT % 2:
                    first(NT // 2, 0)
                    second(NT // 2, 0)


def combine(nc, name, H, top, pos_i, wgt, Y):
    with Phase(nc) as ctx:
        sb = lambda n, s, dt=F32: ctx.enter_context(nc.sbuf_tensor(f"{name}c_{n}", s, dt))
        sem = lambda n: ctx.sem(f"{name}c_{n}")
        yg = [sb(f"yg{b}", [P, G, top, C]) for b in range(2)]
        idx = [sb(f"idx{b}", [P, top, G], I32) for b in range(2)]
        s_idx, s_add, s_alone = sem("idx_ready"), sem("added"), sem("stand_alone")
        s_g = [sem(f"gathered{b}") for b in range(2)]
        n_dma = 16 * top * G
        adds = 1 if top == 1 else top * G

        with nc.Block() as block:
            @block.gpsimd
            def _(pool):
                def gather(i, b):
                    g = i * 2 + b
                    if not isinstance(i, int) or i > 0:
                        pool.wait_ge(s_add, (g - 1) * adds)
                    pool.tensor_copy(idx[b][:, :, :], pos_i[:, :, bass.ds(g * G, G)]).then_inc(s_idx, 1)
                    pool.wait_ge(s_idx, g + 1)
                    pool.sem_inc(s_alone, 1)
                    for j in range(G):
                        for k in range(top):
                            pool.indirect_dma_start(yg[b][:, j, k, :], None, Y,
                                                    bass.IndirectOffsetOnAxis(idx[b][:, k, j:j + 1].bitcast(U32), 0)).then_inc(s_g[b], 16)
                for b in range(2):
                    gather(0, b)
                with pool.Fori(1, NG // 2) as i:
                    for b in range(2):
                        gather(i, b)

            @block.vector
            def _(dve):
                def add(i, b):
                    g = i * 2 + b
                    dve.wait_ge(s_g[b], i * n_dma + n_dma)
                    if top == 1:
                        hs = H[:, bass.ds(g * G, G), :]
                        dve.tensor_tensor(hs, hs, yg[b][:, :, 0, :], ALU.add).then_inc(s_add, 1)
                        return
                    for k in range(top):
                        for j in range(G):
                            hs = H[:, bass.ds(g * G + j, 1), :].rearrange("p a c -> p (a c)")
                            if k:
                                dve.wait_ge(s_add, g * adds + j + 1)
                            dve.scalar_tensor_tensor(hs, yg[b][:, j, k, :], wgt[:, k, bass.ds(g * G + j, 1)], hs,
                                                     ALU.mult, ALU.add).then_inc(s_add, 1)
                for b in range(2):
                    add(0, b)
                with dve.Fori(1, NG // 2) as i:
                    for b in range(2):
                        add(i, b)


def mamba_phase(nc, A, H, bank, K):
    with Phase(nc) as ctx:
        sb = lambda n, s, dt=F32: ctx.enter_context(nc.sbuf_tensor(f"m_{n}", s, dt))
        sem = lambda n: ctx.sem(f"m_{n}")
        two = range(2)
        DC, NS, TAPS, R = 3, 16, 4, 12
        PB, PC = 32, 64
        PW = P + 2 * (TAPS - 1)
        L1 = P + 1
        FL = DC * G * L1
        win_a, win_b = sb("win_a", [P, 2 * DC * P]), sb("win_b", [CR, 2 * DC * P])
        cw, cb = sb("cw", [P, DC, TAPS]), sb("cb", [P, DC])
        wx, wdt = sb("wx", [P, DC, 80]), sb("wdt", [R, DC * P])
        bdt, Ac, Dp = sb("bdt", [P, DC]), sb("Ac", [P, DC, NS]), sb("Dp", [P, DC])
        wo = sb("wo", [P, DC, C])
        zTa, zTb = sb("zTa", [P, TOK]), sb("zTb", [CR, TOK])
        tap = [sb(f"tap{k}", [P, DC, G, PW]) for k in range(TAPS)]
        cs0, cs1 = sb("cs0", [P, DC, TOK]), sb("cs1", [P, DC, TOK])
        e = cs0
        z = cs1[:, :, :].rearrange("p c t -> p (c t)")[:, 0:G * C].rearrange("p (j c) -> p j c", j=G)
        xc = [sb(f"xc{d}", [P, DC, TOK]) for d in two]
        pj = [sb(f"pj{d}", [PC + NS, TOK]) for d in two]
        r = sb("r", [P, DC, TOK])
        dt = [sb(f"dt{d}", [P, DC, TOK]) for d in two]
        u = [sb(f"u{d}", [P, DC, TOK]) for d in two]
        gz = sb("gz", [P, DC, TOK])
        ys = xs = xc[1]
        Bs = [sb(f"Bs{b}", [P, TOK]) for b in two]
        dA = [sb(f"dA{b}", [P, FL + 1]) for b in two]
        dBx = [sb(f"dBx{b}", [P, FL + 1]) for b in two]
        h = [sb(f"h{b}", [P, FL + 1]) for b in two]
        pr = [sb(f"pr{b}", [P, DC, TOK]) for b in two]
        ln = LayerNorm(nc, ctx, "m_ln", 1e-5, K)
        loaded, cleared, s_Ac = sem("loaded"), sem("cleared"), sem("A_ready")
        s_z, s_zTps, s_zT = sem("z_ready"), sem("zTps_ready"), sem("zT_ready")
        s_xps, s_tap, s_zps, s_gz = sem("xps_ready"), sem("taps_ready"), sem("zps_ready"), sem("gate_ready")
        s_cv, s_xc, s_pjps, s_pj = sem("conv_ready"), sem("xc_ready"), sem("pjps_ready"), sem("pj_ready")
        s_dtps, s_abs, s_e, s_w1, s_ln, s_sp = (sem(n) for n in ("dtps_ready", "abs_ready", "e_ready", "e1_ready", "ln_ready", "softplus_steps"))
        s_u, s_xs = sem("u_ready"), sem("xs_ready")
        s_Bps, s_B, s_Cps, s_dA, s_dBx, s_h, s_pr, s_red = (
            sem(n) for n in ("Bps_ready", "B_ready", "Cps_ready", "dA_ready", "dBx_ready", "h_ready", "readout_ready", "summed"))
        s_ys, s_gy, s_ops, s_out = sem("y_ready"), sem("gated_ready"), sem("outps_ready"), sem("res_ready")

        def data(t):
            return t[:, 0:FL].rearrange("p (c b t) -> p c b t", c=DC, b=G)[:, :, :, 1:L1]

        def seqs(t):
            return t[:, :, :].rearrange("p c (b t) -> p c b t", b=G)

        with nc.Block() as block:
            @block.sync
            def _(sp):
                sp.wait_ge(cleared, 1)
                for dst, src in (
                    (win_a[:, :], A["m_WinT"][0:P, :]), (win_b[:, :], A["m_WinT"][P:C, :]),
                    (cw[:, :, :], A["m_conv_w"].rearrange("(c p) k -> p c k", p=P)),
                    (cb[:, :], A["m_conv_b"]),
                    (wx[:, :, 0:R], A["m_WxT"][:, 0:R].rearrange("(c p) r -> p c r", p=P)),
                    (wx[:, :, PB:PB + NS], A["m_WxT"][:, R:R + NS].rearrange("(c p) r -> p c r", p=P)),
                    (wx[:, :, PC:PC + NS], A["m_WxT"][:, R + NS:R + 2 * NS].rearrange("(c p) r -> p c r", p=P)),
                    (wdt[:, :], A["m_WdtT"]), (bdt[:, :], A["m_b_dt"]),
                    (Ac[:, :, :], A["m_A_log"].rearrange("(c p) n -> p c n", p=P)),
                    (Dp[:, :], A["m_D"]),
                    (wo[:, :, :], A["m_WoutT"].rearrange("(c p) n -> p c n", p=P)),
                ):
                    sp.dma_start(dst, src).then_inc(loaded, 16)

            @block.scalar
            def _(act):
                act.wait_ge(loaded, 16 * 12)
                act.activation(Ac[:, :, :], Ac[:, :, :], ACT.Exp).then_inc(s_Ac, 1)

            @block.vector
            def _(dve):
                dve.memset(wx[:, :, :], 0.0).then_inc(cleared, 1)
                for b in two:
                    dve.memset(dA[b][:, :], 0.0)
                    dve.memset(dBx[b][:, :], 0.0)
                for t in tap:
                    dve.memset(t[:, :, :, :], 0.0)
                dve.wait_ge(s_Ac, 1)
                dve.tensor_scalar(Ac[:, :, :], Ac[:, :, :], -1.0, None, ALU.mult)

        def chain(g, d):
            q = g * 2 + d
            static = isinstance(g, int)

            def conv(k):
                o = k if d == 0 else 2 * (TAPS - 1) - k
                return tap[k][:, :, :, o:o + P]

            def pool_conv(pool, part):
                if part == 0:
                    pool.wait_ge(s_tap, g * DC + DC)
                    if not static or q > 0:
                        pool.wait_ge(s_xc, q * DC)
                    pool.tensor_tensor(seqs(cs0), conv(0), conv(1), ALU.add).then_inc(s_cv, 1)
                elif part == 1:
                    pool.tensor_tensor(seqs(cs1), conv(2), conv(3), ALU.add).then_inc(s_cv, 1)
                else:
                    pool.wait_ge(s_cv, q * 3 + 2)
                    pool.tensor_tensor(cs0[:, :, :], cs0[:, :, :], cs1[:, :, :], ALU.add).then_inc(s_cv, 1)

            def act_xc(act):
                act.wait_ge(s_cv, q * 3 + 3)
                if not static or g > 0:
                    if d == 0:
                        act.wait_ge(s_xs, g)
                    else:
                        act.wait_ge(s_ops, g * G)
                if not static or g > 0:
                    act.wait_ge(s_u, q - 1)
                for c in range(DC):
                    act.activation(xc[d][:, c, :], cs0[:, c, :], ACT.Silu, bias=cb[:, c:c + 1]).then_inc(s_xc, 1)

            def pe_proj(pe):
                pe.wait_ge(s_xc, q * DC + DC)
                if d == 1:
                    pe.wait_ge(s_gz, g * DC + DC)
                for c in range(DC):
                    mm = pe.matmul(bank[0:80, 7, :], wx[:, c, :], xc[d][:, c, :], start=(c == 0), stop=(c == DC - 1))
                mm.then_inc(s_pjps, 1)

            def act_pj(act):
                act.wait_ge(s_pjps, q + 1)
                if not static or g > 0:
                    act.wait_ge(s_Cps, (q - 1) * NS)
                act.copy(pj[d][:, :], bank[0:80, 7, :]).then_inc(s_pj, 1)

            def pe_dt(pe, c):
                if c == 0:
                    pe.wait_ge(s_pj, q + 1)
                else:
                    pe.wait_ge(s_abs, q * 2 * DC + 2 * c)
                pe.matmul(bank[:, 6, :], wdt[:, c * P:(c + 1) * P], pj[d][0:R, :], start=True, stop=True).then_inc(s_dtps, 1)

            def act_abs(act, c):
                act.wait_ge(s_dtps, q * DC + c + 1)
                if c == 0 and (not static or q > 0):
                    act.wait_ge(s_sp, q * 3)
                act.activation(e[:, c, :], bank[:, 6, :], ACT.Abs, bias=bdt[:, c:c + 1]).then_inc(s_abs, 1)
                act.activation(r[:, c, :], bank[:, 6, :], ACT.Relu, bias=bdt[:, c:c + 1]).then_inc(s_abs, 1)

            def act_e(act):
                act.wait_ge(s_abs, (q + 1) * 2 * DC)
                act.activation(e[:, :, :], e[:, :, :], ACT.Exp, scale=-1.0).then_inc(s_e, 1)
                act.wait_ge(s_e, q + 1)
                if not static or g > 0:
                    act.wait_ge(s_dA, (q - 1) * NS)
                act.activation(dt[d][:, :, :], e[:, :, :], ACT.Ln, bias=1.0).then_inc(s_ln, 1)

            def dve_w1(dve):
                dve.wait_ge(s_e, q + 1)
                if not static or q > 0:
                    dve.wait_ge(s_cv, q * 3 + 3)
                dve.tensor_scalar(cs1[:, :, :], e[:, :, :], 1.0, -1.0, ALU.add, ALU.add).then_inc(s_w1, 1)

            def pool_sp(pool, part):
                if part == 0:
                    pool.wait_ge(s_w1, q + 1)
                    pool.wait_ge(s_ln, q + 1)
                    pool.tensor_tensor(e[:, :, :], e[:, :, :], cs1[:, :, :], ALU.subtract).then_inc(s_sp, 1)
                elif part == 1:
                    pool.wait_ge(s_sp, q * 3 + 1)
                    pool.tensor_tensor(e[:, :, :], e[:, :, :], dt[d][:, :, :], ALU.add).then_inc(s_sp, 1)
                else:
                    pool.wait_ge(s_sp, q * 3 + 2)
                    pool.tensor_tensor(dt[d][:, :, :], e[:, :, :], r[:, :, :], ALU.add).then_inc(s_sp, 1)

            def dve_u(dve):
                dve.wait_ge(s_sp, q * 3 + 3)
                if not static or g > 0:
                    dve.wait_ge(s_dBx, (q - 1) * NS)
                dve.tensor_tensor(u[d][:, :, :], dt[d][:, :, :], xc[d][:, :, :], ALU.mult).then_inc(s_u, 1)

            hh = lambda j: H[:, bass.ds(g * G + j, 1), :].rearrange("p a c -> p (a c)")

            def dve_norm(dve):
                if not static or g > 0:
                    dve.wait_ge(s_sp, q * 3)
                ln.normalise(dve, g, hh, lambda j: z[:, j, :], s_z)

            def pe_zT(pe):
                pe.wait_ge(s_z, g * G + G)
                if not static or g > 0:
                    pe.wait_ge(s_abs, q * 2 * DC)
                for j in range(G):
                    mm = pe.transpose(bank[:, 6, j * P:(j + 1) * P], z[:, j, 0:P], K.ident[:, :])
                mm.then_inc(s_zTps, 1)
                for j in range(G):
                    mm = pe.transpose(bank[0:CR, 7, j * P:(j + 1) * P], z[:, j, P:C], K.ident[:, :])
                mm.then_inc(s_zTps, 1)

            def act_zT(act):
                if not static or g > 0:
                    act.wait_ge(s_zps, g * DC)
                act.wait_ge(s_zTps, g * 2 + 1)
                act.copy(zTa[:, :], bank[:, 6, :]).then_inc(s_zT, 1)
                act.wait_ge(s_zTps, g * 2 + 2)
                act.copy(zTb[:, :], bank[0:CR, 7, :]).then_inc(s_zT, 1)

            def pe_in(pe, c):
                s_ps, s_used, per = (s_xps, s_tap, 1) if d == 0 else (s_zps, s_gz, 1)
                if c == 0:
                    pe.wait_ge(s_zT, g * 2 + 2)
                    if d == 1:
                        pe.wait_ge(s_abs, q * 2 * DC)
                        if not static or g > 0:
                            pe.wait_ge(s_out, g * G)
                if c == 2:
                    pe.wait_ge(s_used, g * DC + 1)
                m = slice((d * DC + c) * P, (d * DC + c + 1) * P)
                o = bank[:, 6 + c % 2, :]
                pe.matmul(o, win_a[:, m], zTa[:, :], start=True, stop=False)
                pe.matmul(o, win_b[:, m], zTb[:, :], start=False, stop=True).then_inc(s_ps, 1)

            def act_taps(act, c):
                act.wait_ge(s_xps, g * DC + c + 1)
                if c == 0 and (not static or g > 0):
                    act.wait_ge(s_cv, g * 6)
                for k in range(TAPS):
                    ins = act.activation(tap[k][:, c, :, TAPS - 1:TAPS - 1 + P],
                                         bank[:, 6 + c % 2, :].rearrange("p (b t) -> p b t", b=G),
                                         ACT.Copy, scale=cw[:, c, k:k + 1])
                ins.then_inc(s_tap, 1)

            def act_gz(act, c):
                act.wait_ge(s_zps, g * DC + c + 1)
                if c == 0 and (not static or g > 0):
                    act.wait_ge(s_gy, g)
                act.activation(gz[:, c, :], bank[:, 6 + c % 2, :], ACT.Silu).then_inc(s_gz, 1)

            def pool_xs(pool):
                pool.wait_ge(s_xc, q * DC + DC)
                pool.wait_ge(s_u, q + 1)
                pool.tensor_tensor(xs[:, :, :], xc[0][:, :, :], xc[1][:, :, :], ALU.add).then_inc(s_xs, 1)

            W = {"pe": [], "act": [], "dve": [], "pool": []}
            def put(eng, unit, f, *a):
                W[eng].append((unit, f, a))

            if d == 0:
                put("dve", 0, lambda dve: ln.stats(dve, g, hh))
                put("pool", 0, lambda pool: ln.rstd(pool, g))
                put("dve", 1, dve_norm)
                put("pe", 2, pe_zT)
                put("act", 2, act_zT)
                put("pe", 3, pe_in, 0); put("pe", 3, pe_in, 1); put("pe", 4, pe_in, 2)
                put("act", 3, act_taps, 0); put("act", 4, act_taps, 1); put("act", 5, act_taps, 2)
                t = 6
            else:
                put("pe", 0, pe_in, 0); put("pe", 0, pe_in, 1); put("pe", 1, pe_in, 2)
                put("act", 0, act_gz, 0); put("act", 0, act_gz, 1); put("act", 1, act_gz, 2)
                t = 0
            put("pool", t, pool_conv, 0); put("pool", t, pool_conv, 1); put("pool", t + 1, pool_conv, 2)
            if d == 0:
                x0 = t + 2
            else:
                x0 = t + 3
            put("act", x0, act_xc)
            put("pe", x0 + 1, pe_proj)
            put("act", x0 + 1, act_pj)
            put("pe", x0 + 2, pe_dt, 0); put("act", x0 + 2, act_abs, 0)
            put("pe", x0 + 3, pe_dt, 1); put("act", x0 + 3, act_abs, 1)
            put("pe", x0 + 4, pe_dt, 2); put("act", x0 + 4, act_abs, 2)
            put("act", x0 + 4, act_e)
            put("dve", x0 + 5, dve_w1)
            put("pool", x0 + 5, pool_sp, 0); put("pool", x0 + 6, pool_sp, 1); put("pool", x0 + 6, pool_sp, 2)
            put("dve", x0 + 7, dve_u)
            if d == 1:
                put("pool", x0 + 8, pool_xs)
            return W

        def pe_bcast(pe, g, d, n):
            N = (g * 2 + d) * NS + n
            early = isinstance(g, int) and g == 0 and d == 0
            if n == 0:
                pe.wait_ge(s_pj, g * 2 + d + 1)
            if not (early and n == 0):
                pe.wait_ge(s_B, N)
            pe.matmul(bank[:, 5, :], K.ident[PB:PB + NS, PB + n:PB + n + 1].to_broadcast([NS, P]), pj[d][PB:PB + NS, :], start=True, stop=True).then_inc(s_Bps, 1)
            if not (early and n < 2):
                pe.wait_ge(s_pr, N - 1)
            pe.matmul(bank[:, 3 + n % 2, :], K.ident[PC:PC + NS, PC + n:PC + n + 1].to_broadcast([NS, P]), pj[d][PC:PC + NS, :], start=True, stop=True).then_inc(s_Cps, 1)

        def pe_sum(pe, g, d, n):
            N = (g * 2 + d) * NS + n
            pe.wait_ge(s_pr, N + 1)
            if d == 0 and n == 0 and (not isinstance(g, int) or g > 0):
                pe.wait_ge(s_ys, g * DC)
            for c in range(DC):
                mm = pe.matmul(bank[:, c, :], K.ident[:, :], pr[n % 2][:, c, :], start=(d == 0 and n == 0),
                               stop=(d == 1 and n == NS - 1))
            mm.then_inc(s_red, 1)

        def act_unit(act, g, d, n):
            N = (g * 2 + d) * NS + n
            early = isinstance(g, int) and g == 0 and d == 0 and n < 2
            act.wait_ge(s_Bps, N + 1)
            if not early:
                act.wait_ge(s_dBx, N - 1)
            act.copy(Bs[n % 2][:, :], bank[:, 5, :]).then_inc(s_B, 1)
            if n == 0:
                act.wait_ge(s_sp, (g * 2 + d) * 3 + 3)
            if not early:
                act.wait_ge(s_h, N - 1)
            for c in range(DC):
                ins = act.activation(data(dA[n % 2])[:, c, :, :], seqs(dt[d])[:, c, :, :], ACT.Exp, scale=Ac[:, c, n:n + 1])
            ins.then_inc(s_dA, 1)

        def pool_unit(pool, g, d, n):
            N = (g * 2 + d) * NS + n
            early = isinstance(g, int) and g == 0 and d == 0 and n < 2
            if n == 0:
                pool.wait_ge(s_u, g * 2 + d + 1)
            pool.wait_ge(s_B, N + 1)
            if not early:
                pool.wait_ge(s_h, N - 1)
            bb = Bs[n % 2][:, :].rearrange("p (b t) -> p b t", b=G).unsqueeze(1).to_broadcast([P, DC, G, P])
            pool.tensor_tensor(data(dBx[n % 2]), seqs(u[d]), bb, ALU.mult).then_inc(s_dBx, 1)

        def dve_scan(dve, g, d, n):
            N = (g * 2 + d) * NS + n
            dve.wait_ge(s_dA, N + 1)
            dve.wait_ge(s_dBx, N + 1)
            b = n % 2
            v = (lambda t: t[:, 0:FL]) if d == 0 else (lambda t: t[:, FL:0:-1])
            dve.tensor_tensor_scan(v(h[b]), v(dA[b]), v(dBx[b]), 0.0, ALU.mult, ALU.add).then_inc(s_h, 1)

        def dve_read(dve, g, d, n):
            N = (g * 2 + d) * NS + n
            early = isinstance(g, int) and g == 0 and d == 0 and n < 2
            dve.wait_ge(s_h, N + 1)
            dve.wait_ge(s_Cps, N + 1)
            if not early:
                dve.wait_ge(s_red, N - 1)
            cc = bank[:, 3 + n % 2, :].rearrange("p (b t) -> p b t", b=G).unsqueeze(1).to_broadcast([P, DC, G, P])
            dve.tensor_tensor(seqs(pr[n % 2]), data(h[n % 2]), cc, ALU.mult).then_inc(s_pr, 1)

        def dve_y(dve, g):
            dve.wait_ge(s_xs, g + 1)
            dve.wait_ge(s_red, (g + 1) * 2 * NS)
            for c in range(DC):
                dve.scalar_tensor_tensor(ys[:, c, :], xs[:, c, :], Dp[:, c:c + 1], bank[:, c, :], ALU.mult,
                                         ALU.add).then_inc(s_ys, 1)
            dve.wait_ge(s_ys, g * DC + DC)
            dve.wait_ge(s_gz, g * DC + DC)
            dve.tensor_tensor(ys[:, :, :], ys[:, :, :], gz[:, :, :], ALU.mult).then_inc(s_gy, 1)

        def pe_out(pe, g, j, last):
            if j == 0:
                pe.wait_ge(s_gy, g + 1)
                pe.wait_ge(s_abs, (g * 2 + (2 if last else 3)) * 2 * DC)
            else:
                pe.wait_ge(s_out, g * G + j)
            for c in range(DC):
                mm = pe.matmul(bank[:, 6, 0:C], ys[:, c, j * P:(j + 1) * P], wo[:, c, :], start=(c == 0), stop=(c == DC - 1))
            mm.then_inc(s_ops, 1)

        def dve_out(dve, g, j):
            dve.wait_ge(s_ops, g * G + j + 1)
            hs = H[:, bass.ds(g * G + j, 1), :].rearrange("p a c -> p (a c)")
            dve.scalar_tensor_tensor(hs, bank[:, 6, 0:C], 0.5, hs, ALU.mult, ALU.add).then_inc(s_out, 1)

        def slot(eng, name, g, d, nxt, main):
            pend = chain(*nxt)[name] if nxt is not None else []
            i = 0
            for n in range(NS):
                main(eng, g, d, n)
                while i < len(pend) and pend[i][0] <= n:
                    pend[i][1](eng, *pend[i][2])
                    i += 1
            assert i == len(pend)

        def alone(eng, name, g, d):
            for _, f, a in chain(g, d)[name]:
                f(eng, *a)

        def program(eng, name, main, ends=None):
            alone(eng, name, 0, 0)

            def group(g, last):
                slot(eng, name, g, 0, (g, 1), main)
                slot(eng, name, g, 1, None if last else (g + 1, 0), main)
                if ends:
                    ends(eng, g, last)
            group(0, False)
            with eng.Fori(1, NG - 1) as g:
                group(g, False)
            group(NG - 1, True)

        def order(f):
            def inner(g, d):
                W = f(g, d)
                return {k: sorted(v, key=lambda s: s[0]) for k, v in W.items()}
            return inner
        chain = order(chain)

        with nc.Block() as block:
            @block.tensor
            def _(pe):
                def main(pe, g, d, n):
                    pe_bcast(pe, g, d, n)
                    if n > 0:
                        pe_sum(pe, g, d, n - 1)
                    if n == NS - 1:
                        pe_sum(pe, g, d, n)
                def ends(pe, g, last):
                    for j in range(G):
                        pe_out(pe, g, j, last)
                program(pe, "pe", main, ends)

            @block.scalar
            def _(act):
                program(act, "act", act_unit)

            @block.gpsimd
            def _(pool):
                program(pool, "pool", pool_unit)

            @block.vector
            def _(dve):
                def main(dve, g, d, n):
                    dve_scan(dve, g, d, n)
                    if n > 0:
                        dve_read(dve, g, d, n - 1)
                    if n == NS - 1:
                        dve_read(dve, g, d, n)
                def ends(dve, g, last):
                    dve_y(dve, g)
                    for j in range(G):
                        dve_out(dve, g, j)
                program(dve, "dve", main, ends)


def clear_slots(nc, X):
    n = X.shape[0] // P
    with Phase(nc) as ctx, nc.Block() as block:
        zr = ctx.enter_context(nc.sbuf_tensor("zero_rows", [P, n // 12 * C], F32))
        s_set, s_clr = ctx.sem("zr_set"), ctx.sem("x_cleared")

        @block.vector
        def _(dve):
            dve.memset(zr[:, :], 0.0).then_inc(s_set, 1)

        @block.sync
        def _(sp):
            sp.wait_ge(s_set, 1)
            v = X.rearrange("(q p r) c -> q p (r c)", q=12, p=P)
            for q in range(12):
                sp.dma_start(v[q, :, :], zr[:, :]).then_inc(s_clr, 16)
            sp.wait_ge(s_clr, 16 * 12)


def tower(nc, A, out, upto=4):
    with Phase(nc) as ctx:
        H = ctx.enter_context(nc.sbuf_tensor("H", [P, B, C], F32))
        bank = ctx.enter_context(nc.psum_tensor("bank", [P, 8, 512], F32))
        K = constants(nc, ctx, A)
        attention_phase(nc, A, H, bank, K)
        slots = (2 * B * P // TOK + E1 - 1) * TOK
        X = nc.dram_tensor("slots_x", (slots, C), F32).ap()
        Y = nc.dram_tensor("slots_y", (slots, C), F32).ap()
        clear_slots(nc, X)
        if upto > 1:
            expert_phase(nc, "f0", A, H, bank, K, E0, 1, "f0_center", X, Y)
        if upto > 2:
            mamba_phase(nc, A, H, bank, K)
        if upto > 3:
            expert_phase(nc, "f1", A, H, bank, K, E1, 2, None, X, Y)
        stored = ctx.sem("out_stored")
        with nc.Block() as block:
            @block.sync
            def _(sp):
                sp.dma_start(out.rearrange("(t p) c -> p t c", p=P), H[:, :, :]).then_inc(stored, 16)
                sp.wait_ge(stored, 16)


def layout(inputs):
    import numpy as np
    g = lambda n: np.asarray(inputs[n])
    c = np.ascontiguousarray
    return {
        "ids_wordT": c(g("x").T), "ids_posi": c(g("itok_BS_0_511").reshape(-1)),
        "ids_demo": c(g("itok_BS_0_255").reshape(-1)), "ids_seg": c(g("mask_BS_i1_0").reshape(-1)),
        "word_table": c(g("L0_tok_word_table")), "demo_table": c(g("L0_tok_demo_table")),
        "posi_table": c(g("L0_tok_posi_table")), "seg_table": c(g("L0_tok_seg_table")),
        "ln_gamma": c(g("L0_tok_ln_gamma")), "ln_beta": c(g("L0_tok_ln_beta")),
        "WqkvT": c(g("L0_attn_Wqkv_w").T), "bqkv": c(g("L0_attn_Wqkv_b").reshape(1, -1)),
        "WprojT": c(g("L0_attn_Wproj_w").T), "bproj": c(g("L0_attn_Wproj_b").reshape(1, -1)),
        "f0_gate": c(g("L0_ffn_gate_w")), "f0_gate_b": c(g("L0_ffn_gate_b").reshape(1, -1)),
        "f0_center": c(g("L0_ffn_gate_center")),
        "f0_w1": c(g("L0_ffn_w1")), "f0_b1": c(g("L0_ffn_b1")), "f0_w2": c(g("L0_ffn_w2")), "f0_b2": c(g("L0_ffn_b2")),
        "m_WinT": c(g("L1_attn_W_in").T), "m_conv_w": c(g("L1_attn_conv_w")), "m_conv_b": c(g("L1_attn_conv_b").reshape(-1, P).T),
        "m_WxT": c(g("L1_attn_W_xproj").T), "m_WdtT": c(g("L1_attn_W_dt").T), "m_b_dt": c(g("L1_attn_b_dt").reshape(-1, P).T),
        "m_A_log": c(g("L1_attn_A_log")), "m_D": c(g("L1_attn_D_param").reshape(-1, P).T), "m_WoutT": c(g("L1_attn_W_out").T),
        "f1_gate": c(g("L1_ffn_router_w")), "f1_gate_b": c(g("L1_ffn_router_b").reshape(1, -1)),
        "f1_w1": c(g("L1_ffn_w1")), "f1_b1": c(g("L1_ffn_b1")), "f1_w2": c(g("L1_ffn_w2")), "f1_b2": c(g("L1_ffn_b2")),
    }


def kernel(**inputs):
    import numpy as np
    import concourse.bacc as bacc
    from concourse.bass_utils import run_bass_kernel_spmd

    nc = bacc.Bacc("TRN2", target_bir_lowering=False, num_devices=1)
    arrays = layout(inputs)
    A = {n: nc.dram_tensor(n, a.shape, mybir.dt.from_np(a.dtype), kind="ExternalInput").ap() for n, a in arrays.items()}
    out = nc.dram_tensor("out", (B * P, C), F32, kind="ExternalOutput").ap()
    tower(nc, A, out)
    r = run_bass_kernel_spmd(nc, [arrays], core_ids=[0])
    return r.results[0]["out"].reshape(B, P, C)
```

```python
from contextlib import ExitStack

import concourse.bass as bass
from concourse import mybir

ALU = mybir.AluOpType
ACT = mybir.ActivationFunctionType
AX = mybir.AxisListType.X
F32 = mybir.dt.float32
BF16 = mybir.dt.bfloat16
I32 = mybir.dt.int32
U32 = mybir.dt.uint32

P = 128
B = 64
C = 192
CR = C - P
G = 4
NG = B // G
TOK = G * P
HEADS, HD = 12, 16
RG = 4
HC = HEADS // RG
HID = 768
HK = HID // P
E0, E1 = 4, 8
BIG = 1.0e10


class Phase(ExitStack):

    def __init__(self, nc):
        super().__init__()
        self.nc, self.sems = nc, []

    def sem(self, name):
        self.sems.append(self.enter_context(self.nc.semaphore(name)))
        return self.sems[-1]

    def __exit__(self, *exc):
        if exc[0] is None and self.sems:
            nums = sorted(s.num for s in self.sems)
            starts = [n for n in nums if n - 1 not in nums]
            ends = [n + 1 for n in nums if n + 1 not in nums]
            with self.nc.Block() as block:
                @block.gpsimd
                def _(pool):
                    for a, b in zip(starts, ends):
                        pool.sem_clear(range(a, b))
        return super().__exit__(*exc)


def stand_alone(eng, go):
    eng.sem_inc(go, 1)


class LayerNorm:

    def __init__(self, nc, ctx, name, eps, K):
        self.nc, self.eps, self.const, self.go = nc, eps, K.mhalf, K.go
        sb = lambda n, s: ctx.enter_context(nc.sbuf_tensor(f"{name}_{n}", s, F32))
        sem = lambda n: ctx.sem(f"{name}_{n}")
        self.bn = sb("bn", [P, G, 6])
        self.mv = sb("mv", [P, G, 2])
        self.ve = sb("ve", [P, G])
        self.rs = sb("rs", [P, G])
        self.bn_done, self.mv_done = sem("bn_done"), sem("mv_done")
        self.eps_done, self.rs_done = sem("eps_done"), sem("rs_done")

    def stats(self, dve, g, src):
        for j in range(G):
            dve.bn_stats(self.bn[:, j, :], src(j)).then_inc(self.bn_done, 1)
        for j in range(G):
            dve.wait_ge(self.bn_done, g * G + j + 1)
            stand_alone(dve, self.go)
            dve.bn_aggr(self.mv[:, j, :], self.bn[:, j, :]).then_inc(self.mv_done, 1)

    def rstd(self, pool, g):
        pool.wait_ge(self.mv_done, g * G + G)
        stand_alone(pool, self.go)
        pool.tensor_scalar(self.ve[:, :], self.mv[:, :, 1], self.eps, None, ALU.add).then_inc(self.eps_done, 1)
        pool.wait_ge(self.eps_done, g + 1)
        pool.tensor_tensor(self.rs[:, :], self.ve[:, :], self.const[:, 0:G], ALU.pow).then_inc(self.rs_done, 1)

    def normalise(self, dve, g, src, dst, done):
        dve.wait_ge(self.rs_done, g + 1)
        for j in range(G):
            dve.tensor_scalar(dst(j), src(j), self.mv[:, j, 0:1], self.rs[:, j:j + 1],
                              ALU.subtract, ALU.mult).then_inc(done, 1)


def constants(nc, ctx, A):
    sb = lambda n, s, dt=F32: ctx.enter_context(nc.sbuf_tensor(n, s, dt))
    sem = lambda n: ctx.sem(n)
    K = type("Constants", (), {})()
    K.ident = sb("ident", [P, P])
    K.identb = sb("identb", [P, P], BF16)
    K.mhalf = sb("mhalf", [P, G])
    K.ones = sb("ones", [P, P])
    K.go = sem("stand_alone")
    zeroed, made = sem("const_zeroed"), sem("const_made")
    with nc.Block() as block:
        @block.gpsimd
        def _(pool):
            pool.memset(K.ident[:, :], 0.0).then_inc(zeroed, 1)
            pool.memset(K.identb[:, :], 0.0).then_inc(zeroed, 1)
            pool.memset(K.mhalf[:, :], -0.5)
            pool.memset(K.ones[:, :], 1.0)
            pool.wait_ge(zeroed, 2)
            for t in (K.ident, K.identb):
                pool.affine_select(out=t[:, :], in_=t[:, :], compare_op=ALU.not_equal, fill=1.0, base=0,
                                   pattern=[[-1, P]], channel_multiplier=1)
    return K


def attention_phase(nc, A, H, bank, K):
    with Phase(nc) as ctx:
        sb = lambda n, s, dt=F32: ctx.enter_context(nc.sbuf_tensor(n, s, dt))
        sem = lambda n: ctx.sem(n)
        posi_t = sb("posi_t", [P, C])
        ds_t = sb("ds_t", [66, C])
        gam, bet = sb("gam", [P, C]), sb("bet", [P, C])
        wqp_a, wqp_b = sb("wqp_a", [P, HC * P]), sb("wqp_b", [CR + 1, HC * P])
        wq_a, wq_b = sb("wq_a", [P, C]), sb("wq_b", [CR + 1, C])
        wo_a, wo_b = sb("wo_a", [P, C]), sb("wo_b", [CR + 1, C])
        mask = sb("mask", [P, HC, P], BF16)
        col_i = sb("col_i", [P, 2], I32)
        col = sb("col", [P, 2])
        mul3 = sb("mul3", [66, 1])
        ids_w = sb("ids_w", [P, B], I32)
        idx = sb("idx", [P, G], I32)
        pid = sb("pid", [P, TOK], I32)
        did = sb("did", [66, TOK], I32)
        oh_p, oh_d = sb("oh_p", [P, TOK]), sb("oh_d", [66, TOK])
        word = sb("word", [P, G, C])
        emb = sb("emb", [P, G, C])
        xn = sb("xn", [P, G, C])
        h1 = sb("h1", [P, G, C])
        z = sb("z", [P, G, C])
        zTa, zTb = sb("zTa", [P, TOK]), sb("zTb", [CR + 1, TOK])
        V = sb("V", [P, G, HEADS, HD + 1])
        qT = sb("qT", [P, HC, TOK])
        NE = 3
        mx = sb("mx", [P, NE, HC])
        S = sb("S", [P, NE, HC, P])
        ST = sb("ST", [P, 2, HC, P])
        ri = sb("ri", [P, 2, HEADS])
        at = sb("at", [P, 2, C])
        aTa, aTb = sb("aTa", [P, 2, P]), sb("aTb", [CR + 1, 2, P])
        ln_e = LayerNorm(nc, ctx, "ln_e", 1e-12, K)
        ln_a = LayerNorm(nc, ctx, "ln_a", 1e-5, K)

        loaded, cleared, mul3_set = sem("a_loaded"), sem("a_cleared"), sem("mul3_set")
        s_ids, s_idx, s_word = sem("ids_in"), sem("idx_ready"), sem("word_in")
        s_onehot, s_embps, s_emb = sem("onehot_ready"), sem("embps_ready"), sem("emb_ready")
        s_xn, s_gam, s_h1, s_h1kept = sem("xn_ready"), sem("gamma_done"), sem("h1_ready"), sem("h1_kept")
        s_z, s_zTps, s_zT = sem("z_ready"), sem("zTps_ready"), sem("zT_ready")
        s_qps, s_q = sem("qps_ready"), sem("q_ready")
        s_sc, s_mx, s_sub, s_exp = sem("scores_ready"), sem("max_ready"), sem("sub_ready"), sem("exp_ready")
        s_pT, s_pTc, s_pv = sem("probsT_ready"), sem("probsT_copied"), sem("pv_ready")
        s_ri, s_at, s_aT, s_aTc = sem("rowsum_inv"), sem("att_ready"), sem("attT_ready"), sem("attT_copied")
        s_pr, s_out = sem("proj_ready"), sem("res_ready")

        OB = (5, 2)
        UN = G * RG

        with nc.Block() as block:
            @block.gpsimd
            def _(pool):
                pool.memset(wqp_a[:, :], 0.0).then_inc(cleared, 1)
                pool.memset(wqp_b[:, :], 0.0).then_inc(cleared, 1)
                pool.memset(mask[:, :, :], 0.0).then_inc(cleared, 1)
                pool.iota(col_i[:, :], pattern=[[0, 2]], base=0, channel_multiplier=1).then_inc(cleared, 1)
                pool.wait_ge(cleared, 4)
                pool.affine_select(out=mask[:, :, :], in_=mask[:, :, :], compare_op=ALU.is_ge,
                                   fill=-4.0 * BIG, base=0, pattern=[[0, HC], [-1, P]], channel_multiplier=1).then_inc(cleared, 1)
                pool.wait_ge(cleared, 5)
                pool.iota(col_i[64:128, 1:2], pattern=[[0, 1]], base=0, channel_multiplier=1).then_inc(cleared, 1)
                pool.wait_ge(cleared, 6)
                pool.tensor_copy(col[:, :], col_i[:, :])
                pool.memset(V[:, :, :, HD:HD + 1], 1.0)

            @block.vector
            def _(dve):
                dve.memset(mul3[:, :], 3.0).then_inc(mul3_set, 1)
                dve.memset(zTb[CR:CR + 1, :], 1.0)
                dve.memset(aTb[CR:CR + 1, :, :], 1.0)
                dve.wait_ge(mul3_set, 1)
                dve.memset(mul3[64:66, :], 1.0)

            @block.sync
            def _(sp):
                n = 0
                sp.wait_ge(cleared, 4)
                for dst, src in (
                    (posi_t[:, :], A["posi_table"]), (ds_t[0:64, :], A["demo_table"]), (ds_t[64:66, :], A["seg_table"]),
                    (gam[:, :], A["ln_gamma"].partition_broadcast(P)), (bet[:, :], A["ln_beta"].partition_broadcast(P)),
                    (wq_a[:, :], A["WqkvT"][0:P, 0:C]), (wq_b[0:CR, :], A["WqkvT"][P:C, 0:C]),
                    (wq_b[CR:CR + 1, :], A["bqkv"][0:1, 0:C]),
                    (wqp_a[:, :].rearrange("p (h x) -> p h x", x=32)[:, :, 0:HD],
                     A["WqkvT"][0:P, 0:C].rearrange("k (h d) -> k h d", d=HD)),
                    (wqp_b[0:CR, :].rearrange("p (h x) -> p h x", x=32)[:, :, 0:HD],
                     A["WqkvT"][P:C, 0:C].rearrange("k (h d) -> k h d", d=HD)),
                    (wqp_b[CR:CR + 1, :].rearrange("p (h x) -> p h x", x=32)[:, :, 0:HD],
                     A["bqkv"][0:1, 0:C].rearrange("k (h d) -> k h d", d=HD)),
                    (wo_a[:, :], A["WprojT"][0:P, :]), (wo_b[0:CR, :], A["WprojT"][P:C, :]),
                    (wo_b[CR:CR + 1, :], A["bproj"]), (ids_w[:, :], A["ids_wordT"]),
                ):
                    sp.dma_start(dst, src).then_inc(loaded, 16)
                    n += 1
                sp.wait_ge(loaded, 16 * n)

        with nc.Block() as block:
            def ids_front(sp, g):
                if not isinstance(g, int) or g > 0:
                    sp.wait_ge(s_onehot, g * 2)
                sl = bass.ds(g * TOK, TOK)
                sp.dma_start(pid[:, :], A["ids_posi"][sl].partition_broadcast(P)).then_inc(s_ids, 16)
                sp.dma_start(did[0:64, :], A["ids_demo"][sl].partition_broadcast(64)).then_inc(s_ids, 16)
                sp.dma_start(did[64:66, :], A["ids_seg"][sl].partition_broadcast(2)).then_inc(s_ids, 16)

            @block.sync
            def _(sp):
                ids_front(sp, 0)
                with sp.Fori(1, NG) as g:
                    ids_front(sp, g)

            def pool_front(pool, g):
                if not isinstance(g, int) or g > 0:
                    pool.wait_ge(s_emb, g * 2)
                pool.tensor_copy(idx[:, :], ids_w[:, bass.ds(g * G, G)]).then_inc(s_idx, 1)
                pool.wait_ge(s_idx, g + 1)
                stand_alone(pool, K.go)
                for j in range(G):
                    pool.indirect_dma_start(word[:, j, :], None, A["word_table"],
                                            bass.IndirectOffsetOnAxis(idx[:, j:j + 1].bitcast(U32), 0)).then_inc(s_word, 16)
                ln_e.rstd(pool, g)
                ln_a.rstd(pool, g)

            @block.gpsimd
            def _(pool):
                pool_front(pool, 0)
                with pool.Fori(1, NG) as g:
                    pool_front(pool, g)

            def dve_front(dve, g):
                later = not isinstance(g, int) or g > 0

                def onehots():
                    dve.wait_ge(s_ids, g * 48 + 48)
                    if later:
                        dve.wait_ge(s_embps, g * 2)
                    dve.tensor_scalar(oh_p[:, :], pid[:, :], col[:, 0:1], None, ALU.is_equal).then_inc(s_onehot, 1)
                    dve.tensor_scalar(oh_d[:, :], did[:, :], col[0:66, 1:2], mul3[:, :], ALU.is_equal,
                                      ALU.mult).then_inc(s_onehot, 1)

                def embed():
                    dve.wait_ge(s_word, g * 64 + 64)
                    for b in range(2):
                        dve.wait_ge(s_embps, g * 2 + b + 1)
                        dve.tensor_tensor(emb[:, 2 * b:2 * b + 2, :],
                                          bank[:, 6 + b, 0:2 * C].rearrange("p (j c) -> p j c", j=2),
                                          word[:, 2 * b:2 * b + 2, :], ALU.add).then_inc(s_emb, 1)
                    dve.wait_ge(s_emb, g * 2 + 2)
                    ln_e.stats(dve, g, lambda j: emb[:, j, :])

                def norm1():
                    ln_e.normalise(dve, g, lambda j: emb[:, j, :], lambda j: xn[:, j, :], s_xn)
                    dve.wait_ge(s_xn, g * G + G)
                    dve.tensor_tensor(xn[:, :, :], xn[:, :, :], gam[:, :].unsqueeze(1).to_broadcast([P, G, C]),
                                      ALU.mult).then_inc(s_gam, 1)
                    dve.wait_ge(s_gam, g + 1)
                    if later:
                        dve.wait_ge(s_h1kept, g)
                    dve.tensor_tensor(h1[:, :, :], xn[:, :, :], bet[:, :].unsqueeze(1).to_broadcast([P, G, C]),
                                      ALU.add).then_inc(s_h1, 1)
                    dve.wait_ge(s_h1, g + 1)
                    ln_a.stats(dve, g, lambda j: h1[:, j, :])

                def norm2():
                    if later:
                        dve.wait_ge(s_zTps, g * 2)
                    ln_a.normalise(dve, g, lambda j: h1[:, j, :], lambda j: z[:, j, :], s_z)

                return [onehots, embed, norm1, norm2]

            def dve_unit(dve, g, u):
                n = g * UN + u
                dve.wait_ge(s_sc, n + 1)
                s_ps = bank[:, u % 2, 0:HC * P].rearrange("p (c k) -> p c k", c=HC)
                if u >= NE or not isinstance(g, int) or g > 0:
                    dve.wait_ge(s_pT, n - NE + 1)
                dve.reduce_max(mx[:, u % NE, :], s_ps, AX).then_inc(s_mx, 1)
                dve.wait_ge(s_mx, n + 1)
                dve.tensor_tensor(S[:, u % NE, :, :], s_ps,
                                  mx[:, u % NE, :].unsqueeze(2).to_broadcast([P, HC, P]),
                                  ALU.subtract).then_inc(s_sub, 1)

            def dve_norm_att(dve, g, j):
                n = g * G + j
                O = bank[:, OB[j % 2], 0:HEADS * (HD + 1)].rearrange("p (h d) -> p h d", h=HEADS)
                dve.wait_ge(s_pv, n + 1)
                dve.reciprocal(ri[:, j % 2, :], O[:, :, HD]).then_inc(s_ri, 1)
                dve.wait_ge(s_ri, n + 1)
                if j >= 2 or not isinstance(g, int) or g > 0:
                    dve.wait_ge(s_aT, n - 1)
                dve.tensor_tensor(at[:, j % 2, :].rearrange("p (h d) -> p h d", h=HEADS), O[:, :, 0:HD],
                                  ri[:, j % 2, :].unsqueeze(2).to_broadcast([P, HEADS, HD]),
                                  ALU.mult).then_inc(s_at, 1)

            def dve_residual(dve, g, j):
                n = g * G + j
                if j == 0:
                    dve.wait_ge(s_h1kept, g + 1)
                dve.wait_ge(s_pr, n + 1)
                hs = H[:, bass.ds(g * G + j, 1), :]
                dve.tensor_tensor(hs, hs, bank[:, OB[j % 2], 256:256 + C].unsqueeze(1), ALU.add).then_inc(s_out, 1)

            def dve_body(dve, g, nxt):
                front = dve_front(dve, nxt) if nxt is not None else []
                for u in range(UN):
                    dve_unit(dve, g, u)
                    if u % RG == 1 and front:
                        front.pop(0)()
                    if u >= 5 and (u - 5) % RG == 0:
                        dve_norm_att(dve, g, (u - 5) // RG)
                    if u >= 7 and (u - 7) % RG == 0:
                        dve_residual(dve, g, (u - 7) // RG)
                dve_norm_att(dve, g, G - 1)
                dve_residual(dve, g, G - 1)

            @block.vector
            def _(dve):
                for step in dve_front(dve, 0):
                    step()
                dve_body(dve, 0, 1)
                with dve.Fori(1, NG - 1) as g:
                    dve_body(dve, g, g + 1)
                dve_body(dve, NG - 1, None)

            def act_keep(act, g):
                act.wait_ge(s_h1, g + 1)
                act.copy(H[:, bass.ds(g * G, G), :], h1[:, :, :]).then_inc(s_h1kept, 1)

            def act_zT(act, g):
                if not isinstance(g, int) or g > 0:
                    act.wait_ge(s_qps, g * 5)
                act.wait_ge(s_zTps, g * 2 + 1)
                act.copy(zTa[:, :], bank[:, 6, :]).then_inc(s_zT, 1)
                act.wait_ge(s_zTps, g * 2 + 2)
                act.copy(zTb[0:CR, :], bank[0:CR, 7, :]).then_inc(s_zT, 1)

            def act_q(act, g):
                for c in range(HC):
                    act.wait_ge(s_qps, g * 5 + c + 1)
                    act.copy(qT[:, c, :], bank[:, 6 + c % 2, :]).then_inc(s_q, 1)
                for b in range(2):
                    act.wait_ge(s_qps, g * 5 + HC + b + 1)
                    act.copy(V[:, 2 * b:2 * b + 2, :, 0:HD],
                             bank[:, 6 + (HC + b) % 2, 0:2 * C].rearrange("p (j h d) -> p j h d", j=2, h=HEADS)).then_inc(s_q, 1)

            def act_exp(act, g, u):
                act.wait_ge(s_sub, g * UN + u + 1)
                act.activation(S[:, u % NE, :, :], S[:, u % NE, :, :], ACT.Exp, scale=HD ** -0.5).then_inc(s_exp, 1)

            def act_pT(act, g, u):
                n = g * UN + u
                act.wait_ge(s_pT, n + 1)
                act.copy(ST[:, u % 2, :, :], bank[:, 3 + u % 2, 0:HC * P].rearrange("p (c k) -> p c k", c=HC)).then_inc(s_pTc, 1)

            def act_aT(act, g, j):
                n = g * G + j
                act.wait_ge(s_aT, n + 1)
                act.copy(aTa[:, j % 2, :], bank[:, 7, 0:P]).then_inc(s_aTc, 1)
                act.copy(aTb[0:CR, j % 2, :], bank[0:CR, 7, P:2 * P]).then_inc(s_aTc, 1)

            def act_body(act, g, nxt):
                act_q(act, g)
                for u in range(UN):
                    act_exp(act, g, u)
                    if u >= 1:
                        act_pT(act, g, u - 1)
                    if u >= 6 and (u - 6) % RG == 0:
                        act_aT(act, g, (u - 6) // RG)
                    if u == 12 and nxt is not None:
                        act_keep(act, nxt)
                act_pT(act, g, UN - 1)
                act_aT(act, g, G - 1)
                if nxt is not None:
                    act_zT(act, nxt)

            @block.scalar
            def _(act):
                act_keep(act, 0)
                act_zT(act, 0)
                act_body(act, 0, 1)
                with act.Fori(1, NG - 1) as g:
                    act_body(act, g, g + 1)
                act_body(act, NG - 1, None)

            def pe_embed(pe, g):
                later = not isinstance(g, int) or g > 0
                pe.wait_ge(s_onehot, g * 2 + 2)
                if later:
                    pe.wait_ge(s_q, g * 5)
                for b in range(2):
                    for j in (2 * b, 2 * b + 1):
                        o = bank[:, 6 + b, (j % 2) * C:(j % 2 + 1) * C]
                        sl = slice(j * P, (j + 1) * P)
                        pe.matmul(o, oh_p[:, sl], posi_t[:, :], start=True, stop=False)
                        mm = pe.matmul(o, oh_d[:, sl], ds_t[:, :], start=False, stop=True)
                    mm.then_inc(s_embps, 1)

            def pe_zT(pe, g):
                pe.wait_ge(s_z, g * G + G)
                pe.wait_ge(s_emb, g * 2 + 2)
                if not isinstance(g, int) or g > 0:
                    pe.wait_ge(s_aTc, g * 2 * G)
                for j in range(G):
                    mm = pe.transpose(bank[:, 6, j * P:(j + 1) * P], z[:, j, 0:P], K.ident[:, :])
                mm.then_inc(s_zTps, 1)
                for j in range(G):
                    mm = pe.transpose(bank[0:CR, 7, j * P:(j + 1) * P], z[:, j, P:C], K.ident[:, :])
                mm.then_inc(s_zTps, 1)

            def pe_q(pe, g):
                pe.wait_ge(s_zT, g * 2 + 2)
                for c in range(HC):
                    if c == 2:
                        pe.wait_ge(s_q, g * 5 + 1)
                    o = bank[:, 6 + c % 2, :]
                    pe.matmul(o, wqp_a[:, c * P:(c + 1) * P], zTa[:, :], start=True, stop=False)
                    pe.matmul(o, wqp_b[:, c * P:(c + 1) * P], zTb[:, :], start=False, stop=True).then_inc(s_qps, 1)
                for b in range(2):
                    pe.wait_ge(s_q, g * 5 + 2 + b)
                    for j in (2 * b, 2 * b + 1):
                        o = bank[:, 6 + (HC + b) % 2, (j % 2) * C:(j % 2 + 1) * C]
                        sl = slice(j * P, (j + 1) * P)
                        pe.matmul(o, zTa[:, sl], wq_a[:, :], start=True, stop=False)
                        mm = pe.matmul(o, zTb[:, sl], wq_b[:, :], start=False, stop=True)
                    mm.then_inc(s_qps, 1)

            def pe_scores(pe, g, u):
                j, r = u // RG, u % RG
                n = g * UN + u
                if u == 0:
                    pe.wait_ge(s_q, g * 5 + 5)
                if u >= 2 or not isinstance(g, int) or g > 0:
                    pe.wait_ge(s_sub, n - 1)
                pe.matmul(bank[:, u % 2, 0:HC * P], K.identb[:, :], mask[:, :, :], start=True, stop=False)
                for c in range(HC):
                    q = qT[32 * r:32 * r + HD, c, j * P:(j + 1) * P]
                    mm = pe.matmul(bank[:, u % 2, c * P:(c + 1) * P], q, q, start=False, stop=(c == HC - 1))
                mm.then_inc(s_sc, 1)

            def pe_probsT(pe, g, u):
                n = g * UN + u
                pe.wait_ge(s_exp, n + 1)
                if u >= 2 or not isinstance(g, int) or g > 0:
                    pe.wait_ge(s_pTc, n - 1)
                for c in range(HC):
                    mm = pe.transpose(bank[:, 3 + u % 2, c * P:(c + 1) * P], S[:, u % NE, c, :], K.ident[:, :])
                mm.then_inc(s_pT, 1)

            def pe_pv(pe, g, u):
                j, r = u // RG, u % RG
                n = g * UN + u
                pe.wait_ge(s_pTc, n + 1)
                if r == 0 and (j >= 2 or not isinstance(g, int) or g > 0):
                    pe.wait_ge(s_out, g * G + j - 1)
                for c in range(HC):
                    h = RG * c + r
                    o = h * (HD + 1)
                    mm = pe.matmul(bank[:, OB[j % 2], o:o + HD + 1], ST[:, u % 2, c, :], V[:, j, h, :], start=True, stop=True)
                if r == RG - 1:
                    mm.then_inc(s_pv, 1)

            def pe_aT(pe, g, j, embedded):
                n = g * G + j
                pe.wait_ge(s_emb, (embedded + 1) * 2)
                pe.wait_ge(s_at, n + 1)
                if j >= 1 or not isinstance(g, int) or g > 0:
                    pe.wait_ge(s_aTc, 2 * n)
                pe.transpose(bank[:, 7, 0:P], at[:, j % 2, 0:P], K.ident[:, :])
                pe.transpose(bank[0:CR, 7, P:2 * P], at[:, j % 2, P:C], K.ident[:, :]).then_inc(s_aT, 1)

            def pe_proj(pe, g, j):
                n = g * G + j
                pe.wait_ge(s_aTc, 2 * n + 2)
                o = bank[:, OB[j % 2], 256:256 + C]
                pe.matmul(o, aTa[:, j % 2, :], wo_a[:, :], start=True, stop=False)
                pe.matmul(o, aTb[:, j % 2, :], wo_b[:, :], start=False, stop=True).then_inc(s_pr, 1)

            def pe_body(pe, g, nxt):
                pe_q(pe, g)
                for u in range(UN):
                    pe_scores(pe, g, u)
                    if u >= 1:
                        pe_probsT(pe, g, u - 1)
                    if u >= 2:
                        pe_pv(pe, g, u - 2)
                    if u >= 6 and (u - 6) % RG == 0:
                        pe_aT(pe, g, (u - 6) // RG, g if nxt is None else nxt)
                    if u >= 7 and (u - 7) % RG == 0:
                        pe_proj(pe, g, (u - 7) // RG)
                    if u == 3 and nxt is not None:
                        pe_embed(pe, nxt)
                pe_probsT(pe, g, UN - 1)
                pe_pv(pe, g, UN - 2)
                pe_pv(pe, g, UN - 1)
                pe_aT(pe, g, G - 1, g if nxt is None else nxt)
                pe_proj(pe, g, G - 1)
                if nxt is not None:
                    pe_zT(pe, nxt)

            @block.tensor
            def _(pe):
                pe_embed(pe, 0)
                pe_zT(pe, 0)
                pe_body(pe, 0, 1)
                with pe.Fori(1, NG - 1) as g:
                    pe_body(pe, g, g + 1)
                pe_body(pe, NG - 1, None)


def expert_phase(nc, name, A, H, bank, K, E, top, center, X, Y):
    NT = top * B * P // TOK + E - 1
    NJ = B * P // TOK
    with Phase(nc) as ctx:
        sb = lambda n, s, dt=F32: ctx.enter_context(nc.sbuf_tensor(f"{name}_{n}", s, dt))
        sem = lambda n: ctx.sem(f"{name}_{n}")
        pos_i = sb("pos_i", [P, top, B], I32)
        wgt = sb("wgt", [P, top, B])
        ex_i = sb("ex_i", [1, NT], I32)

        with Phase(nc) as c2:
            sb2 = lambda n, s, dt=F32: c2.enter_context(nc.sbuf_tensor(f"{name}_{n}", s, dt))
            Z = sb2("Z", [P, B, C])
            L = sb2("L", [P, E, B])
            router_pass(nc, name, A, H, bank, K, E, Z, L)
            routing(nc, name, A, bank, K, E, top, center, NT, NJ, L, pos_i, wgt, ex_i)
            scatter_rows(nc, name, top, Z, pos_i, X)
        X, Y = X[0:NT * TOK, :], Y[0:NT * TOK, :]
        expert_tiles(nc, name, A, bank, K, NT, ex_i, X, Y)
        combine(nc, name, H, top, pos_i, wgt, Y)


def router_pass(nc, name, A, H, bank, K, E, Z, L):
    with Phase(nc) as ctx:
        sb = lambda n, s, dt=F32: ctx.enter_context(nc.sbuf_tensor(f"{name}r_{n}", s, dt))
        sem = lambda n: ctx.sem(f"{name}r_{n}")
        gw_a, gw_b = sb("gw_a", [P, E]), sb("gw_b", [CR + 1, E])
        z = sb("z", [P, G, C])
        zTa, zTb = sb("zTa", [P, TOK]), sb("zTb", [CR + 1, TOK])
        ln = LayerNorm(nc, ctx, name + "_ln", 1e-5, K)
        loaded, ones = sem("loaded"), sem("ones")
        s_z, s_kept, s_zTps, s_zT, s_lg, s_L = (sem(n) for n in ("z_ready", "z_kept", "zTps_ready", "zT_ready", "logits_ready", "logits_kept"))

        with nc.Block() as block:
            @block.sync
            def _(sp):
                for dst, src in ((gw_a[:, :], A[name + "_gate"][0:P, :]), (gw_b[0:CR, :], A[name + "_gate"][P:C, :]),
                                 (gw_b[CR:CR + 1, :], A[name + "_gate_b"])):
                    sp.dma_start(dst, src).then_inc(loaded, 16)

            @block.gpsimd
            def _(pool):
                ln.rstd(pool, 0)
                with pool.Fori(1, NG) as g:
                    ln.rstd(pool, g)

            def dve_step(dve, g):
                later = not isinstance(g, int) or g > 0
                h = lambda j: H[:, bass.ds(g * G + j, 1), :].rearrange("p a c -> p (a c)")
                ln.stats(dve, g, h)
                if later:
                    dve.wait_ge(s_zTps, g * 2)
                    dve.wait_ge(s_kept, g)
                ln.normalise(dve, g, h, lambda j: z[:, j, :], s_z)

            @block.vector
            def _(dve):
                dve.memset(zTb[CR:CR + 1, :], 1.0).then_inc(ones, 1)
                dve_step(dve, 0)
                with dve.Fori(1, NG) as g:
                    dve_step(dve, g)

            def act_step(act, g):
                act.wait_ge(s_z, g * G + G)
                act.copy(Z[:, bass.ds(g * G, G), :], z[:, :, :]).then_inc(s_kept, 1)
                if not isinstance(g, int) or g > 0:
                    act.wait_ge(s_lg, g)
                act.wait_ge(s_zTps, g * 2 + 1)
                act.copy(zTa[:, :], bank[:, 0, :]).then_inc(s_zT, 1)
                act.wait_ge(s_zTps, g * 2 + 2)
                act.copy(zTb[0:CR, :], bank[0:CR, 1, :]).then_inc(s_zT, 1)
                act.wait_ge(s_lg, g + 1)
                act.copy(L[:, :, bass.ds(g * G, G)], bank[:, 2, 0:G * E].rearrange("p (j e) -> p e j", j=G)).then_inc(s_L, 1)

            @block.scalar
            def _(act):
                act_step(act, 0)
                with act.Fori(1, NG) as g:
                    act_step(act, g)

            def pe_step(pe, g):
                later = not isinstance(g, int) or g > 0
                pe.wait_ge(s_z, g * G + G)
                if later:
                    pe.wait_ge(s_zT, g * 2)
                for j in range(G):
                    mm = pe.transpose(bank[:, 0, j * P:(j + 1) * P], z[:, j, 0:P], K.ident[:, :])
                mm.then_inc(s_zTps, 1)
                for j in range(G):
                    mm = pe.transpose(bank[0:CR, 1, j * P:(j + 1) * P], z[:, j, P:C], K.ident[:, :])
                mm.then_inc(s_zTps, 1)
                pe.wait_ge(s_zT, g * 2 + 2)
                if later:
                    pe.wait_ge(s_L, g)
                for j in range(G):
                    sl = slice(j * P, (j + 1) * P)
                    o = bank[:, 2, j * E:(j + 1) * E]
                    pe.matmul(o, zTa[:, sl], gw_a[:, :], start=True, stop=False)
                    mm = pe.matmul(o, zTb[:, sl], gw_b[:, :], start=False, stop=True)
                mm.then_inc(s_lg, 1)

            @block.tensor
            def _(pe):
                pe.wait_ge(loaded, 48)
                pe.wait_ge(ones, 1)
                pe_step(pe, 0)
                with pe.Fori(1, NG) as g:
                    pe_step(pe, g)


def routing(nc, name, A, bank, K, E, top, center, NT, NJ, L, pos_i, wgt, ex_i):
    with Phase(nc) as ctx:
        sb = lambda n, s, dt=F32: ctx.enter_context(nc.sbuf_tensor(f"{name}q_{n}", s, dt))
        sem = lambda n: ctx.sem(f"{name}q_{n}")
        tri = sb("tri", [P, P])
        irow = sb("irow", [P, 64], I32)
        row = sb("row", [P, 64])
        prio, lim, cen = sb("prio", [P, E]), sb("lim", [P, NJ]), sb("cen", [P, E])
        keep = sb("keep", [P, E, B])
        m = sb("m", [P, 2, B])
        pm = sb("pm", [P, B])
        oh = sb("oh", [P, 2, E, B])
        tmp = sb("tmp", [P, E, B])
        Aall = sb("Aall", [P, E, B])
        cnt, incl, pos = sb("cnt", [P, E, B]), sb("incl", [P, E, B]), sb("pos", [P, E, B])
        gt = sb("gt", [P, E, NJ])
        tiles, tincl, tbase, one = sb("tiles", [P, E]), sb("tincl", [P, E]), sb("tbase", [P, E]), sb("one", [P, E])
        exc = sb("exc", [1, NT, E])
        exf = sb("exf", [1, NT])
        posf = sb("posf", [P, B])
        ew, den = sb("ew", [P, B]), sb("den", [P, B])
        s_tri, s_row, s_cen = sem("tri_zeroed"), sem("rows_ready"), sem("center_in")
        s_dif, s_exp, s_all, s_rank, s_step = sem("margin_ready"), sem("exp_ready"), sem("choice_ready"), sem("ranks_ready"), sem("dve_step")

        def over_e(x):
            return x.rearrange("p e t -> p t e")

        with nc.Block() as block:
            @block.gpsimd
            def _(pool):
                pool.memset(tri[:, :], 1.0).then_inc(s_tri, 1)
                pool.iota(irow[:, :], pattern=[[1, 64]], base=0, channel_multiplier=0).then_inc(s_tri, 1)
                pool.wait_ge(s_tri, 2)
                pool.affine_select(out=tri[:, :], in_=tri[:, :], compare_op=ALU.is_gt, fill=0.0, base=0,
                                   pattern=[[1, P]], channel_multiplier=-1).then_inc(s_row, 1)
                pool.tensor_copy(row[:, :], irow[:, :]).then_inc(s_row, 1)

            if center:
                @block.sync
                def _(sp):
                    sp.dma_start(cen[:, :], A[center].partition_broadcast(P)).then_inc(s_cen, 16)

            @block.scalar
            def _(act):
                if top == 2:
                    act.wait_ge(s_dif, 1)
                    act.activation(ew[:, :], posf[:, :], ACT.Exp).then_inc(s_exp, 1)

            @block.tensor
            def _(pe):
                pe.wait_ge(s_all, 1)
                pe.wait_ge(s_row, 2)
                a = Aall[:, :, :].rearrange("p e t -> p (e t)")
                pe.matmul(bank[:, 0, 0:E * B], tri[:, :], a, start=True, stop=True)
                pe.matmul(bank[:, 1, 0:E * B], K.ones[:, :], a, start=True, stop=True).then_inc(s_rank, 1)

            @block.vector
            def _(dve):
                done = [0]

                def step(ins):
                    done[0] += 1
                    ins.then_inc(s_step, 1)
                    dve.wait_ge(s_step, done[0])

                dve.wait_ge(s_row, 2)
                step(dve.tensor_scalar(prio[:, :], row[:, 0:E], -1.0, float(E), ALU.mult, ALU.add))
                step(dve.tensor_scalar(lim[:, :], row[:, 0:NJ], float(TOK), None, ALU.mult))
                step(dve.memset(one[:, :], 1.0))
                step(dve.memset(keep[:, :, :], 1.0))
                step(dve.memset(keep[:, :, 0:1], 0.0))
                if center:
                    dve.wait_ge(s_cen, 16)
                    step(dve.tensor_tensor(L[:, :, :], L[:, :, :], cen[:, :].unsqueeze(2).to_broadcast([P, E, B]), ALU.subtract))
                for k in range(top):
                    step(dve.reduce_max(m[:, k, :], over_e(L[:, :, :]), AX))
                    mk = m[:, k, :].unsqueeze(1).to_broadcast([P, E, B])
                    pb = prio[:, :].unsqueeze(2).to_broadcast([P, E, B])
                    step(dve.tensor_tensor(tmp[:, :, :], L[:, :, :], mk, ALU.is_equal))
                    step(dve.tensor_tensor(tmp[:, :, :], tmp[:, :, :], pb, ALU.mult))
                    step(dve.reduce_max(pm[:, :], over_e(tmp[:, :, :]), AX))
                    step(dve.tensor_tensor(oh[:, k, :, :], pb, pm[:, :].unsqueeze(1).to_broadcast([P, E, B]), ALU.is_equal))
                    if k == 0 and top == 2:
                        step(dve.scalar_tensor_tensor(L[:, :, :], oh[:, 0, :, :], -1.0e30, L[:, :, :], ALU.mult, ALU.add))
                if top == 2:
                    step(dve.tensor_tensor(posf[:, :], m[:, 1, :], m[:, 0, :], ALU.subtract))
                    dve.sem_inc(s_dif, 1)
                    step(dve.tensor_tensor(Aall[:, :, :], oh[:, 0, :, :], oh[:, 1, :, :], ALU.add))
                else:
                    step(dve.tensor_copy(Aall[:, :, :], oh[:, 0, :, :]))
                dve.sem_inc(s_all, 1)
                if top == 2:
                    dve.wait_ge(s_exp, 1)
                    step(dve.tensor_scalar(den[:, :], ew[:, :], 1.0, None, ALU.add))
                    step(dve.reciprocal(wgt[:, 0, :], den[:, :]))
                    step(dve.tensor_tensor(wgt[:, 1, :], ew[:, :], wgt[:, 0, :], ALU.mult))
                dve.wait_ge(s_rank, 1)
                flat = lambda x: x[:, :, :].rearrange("p e t -> p (e t)")
                step(dve.tensor_copy(flat(cnt), bank[:, 1, 0:E * B]))
                step(dve.tensor_tensor_scan(flat(incl), flat(keep), flat(cnt), 0.0, ALU.mult, ALU.add))
                step(dve.tensor_tensor(flat(pos), bank[:, 0, 0:E * B], flat(incl), ALU.add))
                step(dve.tensor_tensor(flat(pos), flat(pos), flat(cnt), ALU.subtract))
                total = incl[:, :, B - 1:B]
                step(dve.tensor_tensor(gt[:, :, :], total.to_broadcast([P, E, NJ]),
                                       lim[:, :].unsqueeze(1).to_broadcast([P, E, NJ]), ALU.is_gt))
                step(dve.reduce_sum(tiles[:, :], gt[:, :, :], AX))
                step(dve.tensor_tensor_scan(tincl[:, :], one[:, :], tiles[:, :], 0.0, ALU.mult, ALU.add))
                step(dve.tensor_tensor(tbase[:, :], tincl[:, :], tiles[:, :], ALU.subtract))
                step(dve.scalar_tensor_tensor(pos[:, :, :], tbase[:, :].unsqueeze(2).to_broadcast([P, E, B]), float(TOK),
                                              pos[:, :, :], ALU.mult, ALU.add))
                for k in range(top):
                    step(dve.tensor_tensor(tmp[:, :, :], oh[:, k, :, :], pos[:, :, :], ALU.mult))
                    step(dve.reduce_sum(posf[:, :], over_e(tmp[:, :, :]), AX))
                    step(dve.tensor_copy(pos_i[:, k, :], posf[:, :]))
                step(dve.tensor_tensor(exc[:, :, :], row[0:1, 0:NT].unsqueeze(2).to_broadcast([1, NT, E]),
                                       tincl[0:1, :].unsqueeze(1).to_broadcast([1, NT, E]), ALU.is_ge))
                step(dve.reduce_sum(exf[:, :], exc[:, :, :], AX))
                step(dve.tensor_scalar(ex_i[:, :], exf[:, :], float(E - 1), None, ALU.min))


def scatter_rows(nc, name, top, Z, pos_i, X):
    with Phase(nc) as ctx:
        sb = lambda n, s, dt=F32: ctx.enter_context(nc.sbuf_tensor(f"{name}s_{n}", s, dt))
        sem = lambda n: ctx.sem(f"{name}s_{n}")
        st = [sb(f"st{b}", [P, G, C]) for b in range(2)]
        idx = [sb(f"idx{b}", [P, top, G], I32) for b in range(2)]
        s_st, s_idx = sem("staged"), sem("idx_ready")
        s_sc = [sem(f"scattered{b}") for b in range(2)]
        n_dma = 16 * top * G

        def scatter(pool, i, b):
            g = i * 2 + b
            if not isinstance(i, int) or i > 0:
                pool.wait_ge(s_sc[b], i * n_dma)
            pool.tensor_copy(idx[b][:, :, :], pos_i[:, :, bass.ds(g * G, G)]).then_inc(s_idx, 1)
            pool.wait_ge(s_idx, g + 1)
            pool.wait_ge(s_st, g + 1)
            pool.sem_inc(s_alone, 1)
            for j in range(G):
                for k in range(top):
                    pool.indirect_dma_start(X, bass.IndirectOffsetOnAxis(idx[b][:, k, j:j + 1].bitcast(U32), 0),
                                            st[b][:, j, :], None).then_inc(s_sc[b], 16)

        s_alone = sem("stand_alone")
        with nc.Block() as block:
            @block.scalar
            def _(act):
                def pair(i):
                    for b in range(2):
                        if not isinstance(i, int) or i > 0:
                            act.wait_ge(s_sc[b], i * n_dma)
                            act.sem_inc(s_alone, 1)
                        act.copy(st[b][:, :, :], Z[:, bass.ds(i * (2 * G) + b * G, G), :]).then_inc(s_st, 1)
                pair(0)
                with act.Fori(1, NG // 2) as i:
                    pair(i)

            @block.gpsimd
            def _(pool):
                for b in range(2):
                    scatter(pool, 0, b)
                with pool.Fori(1, NG // 2) as i:
                    for b in range(2):
                        scatter(pool, i, b)
                for b in range(2):
                    pool.wait_ge(s_sc[b], NG // 2 * n_dma)


def expert_tiles(nc, name, A, bank, K, NT, ex_i, X, Y):
    with Phase(nc) as ctx:
        sb = lambda n, s, dt=F32: ctx.enter_context(nc.sbuf_tensor(f"{name}t_{n}", s, dt))
        sem = lambda n: ctx.sem(f"{name}t_{n}")
        two = range(2)
        w1a, w1b = [sb(f"w1a{b}", [P, HID]) for b in two], [sb(f"w1b{b}", [CR + 1, HID]) for b in two]
        w2, b2 = [sb(f"w2{b}", [P, HK, C]) for b in two], [sb(f"b2{b}", [P, C]) for b in two]
        x = [sb(f"x{b}", [P, G, C]) for b in two]
        y = [sb(f"y{b}", [P, G, C]) for b in two]
        xTa, xTb = [sb(f"xTa{b}", [P, TOK]) for b in two], [sb(f"xTb{b}", [CR + 1, TOK]) for b in two]
        h = [sb(f"h{b}", [P, HK, TOK]) for b in two]
        s_w, s_x, s_yout = ([sem(f"{n}{b}") for b in two] for n in ("w_in", "x_in", "y_stored"))
        s_ones, s_xTps, s_xT, s_h, s_gelu, s_yps, s_y = (
            sem(n) for n in ("ones", "xTps_ready", "xT_ready", "hidden_ready", "gelu_ready", "yps_ready", "y_ready"))
        Xv = X.rearrange("(s p j) c -> p s (j c)", p=P, j=G)
        Yv = Y.rearrange("(s p j) c -> p s (j c)", p=P, j=G)
        W1, B1, W2, B2 = (A[f"{name}_{n}"] for n in ("w1", "b1", "w2", "b2"))
        YB = (5, 6)

        def tiles(step):
            step(0, 0)
            step(0, 1)
            yield 1, NT // 2
            if NT % 2:
                step(NT // 2, 0)

        def run(eng, step):
            for lo, hi in tiles(step):
                with eng.Fori(lo, hi) as i:
                    step(i, 0)
                    step(i, 1)

        with nc.Block() as block:
            @block.sync
            def _(sp):
                def load(i, b):
                    s = i * 2 + b
                    e = sp.value_load(ex_i[0:1, bass.ds(s, 1)], min_val=0, max_val=A[f"{name}_w1"].shape[0] - 1)
                    if not isinstance(i, int) or i > 0:
                        sp.wait_ge(s_xTps, s * 2 - 2)
                    sp.dma_start(x[b][:, :, :].rearrange("p j c -> p (j c)"),
                                 Xv[:, bass.ds(s, 1), :].rearrange("p s n -> p (s n)")).then_inc(s_x[b], 16)
                    if not isinstance(i, int) or i > 0:
                        sp.wait_ge(s_y, (s - 1) * G)
                    sp.dma_start(w1a[b][:, :], W1[bass.ds(e, 1), 0:P, :].rearrange("a k n -> k (a n)")).then_inc(s_w[b], 16)
                    sp.dma_start(w1b[b][0:CR, :], W1[bass.ds(e, 1), P:C, :].rearrange("a k n -> k (a n)")).then_inc(s_w[b], 16)
                    sp.dma_start(w1b[b][CR:CR + 1, :], B1[bass.ds(e, 1), :]).then_inc(s_w[b], 16)
                    sp.dma_start(w2[b][:, :, :], W2[bass.ds(e, 1), :, :].rearrange("a (m p) c -> p (a m) c", p=P)).then_inc(s_w[b], 16)
                    sp.dma_start(b2[b][:, :], B2[bass.ds(e, 1), :].rearrange("a c -> (a c)").partition_broadcast(P)).then_inc(s_w[b], 16)
                run(sp, load)

            @block.gpsimd
            def _(pool):
                def store(i, b):
                    s = i * 2 + b
                    pool.wait_ge(s_y, s * G + G)
                    pool.dma_start(Yv[:, bass.ds(s, 1), :].rearrange("p s n -> p (s n)"),
                                   y[b][:, :, :].rearrange("p j c -> p (j c)")).then_inc(s_yout[b], 16)
                run(pool, store)
                for b in two:
                    pool.wait_ge(s_yout[b], 16 * ((NT + 1 - b) // 2))

            @block.vector
            def _(dve):
                def xT(i, b):
                    s = i * 2 + b
                    dve.wait_ge(s_xTps, s * 2 + 1)
                    if not isinstance(i, int) or i > 0:
                        dve.wait_ge(s_h, s * HK - HK)
                    dve.tensor_copy(xTa[b][:, :], bank[:, 0, :]).then_inc(s_xT, 1)
                    dve.wait_ge(s_xTps, s * 2 + 2)
                    dve.tensor_copy(xTb[b][0:CR, :], bank[0:CR, 1, :]).then_inc(s_xT, 1)

                def out(i, b):
                    s = i * 2 + b
                    if not isinstance(i, int) or i > 0:
                        dve.wait_ge(s_yout[b], i * 16)
                    for j in range(G):
                        dve.wait_ge(s_yps, s * G + j + 1)
                        dve.tensor_tensor(y[b][:, j, :], bank[:, YB[j % 2], 0:C], b2[b][:, :], ALU.add).then_inc(s_y, 1)

                for b in two:
                    dve.memset(xTb[b][CR:CR + 1, :], 1.0).then_inc(s_ones, 1)
                xT(0, 0)
                xT(0, 1)
                out(0, 0)
                def pair(i):
                    xT(i, 0)
                    out(i - 1, 1)
                    xT(i, 1)
                    out(i, 0)

                pair(1)
                with dve.Fori(2, NT // 2) as i:
                    pair(i)
                if NT % 2:
                    xT(NT // 2, 0)
                out(NT // 2 - 1, 1)
                if NT % 2:
                    out(NT // 2, 0)

            @block.scalar
            def _(act):
                def gelus(i, b):
                    s = i * 2 + b
                    if not isinstance(i, int) or i > 0:
                        act.wait_ge(s_yps, s * G - G)
                    for m in range(HK):
                        act.wait_ge(s_h, s * HK + m + 1)
                        act.activation(h[b][:, m, :], bank[:, 2 + m % 3, :], ACT.Gelu).then_inc(s_gelu, 1)
                run(act, gelus)

            @block.tensor
            def _(pe):
                def transposes(i, b):
                    s = i * 2 + b
                    pe.wait_ge(s_x[b], i * 16 + 16)
                    if not (isinstance(i, int) and i == 0 and b == 0):
                        pe.wait_ge(s_xT, s * 2)
                    for j in range(G):
                        mm = pe.transpose(bank[:, 0, j * P:(j + 1) * P], x[b][:, j, 0:P], K.ident[:, :])
                    mm.then_inc(s_xTps, 1)
                    for j in range(G):
                        mm = pe.transpose(bank[0:CR, 1, j * P:(j + 1) * P], x[b][:, j, P:C], K.ident[:, :])
                    mm.then_inc(s_xTps, 1)

                def first(i, b):
                    s = i * 2 + b
                    pe.wait_ge(s_w[b], i * 80 + 80)
                    pe.wait_ge(s_xT, s * 2 + 2)
                    for m in range(HK):
                        if m >= 3 or not (isinstance(i, int) and i == 0 and b == 0):
                            pe.wait_ge(s_gelu, s * HK + m - 2)
                        o = bank[:, 2 + m % 3, :]
                        ms = slice(m * P, (m + 1) * P)
                        pe.matmul(o, w1a[b][:, ms], xTa[b][:, :], start=True, stop=False)
                        pe.matmul(o, w1b[b][:, ms], xTb[b][:, :], start=False, stop=True).then_inc(s_h, 1)

                def second(i, b):
                    s = i * 2 + b
                    pe.wait_ge(s_gelu, s * HK + HK)
                    for j in range(G):
                        if j >= 2 or not (isinstance(i, int) and i == 0 and b == 0):
                            pe.wait_ge(s_y, s * G + j - 1)
                        for m in range(HK):
                            mm = pe.matmul(bank[:, YB[j % 2], 0:C], h[b][:, m, j * P:(j + 1) * P], w2[b][:, m, :],
                                           start=(m == 0), stop=(m == HK - 1))
                        mm.then_inc(s_yps, 1)

                pe.wait_ge(s_ones, 2)
                transposes(0, 0)
                first(0, 0)
                transposes(0, 1)
                second(0, 0)
                with pe.Fori(1, NT // 2) as i:
                    first(i - 1, 1)
                    transposes(i, 0)
                    second(i - 1, 1)
                    first(i, 0)
                    transposes(i, 1)
                    second(i, 0)
                first(NT // 2 - 1, 1)
                if NT % 2:
                    transposes(NT // 2, 0)
                second(NT // 2 - 1, 1)
                if NT % 2:
                    first(NT // 2, 0)
                    second(NT // 2, 0)


def combine(nc, name, H, top, pos_i, wgt, Y):
    with Phase(nc) as ctx:
        sb = lambda n, s, dt=F32: ctx.enter_context(nc.sbuf_tensor(f"{name}c_{n}", s, dt))
        sem = lambda n: ctx.sem(f"{name}c_{n}")
        yg = [sb(f"yg{b}", [P, G, top, C]) for b in range(2)]
        idx = [sb(f"idx{b}", [P, top, G], I32) for b in range(2)]
        s_idx, s_add, s_alone = sem("idx_ready"), sem("added"), sem("stand_alone")
        s_g = [sem(f"gathered{b}") for b in range(2)]
        n_dma = 16 * top * G
        adds = 1 if top == 1 else top * G

        with nc.Block() as block:
            @block.gpsimd
            def _(pool):
                def gather(i, b):
                    g = i * 2 + b
                    if not isinstance(i, int) or i > 0:
                        pool.wait_ge(s_add, (g - 1) * adds)
                    pool.tensor_copy(idx[b][:, :, :], pos_i[:, :, bass.ds(g * G, G)]).then_inc(s_idx, 1)
                    pool.wait_ge(s_idx, g + 1)
                    pool.sem_inc(s_alone, 1)
                    for j in range(G):
                        for k in range(top):
                            pool.indirect_dma_start(yg[b][:, j, k, :], None, Y,
                                                    bass.IndirectOffsetOnAxis(idx[b][:, k, j:j + 1].bitcast(U32), 0)).then_inc(s_g[b], 16)
                for b in range(2):
                    gather(0, b)
                with pool.Fori(1, NG // 2) as i:
                    for b in range(2):
                        gather(i, b)

            @block.vector
            def _(dve):
                def add(i, b):
                    g = i * 2 + b
                    dve.wait_ge(s_g[b], i * n_dma + n_dma)
                    if top == 1:
                        hs = H[:, bass.ds(g * G, G), :]
                        dve.tensor_tensor(hs, hs, yg[b][:, :, 0, :], ALU.add).then_inc(s_add, 1)
                        return
                    for k in range(top):
                        for j in range(G):
                            hs = H[:, bass.ds(g * G + j, 1), :].rearrange("p a c -> p (a c)")
                            if k:
                                dve.wait_ge(s_add, g * adds + j + 1)
                            dve.scalar_tensor_tensor(hs, yg[b][:, j, k, :], wgt[:, k, bass.ds(g * G + j, 1)], hs,
                                                     ALU.mult, ALU.add).then_inc(s_add, 1)
                for b in range(2):
                    add(0, b)
                with dve.Fori(1, NG // 2) as i:
                    for b in range(2):
                        add(i, b)


def mamba_phase(nc, A, H, bank, K):
    with Phase(nc) as ctx:
        sb = lambda n, s, dt=F32: ctx.enter_context(nc.sbuf_tensor(f"m_{n}", s, dt))
        sem = lambda n: ctx.sem(f"m_{n}")
        two = range(2)
        DC, NS, TAPS, R = 3, 16, 4, 12
        BC = 2 * NS
        MID, LO, HI, DT = 0, BC, 2 * BC, 3 * BC
        PW = P + 2 * (TAPS - 1)
        L1 = P + 1
        FL = DC * G * L1
        win_a, win_b = sb("win_a", [P, 2 * DC * P]), sb("win_b", [CR, 2 * DC * P])
        cw, cb = sb("cw", [P, DC, TAPS]), sb("cb", [P, DC])
        wx, wdt = sb("wx", [P, DC, DT + R]), sb("wdt", [DT + R, DC * P])
        bdt, Ac, Dp = sb("bdt", [P, DC]), sb("Ac", [P, DC, NS]), sb("Dp", [P, DC])
        wo = sb("wo", [P, DC, C])
        zTa, zTb = sb("zTa", [P, TOK]), sb("zTb", [CR, TOK])
        xp = sb("xp", [P, DC, G, PW])
        dg = sb("dg", [P, DC, TAPS, P])
        E3 = sb("E3", [DT, BC], BF16)
        e, w1 = sb("e", [P, DC, TOK]), sb("w1", [P, DC, TOK])
        z = sb("z", [P, G, C])
        xc = [sb(f"xc{d}", [P, DC, TOK]) for d in two]
        pdt = sb("pdt", [DT + R, TOK])
        rem = pdt[0:HI, :]
        parts = [sb(f"parts{d}", [DT, TOK], BF16) for d in two]
        r = sb("r", [P, DC, TOK])
        dt = [sb(f"dt{d}", [P, DC, TOK]) for d in two]
        u = [sb(f"u{d}", [P, DC, TOK]) for d in two]
        gz = sb("gz", [P, DC, TOK])
        ys = sb("ys", [P, DC, TOK])
        Bs = [sb(f"Bs{b}", [P, TOK]) for b in two]
        dA = [sb(f"dA{b}", [P, FL + 1]) for b in two]
        dBx = [sb(f"dBx{b}", [P, FL + 1]) for b in two]
        h = [sb(f"h{b}", [P, FL + 1]) for b in two]
        pr = [sb(f"pr{b}", [P, DC, TOK]) for b in two]
        ln = LayerNorm(nc, ctx, "m_ln", 1e-5, K)
        loaded, cleared, s_Ac = sem("loaded"), sem("cleared"), sem("A_ready")
        s_z, s_zTps, s_zT = sem("z_ready"), sem("zTps_ready"), sem("zT_ready")
        s_xps, s_xp, s_zps, s_zc, s_gz = sem("xps_ready"), sem("xp_ready"), sem("zps_ready"), sem("z_copied"), sem("gate_ready")
        s_cvps, s_cv, s_xc, s_pjps, s_part = (sem(n) for n in ("convps_ready", "conv_ready", "xc_ready", "pjps_ready", "part_steps"))
        s_pdt, s_rem, s_lo = sem("pdt_ready"), sem("rem_ready"), sem("lo_ready")
        s_dtps, s_abs, s_e, s_w1, s_ln, s_nc, s_sp = (sem(n) for n in ("dtps_ready", "abs_ready", "e_ready", "e1_ready", "ln_ready", "corr_ready", "dt_ready"))
        s_er, s_dBv, s_dg = sem("r_plus_e_ready"), sem("dBx_by_dve"), sem("E3_steps")
        s_u, s_xs = sem("u_ready"), sem("xs_ready")
        s_Bps, s_B, s_Cps, s_dA, s_dBx, s_h, s_pr, s_red = (
            sem(n) for n in ("Bps_ready", "B_ready", "Cps_ready", "dA_ready", "dBx_ready", "h_ready", "readout_ready", "summed"))
        s_ys, s_gy, s_ops, s_out = sem("y_ready"), sem("gated_ready"), sem("outps_ready"), sem("res_ready")

        def data(t):
            return t[:, 0:FL].rearrange("p (c b t) -> p c b t", c=DC, b=G)[:, :, :, 1:L1]

        def seqs(t):
            return t[:, :, :].rearrange("p c (b t) -> p c b t", b=G)

        with nc.Block() as block:
            @block.sync
            def _(sp):
                for dst, src in (
                    (win_a[:, :], A["m_WinT"][0:P, :]), (win_b[:, :], A["m_WinT"][P:C, :]),
                    (cw[:, :, :], A["m_conv_w"].rearrange("(c p) k -> p c k", p=P)),
                    (cb[:, :], A["m_conv_b"]),
                    *((wx[:, :, o:o + BC], A["m_WxT"][:, R:R + BC].rearrange("(c p) r -> p c r", p=P)) for o in (MID, LO, HI)),
                    (wx[:, :, DT:DT + R], A["m_WxT"][:, 0:R].rearrange("(c p) r -> p c r", p=P)),
                    (wdt[DT:DT + R, :], A["m_WdtT"]), (bdt[:, :], A["m_b_dt"]),
                    (Ac[:, :, :], A["m_A_log"].rearrange("(c p) n -> p c n", p=P)),
                    (Dp[:, :], A["m_D"]),
                    (wo[:, :, :], A["m_WoutT"].rearrange("(c p) n -> p c n", p=P)),
                ):
                    sp.dma_start(dst, src).then_inc(loaded, 16)

            @block.scalar
            def _(act):
                act.wait_ge(loaded, 16 * 13)
                act.activation(Ac[:, :, :], Ac[:, :, :], ACT.Exp).then_inc(s_Ac, 1)

            @block.vector
            def _(dve):
                for b in two:
                    dve.memset(dA[b][:, :], 0.0)
                    dve.memset(dBx[b][:, :], 0.0)
                dve.memset(xp[:, :, :, :], 0.0)
                dve.wait_ge(loaded, 16 * 13)
                for c in range(DC):
                    for k in range(TAPS):
                        dve.tensor_scalar(dg[:, c, k, :], K.ident[:, :], cw[:, c, k:k + 1], None, ALU.mult)
                dve.wait_ge(s_Ac, 1)
                dve.tensor_scalar(Ac[:, :, :], Ac[:, :, :], -1.0, None, ALU.mult)

            @block.gpsimd
            def _(pool):
                pool.memset(E3[:, :], 0.0).then_inc(s_dg, 1)
                for i, o in enumerate((MID, LO, HI)):
                    pool.wait_ge(s_dg, i + 1)
                    pool.affine_select(out=E3[o:o + BC, :], in_=E3[o:o + BC, :], compare_op=ALU.not_equal, fill=1.0,
                                       base=0, pattern=[[-1, BC]], channel_multiplier=1).then_inc(s_dg, 1)

        def chain(g, d, norm=True, first=False):
            q = g * 2 + d
            static = isinstance(g, int)
            gl = g + d
            hh = lambda j: H[:, bass.ds(gl * G + j, 1), :].rearrange("p a c -> p (a c)")

            def pe_conv(pe, c):
                i = q * DC + c
                s_used = s_xp if d == 0 else s_zc
                if c == 0:
                    pe.wait_ge(s_used, g * DC + 2)
                elif c == 1:
                    pe.wait_ge(s_used, g * DC + 3)
                else:
                    pe.wait_ge(s_cv, q * DC + 1)
                for k in range(TAPS):
                    o = k if d == 0 else 2 * (TAPS - 1) - k
                    mm = pe.matmul(bank[:, 7 - c % 2, :], dg[:, c, k, :], xp[:, c, :, o:o + P], start=(k == 0), stop=(k == TAPS - 1))
                mm.then_inc(s_cvps, 1)

            def act_conv(act, c):
                act.wait_ge(s_cvps, q * DC + c + 1)
                if c == 0 and (not static or g > 0):
                    act.wait_ge(s_xs, g)
                    act.wait_ge(s_u, q - 1)
                act.activation(xc[d][:, c, :], bank[:, 7 - c % 2, :], ACT.Identity, bias=cb[:, c:c + 1]).then_inc(s_cv, 1)

            def act_xc(act):
                act.wait_ge(s_cv, q * DC + DC)
                act.activation(xc[d][:, :, :], xc[d][:, :, :], ACT.Silu).then_inc(s_xc, 1)
                if d == 1:
                    act.wait_ge(s_zc, g * DC + DC)
                    act.activation(gz[:, :, :], gz[:, :, :], ACT.Silu).then_inc(s_gz, 1)

            def pe_proj(pe):
                pe.wait_ge(s_xc, q + 1)
                for c in range(DC):
                    mm = pe.matmul(bank[0:DT + R, 6, :], wx[:, c, :], xc[d][:, c, :], start=(c == 0), stop=(c == DC - 1))
                mm.then_inc(s_pjps, 1)

            def act_parts(act):
                act.wait_ge(s_pjps, q + 1)
                if not static or q > 0:
                    act.wait_ge(s_dtps, q * DC)
                act.copy(pdt[DT:DT + R, :], bank[DT:DT + R, 6, :]).then_inc(s_pdt, 1)
                if not static or g > 0:
                    act.wait_ge(s_Cps, (q - 1) * NS)
                act.copy(parts[d][:, :], bank[0:DT, 6, :]).then_inc(s_part, 1)

            def dve_rem(dve):
                dve.wait_ge(s_part, q * 2 + 1)
                dve.tensor_tensor(rem, bank[0:HI, 6, :], parts[d][0:HI, :], ALU.subtract).then_inc(s_rem, 1)

            def act_mid(act):
                act.wait_ge(s_rem, q + 1)
                act.copy(parts[d][0:HI, :], rem).then_inc(s_part, 1)

            def dve_lo(dve):
                dve.wait_ge(s_part, q * 2 + 2)
                v = parts[d][LO:HI, :]
                dve.tensor_tensor(v, pdt[LO:HI, :], v, ALU.subtract).then_inc(s_lo, 1)

            def pe_dt(pe, c):
                if c == 0:
                    pe.wait_ge(s_pdt, q + 1)
                elif c == 1:
                    pe.wait_ge(s_rem, q + 1)
                    pe.wait_ge(s_part, q * 2 + 1)
                else:
                    pe.wait_ge(s_abs, q * 2 * DC + 2)
                pe.matmul(bank[:, 7 - c % 2, :], wdt[DT:DT + R, c * P:(c + 1) * P], pdt[DT:DT + R, :], start=True, stop=True).then_inc(s_dtps, 1)

            def act_abs(act, c):
                act.wait_ge(s_dtps, q * DC + c + 1)
                if c == 0 and (not static or q > 0):
                    act.wait_ge(s_sp, q)
                act.activation(e[:, c, :], bank[:, 7 - c % 2, :], ACT.Abs, bias=bdt[:, c:c + 1]).then_inc(s_abs, 1)
                act.activation(r[:, c, :], bank[:, 7 - c % 2, :], ACT.Relu, bias=bdt[:, c:c + 1]).then_inc(s_abs, 1)

            def act_e(act):
                act.wait_ge(s_abs, (q + 1) * 2 * DC)
                act.activation(e[:, :, :], e[:, :, :], ACT.Exp, scale=-1.0).then_inc(s_e, 1)
                act.wait_ge(s_e, q + 1)
                act.activation(w1[:, :, :], e[:, :, :], ACT.Identity, bias=K.ones[:, 0:1]).then_inc(s_w1, 1)

            def act_ln(act):
                act.wait_ge(s_w1, q + 1)
                if not static or g > 0:
                    act.wait_ge(s_dA, (q - 1) * NS)
                act.activation(dt[d][:, :, :], w1[:, :, :], ACT.Ln).then_inc(s_ln, 1)

            def pool_er(pool):
                pool.wait_ge(s_e, q + 1)
                pool.tensor_tensor(r[:, :, :], r[:, :, :], e[:, :, :], ALU.add).then_inc(s_er, 1)

            def dve_dt(dve):
                dve.wait_ge(s_ln, q + 1)
                dve.scalar_tensor_tensor(w1[:, :, :], w1[:, :, :], -1.0, dt[d][:, :, :], ALU.add, ALU.subtract).then_inc(s_nc, 1)
                dve.wait_ge(s_nc, q + 1)
                dve.wait_ge(s_er, q + 1)
                dve.tensor_tensor(dt[d][:, :, :], r[:, :, :], w1[:, :, :], ALU.subtract).then_inc(s_sp, 1)

            def dve_u(dve):
                dve.wait_ge(s_sp, q + 1)
                if not static or g > 0:
                    wait_dBx(dve, g - 1, d, NS - 1)
                    wait_dBx(dve, g - 1, d, BY_DVE[-1])
                dve.tensor_tensor(u[d][:, :, :], dt[d][:, :, :], xc[d][:, :, :], ALU.mult).then_inc(s_u, 1)

            def dve_norm(dve):
                if not first:
                    dve.wait_ge(s_zTps, gl * 2)
                ln.normalise(dve, gl, hh, lambda j: z[:, j, :], s_z)

            def pe_zT(pe):
                pe.wait_ge(s_z, gl * G + G)
                if not first:
                    pe.wait_ge(s_abs, (q + 1) * 2 * DC)
                for j in range(G):
                    mm = pe.transpose(bank[:, 6, j * P:(j + 1) * P], z[:, j, 0:P], K.ident[:, :])
                mm.then_inc(s_zTps, 1)
                for j in range(G):
                    mm = pe.transpose(bank[0:CR, 7, j * P:(j + 1) * P], z[:, j, P:C], K.ident[:, :])
                mm.then_inc(s_zTps, 1)

            def act_zT(act):
                if not first:
                    act.wait_ge(s_zps, gl * DC)
                act.wait_ge(s_zTps, gl * 2 + 1)
                act.copy(zTa[:, :], bank[:, 6, :]).then_inc(s_zT, 1)
                act.wait_ge(s_zTps, gl * 2 + 2)
                act.copy(zTb[:, :], bank[0:CR, 7, :]).then_inc(s_zT, 1)

            def pe_in(pe, c):
                s_ps, s_used = (s_xps, s_xp) if d == 0 else (s_zps, s_zc)
                if c == 0:
                    pe.wait_ge(s_zT, g * 2 + 2)
                    if d == 1:
                        pe.wait_ge(s_abs, q * 2 * DC)
                if c == 2:
                    pe.wait_ge(s_used, g * DC + 1)
                m = slice((d * DC + c) * P, (d * DC + c + 1) * P)
                o = bank[:, 6 + c % 2, :]
                pe.matmul(o, win_a[:, m], zTa[:, :], start=True, stop=False)
                pe.matmul(o, win_b[:, m], zTb[:, :], start=False, stop=True).then_inc(s_ps, 1)

            def act_in(act, c):
                v = bank[:, 6 + c % 2, :]
                if d == 0:
                    act.wait_ge(s_xps, g * DC + c + 1)
                    if c == 0 and (not static or g > 0):
                        act.wait_ge(s_cvps, g * 2 * DC)
                    act.copy(xp[:, c, :, TAPS - 1:TAPS - 1 + P], v.rearrange("p (b t) -> p b t", b=G)).then_inc(s_xp, 1)
                else:
                    act.wait_ge(s_zps, g * DC + c + 1)
                    if c == 0 and (not static or g > 0):
                        act.wait_ge(s_gy, g)
                    act.copy(gz[:, c, :], v).then_inc(s_zc, 1)

            def pool_xs(pool):
                pool.wait_ge(s_xc, q + 1)
                if not static or g > 0:
                    pool.wait_ge(s_ops, g * 2)
                pool.tensor_tensor(ys[:, :, :], xc[0][:, :, :], xc[1][:, :, :], ALU.add).then_inc(s_xs, 1)

            W = {"pe": [], "act": [], "dve": [], "pool": []}
            def put(eng, unit, f, *a):
                W[eng].append((unit, f, a))

            if norm and (d == 1 or first):
                at = -8 if first else 8
                put("dve", at, lambda dve: ln.stats(dve, gl, hh))
                put("pool", at + 1, lambda pool: ln.rstd(pool, gl))
                put("dve", at + 2, dve_norm)
                put("pe", at + 6, pe_zT)
            if d == 0:
                put("act", 0, act_zT)
            put("pe", 0, pe_in, 0); put("pe", 0, pe_in, 1)
            put("act", 2, act_in, 0); put("act", 2, act_in, 1)
            put("pe", 2, pe_in, 2); put("pe", 3, pe_conv, 0)
            put("act", 4, act_in, 2); put("act", 5, act_conv, 0)
            put("pe", 4, pe_conv, 1); put("pe", 5, pe_conv, 2)
            put("act", 6, act_conv, 1); put("act", 7, act_conv, 2); put("act", 7, act_xc)
            put("pe", 7, pe_proj)
            put("act", 9, act_parts)
            put("dve", 9, dve_rem)
            put("pe", 9, pe_dt, 0)
            put("act", 11, act_mid); put("act", 11, act_abs, 0)
            put("dve", 11, dve_lo)
            put("pe", 11, pe_dt, 1); put("pe", 11, pe_dt, 2)
            put("act", 13, act_abs, 1); put("act", 13, act_abs, 2); put("act", 13, act_e)
            put("act", 14, act_ln)
            put("pool", 13, pool_er)
            put("dve", 14, dve_dt)
            put("dve", 14, dve_u)
            if d == 1:
                put("pool", 9, pool_xs)
            return W

        BY_DVE = (0, 4, 9, 14)
        by_dve = lambda n: sum(k <= n for k in BY_DVE)

        def ahead(g, d, n, k):
            n, d = (n + k) % NS, d + (n + k) // NS
            return g + d // 2, d % 2, n

        def first_two(g, d, n):
            return isinstance(g, int) and g == 0 and d == 0 and n < 2

        def wait_dBx(eng, g, d, n):
            q = g * 2 + d
            if n in BY_DVE:
                eng.wait_ge(s_dBv, q * len(BY_DVE) + by_dve(n))
            else:
                eng.wait_ge(s_dBx, q * (NS - len(BY_DVE)) + n + 1 - by_dve(n))

        def wait_dBx_before(eng, g, d, n, k):
            wait_dBx(eng, *ahead(g, d, n, -k))

        def pe_B(pe, g, d, n):
            N = (g * 2 + d) * NS + n
            if n == 0:
                pe.wait_ge(s_lo, g * 2 + d + 1)
            if not first_two(g, d, n) or n > 0:
                pe.wait_ge(s_B, N)
            pe.matmul(bank[:, 5, :], E3[:, n:n + 1].to_broadcast([DT, P]), parts[d][:, :], start=True, stop=True).then_inc(s_Bps, 1)

        def pe_C(pe, g, d, n):
            N = (g * 2 + d) * NS + n
            if not first_two(g, d, n):
                pe.wait_ge(s_pr, N - 1)
            pe.matmul(bank[:, 3 + n % 2, :], E3[:, NS + n:NS + n + 1].to_broadcast([DT, P]), parts[d][:, :],
                      start=True, stop=True).then_inc(s_Cps, 1)

        def pe_sum(pe, g, d, n):
            N = (g * 2 + d) * NS + n
            pe.wait_ge(s_pr, N + 1)
            if d == 0 and n == 0 and (not isinstance(g, int) or g > 0):
                pe.wait_ge(s_out, g * 2)
            for c in range(DC):
                mm = pe.matmul(bank[:, c, :], K.ident[:, :], pr[n % 2][:, c, :], start=(d == 0 and n == 0),
                               stop=(d == 1 and n == NS - 1))
            mm.then_inc(s_red, 1)

        def act_B(act, g, d, n):
            act.wait_ge(s_Bps, (g * 2 + d) * NS + n + 1)
            if not first_two(g, d, n):
                wait_dBx_before(act, g, d, n, 2)
            act.copy(Bs[n % 2][:, :], bank[:, 5, :]).then_inc(s_B, 1)

        def act_decay(act, g, d, n):
            N = (g * 2 + d) * NS + n
            if n == 0:
                act.wait_ge(s_sp, g * 2 + d + 1)
            if not first_two(g, d, n):
                act.wait_ge(s_h, N - 1)
            for c in range(DC):
                ins = act.activation(data(dA[n % 2])[:, c, :, :], seqs(dt[d])[:, c, :, :], ACT.Exp, scale=Ac[:, c, n:n + 1])
            ins.then_inc(s_dA, 1)

        def make_dBx(eng, g, d, n, done):
            N = (g * 2 + d) * NS + n
            if n < 2:
                eng.wait_ge(s_u, g * 2 + d + 1)
            eng.wait_ge(s_B, N + 1)
            if not first_two(g, d, n):
                eng.wait_ge(s_h, N - 1)
            bb = Bs[n % 2][:, :].rearrange("p (b t) -> p b t", b=G).unsqueeze(1).to_broadcast([P, DC, G, P])
            eng.tensor_tensor(data(dBx[n % 2]), seqs(u[d]), bb, ALU.mult).then_inc(done, 1)

        def dve_scan(dve, g, d, n):
            N = (g * 2 + d) * NS + n
            dve.wait_ge(s_dA, N + 1)
            wait_dBx(dve, g, d, n)
            if not first_two(g, d, n):
                dve.wait_ge(s_pr, N - 1)
            b = n % 2
            v = (lambda t: t[:, 0:FL]) if d == 0 else (lambda t: t[:, FL:0:-1])
            dve.tensor_tensor_scan(v(h[b]), v(dA[b]), v(dBx[b]), 0.0, ALU.mult, ALU.add).then_inc(s_h, 1)

        def dve_read(dve, g, d, n):
            N = (g * 2 + d) * NS + n
            early = isinstance(g, int) and g == 0 and d == 0 and n < 2
            dve.wait_ge(s_h, N + 1)
            dve.wait_ge(s_Cps, N + 1)
            if not early:
                dve.wait_ge(s_red, N - 1)
            cc = bank[:, 3 + n % 2, :].rearrange("p (b t) -> p b t", b=G).unsqueeze(1).to_broadcast([P, DC, G, P])
            dve.tensor_tensor(seqs(pr[n % 2]), data(h[n % 2]), cc, ALU.mult).then_inc(s_pr, 1)

        def dve_y(dve, g):
            dve.wait_ge(s_xs, g + 1)
            dve.wait_ge(s_red, (g + 1) * 2 * NS)
            for c in range(DC):
                dve.scalar_tensor_tensor(ys[:, c, :], ys[:, c, :], Dp[:, c:c + 1], bank[:, c, :], ALU.mult,
                                         ALU.add).then_inc(s_ys, 1)
            dve.wait_ge(s_ys, g * DC + DC)
            dve.wait_ge(s_gz, g + 1)
            dve.tensor_tensor(ys[:, :, :], ys[:, :, :], gz[:, :, :], ALU.mult).then_inc(s_gy, 1)

        def pe_out(pe, g):
            pe.wait_ge(s_gy, g + 1)
            for j in range(G):
                for c in range(DC):
                    mm = pe.matmul(bank[:, j // 2, (j % 2) * C:(j % 2 + 1) * C], ys[:, c, j * P:(j + 1) * P],
                                   wo[:, c, :], start=(c == 0), stop=(c == DC - 1))
                if j % 2:
                    mm.then_inc(s_ops, 1)

        def dve_out(dve, g):
            for b in two:
                dve.wait_ge(s_ops, g * 2 + b + 1)
                hs = H[:, bass.ds(g * G + 2 * b, 2), :]
                dve.scalar_tensor_tensor(hs, bank[:, b, 0:2 * C].rearrange("p (j c) -> p j c", j=2), 0.5, hs,
                                         ALU.mult, ALU.add).then_inc(s_out, 1)

        def in_order(steps):
            return sorted(steps, key=lambda s: s[0])

        def slot(eng, name, g, d, steps, main, last):
            pend = in_order(steps)
            for n in range(NS):
                now = [s for s in pend if s[0] == n]
                pend = pend[len(now):]
                main(eng, g, d, n, last and d == 1, lambda: [f(eng, *a) for _, f, a in now])
            assert not pend

        def program(eng, name, main, before, after):
            for _, f, a in in_order(chain(0, 0, first=True)[name]):
                f(eng, *a)
            before(eng)

            def group(g, last):
                slot(eng, name, g, 0, chain(g, 1, norm=not last)[name], main, last)
                slot(eng, name, g, 1, [] if last else chain(g + 1, 0)[name], main, last)

            group(0, False)
            with eng.Fori(1, NG - 1) as g:
                group(g, False)
            group(NG - 1, True)
            after(eng)

        def nothing(*a):
            pass

        def very_first(g, d, n):
            return isinstance(g, int) and (g, d, n) == (0, 0, 0)

        def after_group(g, d):
            return d == 0 and (not isinstance(g, int) or g > 0)

        LAST = (NG - 1, 1, NS - 1)
        with nc.Block() as block:
            @block.tensor
            def _(pe):
                def main(pe, g, d, n, end, prepare):
                    if not (end and n >= NS - 3):
                        pe_B(pe, *ahead(g, d, n, 3))
                    prepare()
                    if not (end and n >= NS - 1):
                        pe_C(pe, *ahead(g, d, n, 1))
                    if after_group(g, d) and n == 1:
                        pe_out(pe, g - 1)
                    elif not very_first(g, d, n):
                        if after_group(g, d) and n == 2:
                            pe_sum(pe, g, d, 0)
                        pe_sum(pe, *ahead(g, d, n, -1))

                def before(pe):
                    for n in range(3):
                        pe_B(pe, 0, 0, n)
                    pe_C(pe, 0, 0, 0)

                def after(pe):
                    pe_sum(pe, *LAST)
                    pe_out(pe, NG - 1)
                program(pe, "pe", main, before, after)

            @block.scalar
            def _(act):
                def main(act, g, d, n, end, prepare):
                    act_decay(act, g, d, n)
                    if not (end and n >= NS - 1):
                        act_B(act, *ahead(g, d, n, 1))
                    prepare()
                program(act, "act", main, lambda act: act_B(act, 0, 0, 0), nothing)

            @block.gpsimd
            def _(pool):
                def main(pool, g, d, n, end, prepare):
                    if n not in BY_DVE:
                        make_dBx(pool, g, d, n, s_dBx)
                    prepare()
                program(pool, "pool", main, nothing, nothing)

            @block.vector
            def _(dve):
                def main(dve, g, d, n, end, prepare):
                    dve_scan(dve, g, d, n)
                    if after_group(g, d) and n == 1:
                        dve_y(dve, g - 1)
                    if not very_first(g, d, n):
                        dve_read(dve, *ahead(g, d, n, -1))
                    if (n + 1) % NS in BY_DVE and not (end and n == NS - 1):
                        make_dBx(dve, *ahead(g, d, n, 1), s_dBv)
                    if after_group(g, d) and n == 2:
                        dve_out(dve, g - 1)
                    prepare()

                def before(dve):
                    make_dBx(dve, 0, 0, 0, s_dBv)

                def after(dve):
                    dve_read(dve, *LAST)
                    dve_y(dve, NG - 1)
                    dve_out(dve, NG - 1)
                program(dve, "dve", main, before, after)


def clear_slots(nc, X):
    n = X.shape[0] // P
    with Phase(nc) as ctx, nc.Block() as block:
        zr = ctx.enter_context(nc.sbuf_tensor("zero_rows", [P, n // 12 * C], F32))
        s_set, s_clr = ctx.sem("zr_set"), ctx.sem("x_cleared")

        @block.vector
        def _(dve):
            dve.memset(zr[:, :], 0.0).then_inc(s_set, 1)

        @block.sync
        def _(sp):
            sp.wait_ge(s_set, 1)
            v = X.rearrange("(q p r) c -> q p (r c)", q=12, p=P)
            for q in range(12):
                sp.dma_start(v[q, :, :], zr[:, :]).then_inc(s_clr, 16)
            sp.wait_ge(s_clr, 16 * 12)


def tower(nc, A, out, upto=4):
    with Phase(nc) as ctx:
        H = ctx.enter_context(nc.sbuf_tensor("H", [P, B, C], F32))
        bank = ctx.enter_context(nc.psum_tensor("bank", [P, 8, 512], F32))
        K = constants(nc, ctx, A)
        attention_phase(nc, A, H, bank, K)
        slots = (2 * B * P // TOK + E1 - 1) * TOK
        X = nc.dram_tensor("slots_x", (slots, C), F32).ap()
        Y = nc.dram_tensor("slots_y", (slots, C), F32).ap()
        clear_slots(nc, X)
        if upto > 1:
            expert_phase(nc, "f0", A, H, bank, K, E0, 1, "f0_center", X, Y)
        if upto > 2:
            mamba_phase(nc, A, H, bank, K)
        if upto > 3:
            expert_phase(nc, "f1", A, H, bank, K, E1, 2, None, X, Y)
        stored = ctx.sem("out_stored")
        with nc.Block() as block:
            @block.sync
            def _(sp):
                sp.dma_start(out.rearrange("(t p) c -> p t c", p=P), H[:, :, :]).then_inc(stored, 16)
                sp.wait_ge(stored, 16)


def layout(inputs):
    import numpy as np
    g = lambda n: np.asarray(inputs[n])
    c = np.ascontiguousarray
    return {
        "ids_wordT": c(g("x").T), "ids_posi": c(g("itok_BS_0_511").reshape(-1)),
        "ids_demo": c(g("itok_BS_0_255").reshape(-1)), "ids_seg": c(g("mask_BS_i1_0").reshape(-1)),
        "word_table": c(g("L0_tok_word_table")), "demo_table": c(g("L0_tok_demo_table")),
        "posi_table": c(g("L0_tok_posi_table")), "seg_table": c(g("L0_tok_seg_table")),
        "ln_gamma": c(g("L0_tok_ln_gamma")), "ln_beta": c(g("L0_tok_ln_beta")),
        "WqkvT": c(g("L0_attn_Wqkv_w").T), "bqkv": c(g("L0_attn_Wqkv_b").reshape(1, -1)),
        "WprojT": c(g("L0_attn_Wproj_w").T), "bproj": c(g("L0_attn_Wproj_b").reshape(1, -1)),
        "f0_gate": c(g("L0_ffn_gate_w")), "f0_gate_b": c(g("L0_ffn_gate_b").reshape(1, -1)),
        "f0_center": c(g("L0_ffn_gate_center")),
        "f0_w1": c(g("L0_ffn_w1")), "f0_b1": c(g("L0_ffn_b1")), "f0_w2": c(g("L0_ffn_w2")), "f0_b2": c(g("L0_ffn_b2")),
        "m_WinT": c(g("L1_attn_W_in").T), "m_conv_w": c(g("L1_attn_conv_w")), "m_conv_b": c(g("L1_attn_conv_b").reshape(-1, P).T),
        "m_WxT": c(g("L1_attn_W_xproj").T), "m_WdtT": c(g("L1_attn_W_dt").T), "m_b_dt": c(g("L1_attn_b_dt").reshape(-1, P).T),
        "m_A_log": c(g("L1_attn_A_log")), "m_D": c(g("L1_attn_D_param").reshape(-1, P).T), "m_WoutT": c(g("L1_attn_W_out").T),
        "f1_gate": c(g("L1_ffn_router_w")), "f1_gate_b": c(g("L1_ffn_router_b").reshape(1, -1)),
        "f1_w1": c(g("L1_ffn_w1")), "f1_b1": c(g("L1_ffn_b1")), "f1_w2": c(g("L1_ffn_w2")), "f1_b2": c(g("L1_ffn_b2")),
    }


def kernel(**inputs):
    import numpy as np
    import concourse.bacc as bacc
    from concourse.bass_utils import run_bass_kernel_spmd

    nc = bacc.Bacc("TRN2", target_bir_lowering=False, num_devices=1)
    arrays = layout(inputs)
    A = {n: nc.dram_tensor(n, a.shape, mybir.dt.from_np(a.dtype), kind="ExternalInput").ap() for n, a in arrays.items()}
    out = nc.dram_tensor("out", (B * P, C), F32, kind="ExternalOutput").ap()
    tower(nc, A, out)
    r = run_bass_kernel_spmd(nc, [arrays], core_ids=[0])
    return r.results[0]["out"].reshape(B, P, C)
```

```python
from contextlib import ExitStack

import concourse.bass as bass
from concourse import mybir

ALU = mybir.AluOpType
ACT = mybir.ActivationFunctionType
AX = mybir.AxisListType.X
F32 = mybir.dt.float32
BF16 = mybir.dt.bfloat16
I32 = mybir.dt.int32
U32 = mybir.dt.uint32

P = 128
B = 64
C = 192
CR = C - P
G = 4
NG = B // G
TOK = G * P
HEADS, HD = 12, 16
RG = 4
HC = HEADS // RG
HID = 768
HK = HID // P
E0, E1 = 4, 8
BIG = 1.0e10
SPARE = 13 * P


class Phase(ExitStack):

    def __init__(self, nc):
        super().__init__()
        self.nc, self.sems = nc, []

    def sem(self, name):
        self.sems.append(self.enter_context(self.nc.semaphore(name)))
        return self.sems[-1]

    def software(self, K, n):
        return [K.software.pop() for _ in range(n)]

    def __exit__(self, *exc):
        if exc[0] is None and self.sems:
            nums = sorted(s.num for s in self.sems)
            starts = [n for n in nums if n - 1 not in nums]
            ends = [n + 1 for n in nums if n + 1 not in nums]
            with self.nc.Block() as block:
                @block.gpsimd
                def _(pool):
                    for a, b in zip(starts, ends):
                        pool.sem_clear(range(a, b))
        return super().__exit__(*exc)


def stand_alone(eng, go):
    eng.sem_inc(go, 1)


class LayerNorm:

    def __init__(self, nc, ctx, name, eps, K):
        self.nc, self.eps, self.const, self.go = nc, eps, K.mhalf, K.go
        sb = lambda n, s: ctx.enter_context(nc.sbuf_tensor(f"{name}_{n}", s, F32))
        sem = lambda n: ctx.sem(f"{name}_{n}")
        self.bn = sb("bn", [P, G, 6])
        self.mv = sb("mv", [P, G, 2])
        self.ve = sb("ve", [P, G])
        self.rs = sb("rs", [P, G])
        self.bn_done, self.mv_done = sem("bn_done"), sem("mv_done")
        self.eps_done, self.rs_done = sem("eps_done"), sem("rs_done")

    def stats(self, dve, g, src):
        for j in range(G):
            dve.bn_stats(self.bn[:, j, :], src(j)).then_inc(self.bn_done, 1)
        for j in range(G):
            dve.wait_ge(self.bn_done, g * G + j + 1)
            stand_alone(dve, self.go)
            dve.bn_aggr(self.mv[:, j, :], self.bn[:, j, :]).then_inc(self.mv_done, 1)

    def rstd(self, pool, g):
        pool.wait_ge(self.mv_done, g * G + G)
        stand_alone(pool, self.go)
        pool.tensor_scalar(self.ve[:, :], self.mv[:, :, 1], self.eps, None, ALU.add).then_inc(self.eps_done, 1)
        pool.wait_ge(self.eps_done, g + 1)
        pool.tensor_tensor(self.rs[:, :], self.ve[:, :], self.const[:, 0:G], ALU.pow).then_inc(self.rs_done, 1)

    def normalise(self, dve, g, src, dst, done):
        dve.wait_ge(self.rs_done, g + 1)
        for j in range(G):
            dve.tensor_scalar(dst(j), src(j), self.mv[:, j, 0:1], self.rs[:, j:j + 1],
                              ALU.subtract, ALU.mult).then_inc(done, 1)


def constants(nc, ctx, A):
    sb = lambda n, s, dt=F32: ctx.enter_context(nc.sbuf_tensor(n, s, dt))
    sem = lambda n: ctx.sem(n)
    K = type("Constants", (), {})()
    K.ident = sb("ident", [P, P])
    K.identb = sb("identb", [P, P], BF16)
    K.mhalf = sb("mhalf", [P, G])
    K.ones = sb("ones", [P, P])
    K.go = sem("stand_alone")
    K.software = [sem(f"software_dma{b}") for b in range(10)]
    zeroed = sem("const_zeroed")
    with nc.Block() as block:
        @block.gpsimd
        def _(pool):
            pool.memset(K.ident[:, :], 0.0).then_inc(zeroed, 1)
            pool.memset(K.identb[:, :], 0.0).then_inc(zeroed, 1)
            pool.memset(K.mhalf[:, :], -0.5)
            pool.memset(K.ones[:, :], 1.0)
            pool.wait_ge(zeroed, 2)
            for t in (K.ident, K.identb):
                pool.affine_select(out=t[:, :], in_=t[:, :], compare_op=ALU.not_equal, fill=1.0, base=0,
                                   pattern=[[-1, P]], channel_multiplier=1)
    return K


def attention_phase(nc, A, H, bank, K, X0, X1):
    with Phase(nc) as ctx:
        sb = lambda n, s, dt=F32: ctx.enter_context(nc.sbuf_tensor(n, s, dt))
        sem = lambda n: ctx.sem(n)
        posi_t = sb("posi_t", [P, C])
        ds_t = sb("ds_t", [66, C])
        gam, bet = sb("gam", [P, C]), sb("bet", [P, C])
        wqp_a, wqp_b = sb("wqp_a", [P, HC * P]), sb("wqp_b", [CR + 1, HC * P])
        wq_a, wq_b = sb("wq_a", [P, C]), sb("wq_b", [CR + 1, C])
        wo_a, wo_b = sb("wo_a", [P, C]), sb("wo_b", [CR + 1, C])
        mask = sb("mask", [P, HC, P], BF16)
        col_i = sb("col_i", [P, 2], I32)
        col = sb("col", [P, 2])
        mul3 = sb("mul3", [66, 1])
        ids_w = sb("ids_w", [P, B], I32)
        idx = sb("idx", [P, G], I32)
        pid = sb("pid", [P, TOK], I32)
        did = sb("did", [66, TOK], I32)
        oh_p, oh_d = sb("oh_p", [P, TOK]), sb("oh_d", [66, TOK])
        word = sb("word", [P, G, C])
        emb = sb("emb", [P, G, C])
        xn = sb("xn", [P, G, C])
        h1 = sb("h1", [P, G, C])
        z = sb("z", [P, G, C])
        zTa, zTb = sb("zTa", [P, TOK]), sb("zTb", [CR + 1, TOK])
        V = [sb(f"V{i}", [P, G, HEADS, 32]) for i in range(2)]
        qT = [sb(f"qT{i}", [P, HC, TOK]) for i in range(2)]
        NE = 4
        mx = sb("mx", [P, NE, HC])
        S = sb("S", [P, NE, HC, P])
        ST = sb("ST", [P, NE, HC, P])
        OT = sb("OT", [P, 2, HC, P])
        ri = sb("ri", [P, 2, HEADS])
        at = sb("at", [P, 2, C])
        aTa, aTb = sb("aTa", [P, 2, P]), sb("aTb", [CR + 1, 2, P])
        ln_e = LayerNorm(nc, ctx, "ln_e", 1e-12, K)
        ln_a = LayerNorm(nc, ctx, "ln_a", 1e-5, K)

        R0, R1 = 4, SPARE // P
        zeros = sb("zeros", [P, R1, C + 1])
        s_zeros, s_clr = sem("zeros_set"), sem("slots_cleared")
        loaded, cleared, mul3_set = sem("a_loaded"), sem("a_cleared"), sem("mul3_set")
        s_ids, s_idx, s_word = sem("ids_in"), sem("idx_ready"), *ctx.software(K, 1)
        s_onehot, s_embps, s_emb = sem("onehot_ready"), sem("embps_ready"), sem("emb_ready")
        s_xn, s_gam, s_h1, s_h1kept = sem("xn_ready"), sem("gamma_done"), sem("h1_ready"), sem("h1_kept")
        s_z, s_zTps, s_zT = sem("z_ready"), sem("zTps_ready"), sem("zT_ready")
        s_qps, s_q = sem("qps_ready"), sem("q_ready")
        s_sc, s_mx, s_sub, s_exp = sem("scores_ready"), sem("max_ready"), sem("sub_ready"), sem("exp_ready")
        s_pT, s_pTc, s_pv = sem("probsT_ready"), sem("probsT_copied"), sem("pv_ready")
        s_OT, s_O, s_V = sem("heads_copied"), sem("heads_back"), sem("V_cleared")
        s_ri, s_at, s_aT, s_aTc = sem("rowsum_inv"), sem("att_ready"), sem("attT_ready"), sem("attT_copied")
        s_pr, s_out = sem("proj_ready"), sem("res_ready")

        OB = (5, 2)
        UN = G * RG
        LT, LP = 2, 4
        LC, LO, LA, LR = 7, 8, 9, 10

        with nc.Block() as block:
            @block.gpsimd
            def _(pool):
                pool.wait_ge(s_zeros, 1)
                pool.iota(zeros[:, :, C:C + 1].bitcast(I32), pattern=[[1, R1], [0, 1]], base=2 * B * P, channel_multiplier=R1).then_inc(s_zeros, 1)
                pool.memset(wqp_a[:, :], 0.0).then_inc(cleared, 1)
                pool.memset(wqp_b[:, :], 0.0).then_inc(cleared, 1)
                pool.memset(mask[:, :, :], 0.0).then_inc(cleared, 1)
                pool.iota(col_i[:, :], pattern=[[0, 2]], base=0, channel_multiplier=1).then_inc(cleared, 1)
                pool.wait_ge(cleared, 4)
                pool.affine_select(out=mask[:, :, :], in_=mask[:, :, :], compare_op=ALU.is_ge,
                                   fill=-4.0 * BIG, base=0, pattern=[[0, HC], [-1, P]], channel_multiplier=1).then_inc(cleared, 1)
                pool.wait_ge(cleared, 5)
                pool.iota(col_i[64:128, 1:2], pattern=[[0, 1]], base=0, channel_multiplier=1).then_inc(cleared, 1)
                pool.wait_ge(cleared, 6)
                pool.tensor_copy(col[:, :], col_i[:, :])

            @block.vector
            def _(dve):
                for v in V:
                    dve.memset(v[:, :, :, :], 0.0).then_inc(s_V, 1)
                dve.wait_ge(s_V, 2)
                for v in V:
                    dve.memset(v[:, :, :, HD:HD + 1], 1.0)
                dve.memset(zeros[:, :, :], 0.0).then_inc(s_zeros, 1)
                dve.memset(mul3[:, :], 3.0).then_inc(mul3_set, 1)
                dve.memset(zTb[CR:CR + 1, :], 1.0)
                dve.memset(aTb[CR:CR + 1, :, :], 1.0)
                dve.wait_ge(mul3_set, 1)
                dve.memset(mul3[64:66, :], 1.0)

            @block.sync
            def _(sp):
                n = 0
                sp.wait_ge(cleared, 4)
                for dst, src in (
                    (posi_t[:, :], A["posi_table"]), (ds_t[0:64, :], A["demo_table"]), (ds_t[64:66, :], A["seg_table"]),
                    (gam[:, :], A["ln_gamma"].partition_broadcast(P)), (bet[:, :], A["ln_beta"].partition_broadcast(P)),
                    (wq_a[:, :], A["WqkvT"][0:P, 0:C]), (wq_b[0:CR, :], A["WqkvT"][P:C, 0:C]),
                    (wq_b[CR:CR + 1, :], A["bqkv"][0:1, 0:C]),
                    (wqp_a[:, :].rearrange("p (h x) -> p h x", x=32)[:, :, 0:HD],
                     A["WqkvT"][0:P, 0:C].rearrange("k (h d) -> k h d", d=HD)),
                    (wqp_b[0:CR, :].rearrange("p (h x) -> p h x", x=32)[:, :, 0:HD],
                     A["WqkvT"][P:C, 0:C].rearrange("k (h d) -> k h d", d=HD)),
                    (wqp_b[CR:CR + 1, :].rearrange("p (h x) -> p h x", x=32)[:, :, 0:HD],
                     A["bqkv"][0:1, 0:C].rearrange("k (h d) -> k h d", d=HD)),
                    (wo_a[:, :], A["WprojT"][0:P, :]), (wo_b[0:CR, :], A["WprojT"][P:C, :]),
                    (wo_b[CR:CR + 1, :], A["bproj"]), (ids_w[:, :], A["ids_wordT"]),
                ):
                    sp.dma_start(dst, src).then_inc(loaded, 16)
                    n += 1
                sp.wait_ge(loaded, 16 * n)

        with nc.Block() as block:
            def tile(step, eng, g, u, lag):
                if (u - lag) % RG == 0:
                    j = (u - lag) // RG
                    if j < G and (not isinstance(g, int) or g * G + j >= 0):
                        step(eng, g + j // G if j < 0 else g, j % G if j < 0 else j)

            def unit(step, eng, g, u, lag):
                v = u - lag
                if v < UN and (not isinstance(g, int) or g * UN + v >= 0):
                    step(eng, g - 1 if v < 0 else g, v % UN)

            def every_group(eng, body):
                body(eng, 0, 1, 0, range(UN))
                with eng.Fori(0, NG // 2 - 1) as i:
                    body(eng, i * 2 + 1, i * 2 + 2, 1, range(UN))
                    body(eng, i * 2 + 2, i * 2 + 3, 0, range(UN))
                body(eng, NG - 1, None, 1, range(UN + LR + 2))

            first = lambda g: isinstance(g, int) and g == 0

            def ids_front(sp, g):
                if not isinstance(g, int) or g > 0:
                    sp.wait_ge(s_onehot, g * 2)
                sl = bass.ds(g * TOK, TOK)
                sp.dma_start(pid[:, :], A["ids_posi"][sl].partition_broadcast(P)).then_inc(s_ids, 16)
                sp.dma_start(did[0:64, :], A["ids_demo"][sl].partition_broadcast(64)).then_inc(s_ids, 16)
                sp.dma_start(did[64:66, :], A["ids_seg"][sl].partition_broadcast(2)).then_inc(s_ids, 16)

            @block.sync
            def _(sp):
                ids_front(sp, 0)
                sp.wait_ge(s_zeros, 2)
                n = 0
                for X, r, w in ((X0, R0, C), (X1, R1, C + 1)):
                    rows = X.rearrange("(q p r) c -> q p r c", r=r, p=P)
                    for q in range(X.shape[0] // (P * r)):
                        sp.dma_start(rows[q, :, :, :], zeros[:, 0:r, 0:w]).then_inc(s_clr, 16)
                        n += 16
                with sp.Fori(1, NG) as g:
                    ids_front(sp, g)
                sp.wait_ge(s_clr, n)

            def pool_front(pool, g):
                if not isinstance(g, int) or g > 0:
                    pool.wait_ge(s_emb, g * 2)
                pool.tensor_copy(idx[:, :], ids_w[:, bass.ds(g * G, G)]).then_inc(s_idx, 1)
                pool.wait_ge(s_idx, g + 1)
                stand_alone(pool, K.go)
                for j in range(G):
                    pool.indirect_dma_start(word[:, j, :], None, A["word_table"],
                                            bass.IndirectOffsetOnAxis(idx[:, j:j + 1].bitcast(U32), 0)).then_inc(s_word, 16)
                ln_e.rstd(pool, g)
                pool.wait_ge(s_xn, g * G + G)
                pool.tensor_tensor(xn[:, :, :], xn[:, :, :], gam[:, :].unsqueeze(1).to_broadcast([P, G, C]),
                                   ALU.mult).then_inc(s_gam, 1)
                pool.wait_ge(s_gam, g + 1)
                if not isinstance(g, int) or g > 0:
                    pool.wait_ge(s_h1kept, g)
                pool.tensor_tensor(h1[:, :, :], xn[:, :, :], bet[:, :].unsqueeze(1).to_broadcast([P, G, C]),
                                   ALU.add).then_inc(s_h1, 1)
                ln_a.rstd(pool, g)

            @block.gpsimd
            def _(pool):
                pool_front(pool, 0)
                with pool.Fori(1, NG) as g:
                    pool_front(pool, g)

            def dve_front(dve, g):
                later = not isinstance(g, int) or g > 0

                def onehots():
                    dve.wait_ge(s_ids, g * 48 + 48)
                    if later:
                        dve.wait_ge(s_embps, g * 2)
                    dve.tensor_scalar(oh_p[:, :], pid[:, :], col[:, 0:1], None, ALU.is_equal).then_inc(s_onehot, 1)
                    dve.tensor_scalar(oh_d[:, :], did[:, :], col[0:66, 1:2], mul3[:, :], ALU.is_equal,
                                      ALU.mult).then_inc(s_onehot, 1)

                def embed():
                    dve.wait_ge(s_word, g * 64 + 64)
                    for b in range(2):
                        dve.wait_ge(s_embps, g * 2 + b + 1)
                        dve.tensor_tensor(emb[:, 2 * b:2 * b + 2, :],
                                          bank[:, 6 + b, 0:2 * C].rearrange("p (j c) -> p j c", j=2),
                                          word[:, 2 * b:2 * b + 2, :], ALU.add).then_inc(s_emb, 1)

                def stats1():
                    dve.wait_ge(s_emb, g * 2 + 2)
                    ln_e.stats(dve, g, lambda j: emb[:, j, :])

                def norm1():
                    ln_e.normalise(dve, g, lambda j: emb[:, j, :], lambda j: xn[:, j, :], s_xn)

                def stats2():
                    dve.wait_ge(s_h1, g + 1)
                    ln_a.stats(dve, g, lambda j: h1[:, j, :])

                def norm2():
                    if later:
                        dve.wait_ge(s_zTps, g * 2)
                    ln_a.normalise(dve, g, lambda j: h1[:, j, :], lambda j: z[:, j, :], s_z)

                return {0: onehots, 2: embed, 3: stats1, 4: norm1, 7: stats2, 8: norm2}

            def dve_unit(dve, g, u):
                n = g * UN + u
                dve.wait_ge(s_sc, n + 1)
                s_ps = bank[:, u % 2, 0:HC * P].rearrange("p (c k) -> p c k", c=HC)
                if u >= NE or not isinstance(g, int) or g > 0:
                    dve.wait_ge(s_pT, n - NE + 1)
                dve.reduce_max(mx[:, u % NE, :], s_ps, AX).then_inc(s_mx, 1)
                dve.wait_ge(s_mx, n + 1)
                dve.tensor_tensor(S[:, u % NE, :, :], s_ps,
                                  mx[:, u % NE, :].unsqueeze(2).to_broadcast([P, HC, P]),
                                  ALU.subtract).then_inc(s_sub, 1)

            def dve_norm_att(dve, g, j):
                n = g * G + j
                O = bank[:, OB[j % 2], 0:HEADS * 32].rearrange("p (h d) -> p h d", h=HEADS)
                dve.wait_ge(s_O, n + 1)
                dve.reciprocal(ri[:, j % 2, :], O[:, :, HD]).then_inc(s_ri, 1)
                dve.wait_ge(s_ri, n + 1)
                if j >= 2 or not isinstance(g, int) or g > 0:
                    dve.wait_ge(s_aT, n - 1)
                dve.tensor_tensor(at[:, j % 2, :].rearrange("p (h d) -> p h d", h=HEADS), O[:, :, 0:HD],
                                  ri[:, j % 2, :].unsqueeze(2).to_broadcast([P, HEADS, HD]),
                                  ALU.mult).then_inc(s_at, 1)

            def dve_residual(dve, g, j):
                n = g * G + j
                if j == 0:
                    dve.wait_ge(s_h1kept, g + 1)
                dve.wait_ge(s_pr, n + 1)
                hs = H[:, bass.ds(g * G + j, 1), :]
                dve.tensor_tensor(hs, hs, bank[:, OB[j % 2], 256:256 + C].unsqueeze(1), ALU.add).then_inc(s_out, 1)

            def dve_body(dve, g, nxt, i, units):
                front = dve_front(dve, nxt) if nxt is not None else {}
                for u in units:
                    if u < UN:
                        dve_unit(dve, g, u)
                    if u in front:
                        front[u]()
                    for step, lag in ((dve_residual, LR + 1), (dve_norm_att, LO)):
                        tile(step, dve, g, u, lag)

            @block.vector
            def _(dve):
                for step in dve_front(dve, 0).values():
                    step()
                every_group(dve, dve_body)

            Q_AT = {11: (0, 1), 13: (2, 3), 15: (4,)}

            def act_keep(act, g):
                act.wait_ge(s_h1, g + 1)
                act.copy(H[:, bass.ds(g * G, G), :], h1[:, :, :]).then_inc(s_h1kept, 1)

            def act_zT(act, g):
                if not isinstance(g, int) or g > 0:
                    act.wait_ge(s_qps, g * 5)
                act.wait_ge(s_zTps, g * 2 + 1)
                act.copy(zTa[:, :], bank[:, 6, :]).then_inc(s_zT, 1)
                act.wait_ge(s_zTps, g * 2 + 2)
                act.copy(zTb[0:CR, :], bank[0:CR, 7, :]).then_inc(s_zT, 1)

            def act_q(act, g, i, k):
                act.wait_ge(s_qps, g * 5 + k + 1)
                if k < HC:
                    act.copy(qT[i][:, k, :], bank[:, 6 + k % 2, :]).then_inc(s_q, 1)
                else:
                    b = k - HC
                    act.copy(V[i][:, 2 * b:2 * b + 2, :, 0:HD],
                             bank[:, 6 + k % 2, 0:2 * C].rearrange("p (j h d) -> p j h d", j=2, h=HEADS)).then_inc(s_q, 1)

            def act_exp(act, g, u):
                act.wait_ge(s_sub, g * UN + u + 1)
                act.activation(S[:, u % NE, :, :], S[:, u % NE, :, :], ACT.Exp, scale=HD ** -0.5).then_inc(s_exp, 1)

            def act_pT(act, g, u):
                n = g * UN + u
                act.wait_ge(s_pT, n + 1)
                act.copy(ST[:, u % NE, :, :], bank[:, 3 + u % 2, 0:HC * P].rearrange("p (c k) -> p c k", c=HC)).then_inc(s_pTc, 1)

            def act_OT(act, g, j):
                n = g * G + j
                act.wait_ge(s_pv, n + 1)
                if j >= 2 or not isinstance(g, int) or g > 0:
                    act.wait_ge(s_O, n - 1)
                act.copy(OT[:, j % 2, :, :], bank[:, OB[j % 2], 0:HC * P].rearrange("p (c q) -> p c q", c=HC)).then_inc(s_OT, 1)

            def act_aT(act, g, j):
                n = g * G + j
                act.wait_ge(s_aT, n + 1)
                act.copy(aTa[:, j % 2, :], bank[:, OB[j % 2], 0:P]).then_inc(s_aTc, 1)
                act.copy(aTb[0:CR, j % 2, :], bank[0:CR, OB[j % 2], P:2 * P]).then_inc(s_aTc, 1)

            def act_body(act, g, nxt, i, units):
                for u in units:
                    if u < UN:
                        act_exp(act, g, u)
                    unit(act_pT, act, g, u, LT)
                    tile(act_OT, act, g, u, LC)
                    tile(act_aT, act, g, u, LA)
                    if u == 0 and not first(g):
                        act_q(act, g, i, HC + 1)
                    if nxt is not None:
                        if u == 7:
                            act_keep(act, nxt)
                        elif u == 10:
                            act_zT(act, nxt)
                        elif u - 1 in Q_AT:
                            for k in Q_AT[u - 1]:
                                act_q(act, nxt, 1 - i, k)

            @block.scalar
            def _(act):
                act_keep(act, 0)
                act_zT(act, 0)
                for k in range(HC + 2):
                    act_q(act, 0, 0, k)
                every_group(act, act_body)

            def pe_embed(pe, g):
                later = not isinstance(g, int) or g > 0
                pe.wait_ge(s_onehot, g * 2 + 2)
                if later:
                    pe.wait_ge(s_q, g * 5)
                for b in range(2):
                    for j in (2 * b, 2 * b + 1):
                        o = bank[:, 6 + b, (j % 2) * C:(j % 2 + 1) * C]
                        sl = slice(j * P, (j + 1) * P)
                        pe.matmul(o, oh_p[:, sl], posi_t[:, :], start=True, stop=False)
                        mm = pe.matmul(o, oh_d[:, sl], ds_t[:, :], start=False, stop=True)
                    mm.then_inc(s_embps, 1)

            def pe_zT(pe, g):
                pe.wait_ge(s_z, g * G + G)
                pe.wait_ge(s_emb, g * 2 + 2)
                for j in range(G):
                    mm = pe.transpose(bank[:, 6, j * P:(j + 1) * P], z[:, j, 0:P], K.ident[:, :])
                mm.then_inc(s_zTps, 1)
                for j in range(G):
                    mm = pe.transpose(bank[0:CR, 7, j * P:(j + 1) * P], z[:, j, P:C], K.ident[:, :])
                mm.then_inc(s_zTps, 1)

            def pe_q(pe, g, k):
                if k == 0:
                    pe.wait_ge(s_zT, g * 2 + 2)
                if k >= 2:
                    pe.wait_ge(s_q, g * 5 + k - 1)
                if k < HC:
                    o = bank[:, 6 + k % 2, :]
                    pe.matmul(o, wqp_a[:, k * P:(k + 1) * P], zTa[:, :], start=True, stop=False)
                    pe.matmul(o, wqp_b[:, k * P:(k + 1) * P], zTb[:, :], start=False, stop=True).then_inc(s_qps, 1)
                else:
                    for j in (2 * (k - HC), 2 * (k - HC) + 1):
                        o = bank[:, 6 + k % 2, (j % 2) * C:(j % 2 + 1) * C]
                        sl = slice(j * P, (j + 1) * P)
                        pe.matmul(o, zTa[:, sl], wq_a[:, :], start=True, stop=False)
                        mm = pe.matmul(o, zTb[:, sl], wq_b[:, :], start=False, stop=True)
                    mm.then_inc(s_qps, 1)

            def pe_scores(pe, g, u, i):
                j, r = u // RG, u % RG
                n = g * UN + u
                if u == 0:
                    pe.wait_ge(s_q, g * 5 + HC)
                if u >= 2 or not isinstance(g, int) or g > 0:
                    pe.wait_ge(s_sub, n - 1)
                pe.matmul(bank[:, u % 2, 0:HC * P], K.identb[:, :], mask[:, :, :], start=True, stop=False)
                for c in range(HC):
                    q = qT[i][32 * r:32 * r + HD, c, j * P:(j + 1) * P]
                    mm = pe.matmul(bank[:, u % 2, c * P:(c + 1) * P], q, q, start=False, stop=(c == HC - 1))
                mm.then_inc(s_sc, 1)

            def pe_probsT(pe, g, u):
                n = g * UN + u
                pe.wait_ge(s_exp, n + 1)
                if u >= 2 or not isinstance(g, int) or g > 0:
                    pe.wait_ge(s_pTc, n - 1)
                for c in range(HC):
                    mm = pe.transpose(bank[:, 3 + u % 2, c * P:(c + 1) * P], S[:, u % NE, c, :], K.ident[:, :])
                mm.then_inc(s_pT, 1)

            def pe_pv(pe, g, u, i):
                j, r = u // RG, u % RG
                n = g * UN + u
                pe.wait_ge(s_pTc, n + 1)
                if r == 0 and j % 2 == 0:
                    pe.wait_ge(s_q, g * 5 + HC + j // 2 + 1)
                if r == 0 and (j >= 2 or not isinstance(g, int) or g > 0):
                    pe.wait_ge(s_out, g * G + j - 1)
                for c in range(HC):
                    h = RG * c + r
                    mm = pe.matmul(bank[32 * r:32 * r + 32, OB[j % 2], c * P:(c + 1) * P], V[i][:, j, h, :], ST[:, u % NE, c, :],
                                   start=True, stop=True)
                if r == RG - 1:
                    mm.then_inc(s_pv, 1)

            def pe_O(pe, g, j):
                pe.wait_ge(s_OT, g * G + j + 1)
                for c in range(HC):
                    mm = pe.transpose(bank[:, OB[j % 2], c * P:(c + 1) * P], OT[:, j % 2, c, :], K.ident[:, :])
                mm.then_inc(s_O, 1)

            def pe_aT(pe, g, j):
                pe.wait_ge(s_at, g * G + j + 1)
                pe.transpose(bank[:, OB[j % 2], 0:P], at[:, j % 2, 0:P], K.ident[:, :])
                pe.transpose(bank[0:CR, OB[j % 2], P:2 * P], at[:, j % 2, P:C], K.ident[:, :]).then_inc(s_aT, 1)

            def pe_proj(pe, g, j):
                n = g * G + j
                pe.wait_ge(s_aTc, 2 * n + 2)
                o = bank[:, OB[j % 2], 256:256 + C]
                pe.matmul(o, aTa[:, j % 2, :], wo_a[:, :], start=True, stop=False)
                pe.matmul(o, aTb[:, j % 2, :], wo_b[:, :], start=False, stop=True).then_inc(s_pr, 1)

            def pe_body(pe, g, nxt, i, units):
                for u in units:
                    if u < UN:
                        pe_scores(pe, g, u, i)
                    unit(pe_probsT, pe, g, u, LT)
                    tile(pe_aT, pe, g, u, LA)
                    tile(pe_proj, pe, g, u, LR)
                    unit(lambda pe, g, v: pe_pv(pe, g, v, i if u >= LP else 1 - i), pe, g, u, LP)
                    tile(pe_O, pe, g, u, LO)
                    if nxt is not None:
                        if u == 1:
                            pe_embed(pe, nxt)
                        elif u == 9:
                            pe_zT(pe, nxt)
                        elif u in Q_AT:
                            for k in Q_AT[u]:
                                pe_q(pe, nxt, k)

            @block.tensor
            def _(pe):
                pe_embed(pe, 0)
                pe_zT(pe, 0)
                for k in range(HC + 2):
                    pe_q(pe, 0, k)
                every_group(pe, pe_body)


def expert_tiles_of(E, top):
    return top * B * P // TOK + E - 1


def expert_phase(nc, name, A, H, bank, K, E, top, center, X, Y, pos_i=None, out=None):
    NT = expert_tiles_of(E, top)
    NJ = B * P // TOK
    with Phase(nc) as ctx:
        sb = lambda n, s, dt=F32: ctx.enter_context(nc.sbuf_tensor(f"{name}_{n}", s, dt))
        homing = pos_i is None
        if homing:
            pos_i = sb("pos_i", [P, top, B], I32)
        wgt = sb("wgt", [P, top, B])
        ex_i = sb("ex_i", [1, NT], I32)

        with Phase(nc) as c2:
            sb2 = lambda n, s, dt=F32: c2.enter_context(nc.sbuf_tensor(f"{name}_{n}", s, dt))
            Z = sb2("Z", [P, B, C])
            L = sb2("L", [P, E, B])
            router_pass(nc, name, A, H, bank, K, E, Z, L)
            routing(nc, name, A, bank, K, E, top, center, NT, NJ, L, pos_i, wgt, ex_i)
            scatter_rows(nc, name, K, top, Z, pos_i, X)
        expert_tiles(nc, name, A, bank, K, NT, ex_i, X, Y)
        if homing:
            combine(nc, name, H, top, wgt, Y, out)


def router_pass(nc, name, A, H, bank, K, E, Z, L):
    with Phase(nc) as ctx:
        sb = lambda n, s, dt=F32: ctx.enter_context(nc.sbuf_tensor(f"{name}r_{n}", s, dt))
        sem = lambda n: ctx.sem(f"{name}r_{n}")
        two = range(2)
        gw_a, gw_b = sb("gw_a", [P, E]), sb("gw_b", [CR + 1, E])
        z = [sb(f"z{b}", [P, G, C]) for b in two]
        zTa, zTb = [sb(f"zTa{b}", [P, TOK]) for b in two], [sb(f"zTb{b}", [CR + 1, TOK]) for b in two]
        lgT = [sb(f"lgT{b}", [E, TOK]) for b in two]
        ln = [LayerNorm(nc, ctx, f"{name}_ln{b}", 1e-5, K) for b in two]
        loaded, ones = sem("loaded"), sem("ones")
        s_z, s_kept, s_zTps, s_zT, s_lg, s_L = (sem(n) for n in ("z_ready", "z_kept", "zTps_ready", "zT_ready", "logits_ready", "logits_kept"))
        s_lT = sem("logitsT_ready")
        s_lTc = sem("logitsT_copied")
        PAIRS = NG // 2

        def pairs(eng, body):
            body(0, True, False)
            with eng.Fori(1, PAIRS - 1) as i:
                body(i, False, False)
            body(PAIRS - 1, False, True)

        with nc.Block() as block:
            @block.sync
            def _(sp):
                for dst, src in ((gw_a[:, :], A[name + "_gate"][0:P, :]), (gw_b[0:CR, :], A[name + "_gate"][P:C, :]),
                                 (gw_b[CR:CR + 1, :], A[name + "_gate_b"])):
                    sp.dma_start(dst, src).then_inc(loaded, 16)

            @block.gpsimd
            def _(pool):
                def body(i, first, last):
                    for b in two:
                        ln[b].rstd(pool, i)
                pairs(pool, body)

            @block.vector
            def _(dve):
                def rows(i, b):
                    return lambda j: H[:, bass.ds((i * 2 + b) * G + j, 1), :].rearrange("p a c -> p (a c)")

                def norm(i, b, first):
                    g = i * 2 + b
                    if not first:
                        dve.wait_ge(s_zTps, (g - 1) * 2)
                        dve.wait_ge(s_kept, g - 1)
                    ln[b].normalise(dve, i, rows(i, b), lambda j: z[b][:, j, :], s_z)

                def body(i, first, last):
                    ln[1].stats(dve, i, rows(i, 1))
                    norm(i, 0, first)
                    if not last:
                        ln[0].stats(dve, i + 1, rows(i + 1, 0))
                    norm(i, 1, first)

                for b in two:
                    dve.memset(zTb[b][CR:CR + 1, :], 1.0).then_inc(ones, 1)
                ln[0].stats(dve, 0, rows(0, 0))
                pairs(dve, body)

            @block.scalar
            def _(act):
                def zT(i, b, first):
                    g = i * 2 + b
                    act.wait_ge(s_z, g * G + G)
                    act.copy(Z[:, bass.ds(g * G, G), :], z[b][:, :, :]).then_inc(s_kept, 1)
                    if not first:
                        act.wait_ge(s_lT, g - 1)
                    act.wait_ge(s_zTps, g * 2 + 1)
                    act.copy(zTa[b][:, :], bank[:, 3 * b, :]).then_inc(s_zT, 1)
                    act.wait_ge(s_zTps, g * 2 + 2)
                    act.copy(zTb[b][0:CR, :], bank[0:CR, 3 * b + 1, :]).then_inc(s_zT, 1)

                def lT(i, b):
                    act.wait_ge(s_lT, i * 2 + b + 1)
                    act.copy(lgT[b][:, :], bank[0:E, 3 * b + 2, :]).then_inc(s_lTc, 1)

                def keep(i, b):
                    g = i * 2 + b
                    act.wait_ge(s_lg, g + 1)
                    act.copy(L[:, :, bass.ds(g * G, G)], bank[:, 3 * b + 2, 0:G * E].rearrange("p (j e) -> p e j", j=G)).then_inc(s_L, 1)

                def body(i, first, last):
                    zT(i, 0, first)
                    if not first:
                        lT(i - 1, 1)
                        keep(i - 1, 0)
                    zT(i, 1, first)
                    lT(i, 0)
                    if not first:
                        keep(i - 1, 1)
                pairs(act, body)
                lT(PAIRS - 1, 1)
                for b in two:
                    keep(PAIRS - 1, b)

            @block.tensor
            def _(pe):
                def transposes(i, b, first):
                    g = i * 2 + b
                    pe.wait_ge(s_z, g * G + G)
                    if not first:
                        pe.wait_ge(s_zT, (g - 1) * 2)
                    for j in range(G):
                        mm = pe.transpose(bank[:, 3 * b, j * P:(j + 1) * P], z[b][:, j, 0:P], K.ident[:, :])
                    mm.then_inc(s_zTps, 1)
                    for j in range(G):
                        mm = pe.transpose(bank[0:CR, 3 * b + 1, j * P:(j + 1) * P], z[b][:, j, P:C], K.ident[:, :])
                    mm.then_inc(s_zTps, 1)

                def logits(i, b, first):
                    g = i * 2 + b
                    pe.wait_ge(s_zT, g * 2 + 2)
                    if not first:
                        pe.wait_ge(s_L, g - 1)
                    pe.matmul(bank[0:E, 3 * b + 2, :], gw_a[:, :], zTa[b][:, :], start=True, stop=False)
                    pe.matmul(bank[0:E, 3 * b + 2, :], gw_b[:, :], zTb[b][:, :], start=False, stop=True).then_inc(s_lT, 1)

                def back(i, b):
                    pe.wait_ge(s_lTc, i * 2 + b + 1)
                    stand_alone(pe, K.go)
                    for j in range(G):
                        mm = pe.transpose(bank[:, 3 * b + 2, j * E:(j + 1) * E], lgT[b][:, j * P:(j + 1) * P], K.ident[0:E, 0:E])
                    mm.then_inc(s_lg, 1)

                def body(i, first, last):
                    transposes(i, 1, first)
                    if not first:
                        back(i - 1, 1)
                    logits(i, 0, first)
                    if not last:
                        transposes(i + 1, 0, False)
                    back(i, 0)
                    logits(i, 1, first)

                pe.wait_ge(loaded, 48)
                pe.wait_ge(ones, 2)
                transposes(0, 0, True)
                pairs(pe, body)
                back(PAIRS - 1, 1)


def routing(nc, name, A, bank, K, E, top, center, NT, NJ, L, pos_i, wgt, ex_i):
    with Phase(nc) as ctx:
        sb = lambda n, s, dt=F32: ctx.enter_context(nc.sbuf_tensor(f"{name}q_{n}", s, dt))
        sem = lambda n: ctx.sem(f"{name}q_{n}")
        tri = sb("tri", [P, P])
        irow = sb("irow", [P, 64], I32)
        row = sb("row", [P, 64])
        prio, lim, cen = sb("prio", [P, E]), sb("lim", [P, NJ]), sb("cen", [P, E])
        keep = sb("keep", [P, E, B])
        m = sb("m", [P, 2, B])
        pm = sb("pm", [P, B])
        oh = sb("oh", [P, 2, E, B])
        tmp = sb("tmp", [P, E, B])
        Aall = sb("Aall", [P, E, B])
        cnt, incl, pos = sb("cnt", [P, E, B]), sb("incl", [P, E, B]), sb("pos", [P, E, B])
        gt = sb("gt", [P, E, NJ])
        tiles, tincl, tbase, one = sb("tiles", [P, E]), sb("tincl", [P, E]), sb("tbase", [P, E]), sb("one", [P, E])
        exc = sb("exc", [1, NT, E])
        exf = sb("exf", [1, NT])
        posf = sb("posf", [P, B])
        ew, den = sb("ew", [P, B]), sb("den", [P, B])
        s_tri, s_row, s_cen = sem("tri_zeroed"), sem("rows_ready"), sem("center_in")
        s_dif, s_exp, s_all, s_rank, s_step = sem("margin_ready"), sem("exp_ready"), sem("choice_ready"), sem("ranks_ready"), sem("dve_step")

        def over_e(x):
            return x.rearrange("p e t -> p t e")

        with nc.Block() as block:
            @block.gpsimd
            def _(pool):
                pool.memset(tri[:, :], 1.0).then_inc(s_tri, 1)
                pool.iota(irow[:, :], pattern=[[1, 64]], base=0, channel_multiplier=0).then_inc(s_tri, 1)
                pool.wait_ge(s_tri, 2)
                pool.affine_select(out=tri[:, :], in_=tri[:, :], compare_op=ALU.is_gt, fill=0.0, base=0,
                                   pattern=[[1, P]], channel_multiplier=-1).then_inc(s_row, 1)
                pool.tensor_copy(row[:, :], irow[:, :]).then_inc(s_row, 1)

            if center:
                @block.sync
                def _(sp):
                    sp.dma_start(cen[:, :], A[center].partition_broadcast(P)).then_inc(s_cen, 16)

            @block.scalar
            def _(act):
                if top == 2:
                    act.wait_ge(s_dif, 1)
                    act.activation(ew[:, :], posf[:, :], ACT.Exp).then_inc(s_exp, 1)

            @block.tensor
            def _(pe):
                pe.wait_ge(s_all, 1)
                pe.wait_ge(s_row, 2)
                a = Aall[:, :, :].rearrange("p e t -> p (e t)")
                pe.matmul(bank[:, 0, 0:E * B], tri[:, :], a, start=True, stop=True)
                pe.matmul(bank[:, 1, 0:E * B], K.ones[:, :], a, start=True, stop=True).then_inc(s_rank, 1)

            @block.vector
            def _(dve):
                done = [0]

                def step(ins):
                    done[0] += 1
                    ins.then_inc(s_step, 1)
                    dve.wait_ge(s_step, done[0])

                dve.wait_ge(s_row, 2)
                step(dve.tensor_scalar(prio[:, :], row[:, 0:E], -1.0, float(E), ALU.mult, ALU.add))
                step(dve.tensor_scalar(lim[:, :], row[:, 0:NJ], float(TOK), None, ALU.mult))
                step(dve.memset(one[:, :], 1.0))
                step(dve.memset(keep[:, :, :], 1.0))
                step(dve.memset(keep[:, :, 0:1], 0.0))
                if center:
                    dve.wait_ge(s_cen, 16)
                    step(dve.tensor_tensor(L[:, :, :], L[:, :, :], cen[:, :].unsqueeze(2).to_broadcast([P, E, B]), ALU.subtract))
                for k in range(top):
                    step(dve.reduce_max(m[:, k, :], over_e(L[:, :, :]), AX))
                    mk = m[:, k, :].unsqueeze(1).to_broadcast([P, E, B])
                    pb = prio[:, :].unsqueeze(2).to_broadcast([P, E, B])
                    step(dve.tensor_tensor(tmp[:, :, :], L[:, :, :], mk, ALU.is_equal))
                    step(dve.tensor_tensor(tmp[:, :, :], tmp[:, :, :], pb, ALU.mult))
                    step(dve.reduce_max(pm[:, :], over_e(tmp[:, :, :]), AX))
                    step(dve.tensor_tensor(oh[:, k, :, :], pb, pm[:, :].unsqueeze(1).to_broadcast([P, E, B]), ALU.is_equal))
                    if k == 0 and top == 2:
                        step(dve.scalar_tensor_tensor(L[:, :, :], oh[:, 0, :, :], -1.0e30, L[:, :, :], ALU.mult, ALU.add))
                if top == 2:
                    step(dve.tensor_tensor(posf[:, :], m[:, 1, :], m[:, 0, :], ALU.subtract))
                    dve.sem_inc(s_dif, 1)
                    step(dve.tensor_tensor(Aall[:, :, :], oh[:, 0, :, :], oh[:, 1, :, :], ALU.add))
                else:
                    step(dve.tensor_copy(Aall[:, :, :], oh[:, 0, :, :]))
                dve.sem_inc(s_all, 1)
                if top == 2:
                    dve.wait_ge(s_exp, 1)
                    step(dve.tensor_scalar(den[:, :], ew[:, :], 1.0, None, ALU.add))
                    step(dve.reciprocal(wgt[:, 0, :], den[:, :]))
                    step(dve.tensor_tensor(wgt[:, 1, :], ew[:, :], wgt[:, 0, :], ALU.mult))
                dve.wait_ge(s_rank, 1)
                flat = lambda x: x[:, :, :].rearrange("p e t -> p (e t)")
                step(dve.tensor_copy(flat(cnt), bank[:, 1, 0:E * B]))
                step(dve.tensor_tensor_scan(flat(incl), flat(keep), flat(cnt), 0.0, ALU.mult, ALU.add))
                step(dve.tensor_tensor(flat(pos), bank[:, 0, 0:E * B], flat(incl), ALU.add))
                step(dve.tensor_tensor(flat(pos), flat(pos), flat(cnt), ALU.subtract))
                total = incl[:, :, B - 1:B]
                step(dve.tensor_tensor(gt[:, :, :], total.to_broadcast([P, E, NJ]),
                                       lim[:, :].unsqueeze(1).to_broadcast([P, E, NJ]), ALU.is_gt))
                step(dve.reduce_sum(tiles[:, :], gt[:, :, :], AX))
                step(dve.tensor_tensor_scan(tincl[:, :], one[:, :], tiles[:, :], 0.0, ALU.mult, ALU.add))
                step(dve.tensor_tensor(tbase[:, :], tincl[:, :], tiles[:, :], ALU.subtract))
                step(dve.scalar_tensor_tensor(pos[:, :, :], tbase[:, :].unsqueeze(2).to_broadcast([P, E, B]), float(TOK),
                                              pos[:, :, :], ALU.mult, ALU.add))
                for k in range(top):
                    step(dve.tensor_tensor(tmp[:, :, :], oh[:, k, :, :], pos[:, :, :], ALU.mult))
                    step(dve.reduce_sum(posf[:, :], over_e(tmp[:, :, :]), AX))
                    step(dve.tensor_copy(pos_i[:, k, :], posf[:, :]))
                step(dve.tensor_tensor(exc[:, :, :], row[0:1, 0:NT].unsqueeze(2).to_broadcast([1, NT, E]),
                                       tincl[0:1, :].unsqueeze(1).to_broadcast([1, NT, E]), ALU.is_ge))
                step(dve.reduce_sum(exf[:, :], exc[:, :, :], AX))
                step(dve.tensor_scalar(ex_i[:, :], exf[:, :], float(E - 1), None, ALU.min))


def scatter_rows(nc, name, K, top, Z, pos_i, X):
    with Phase(nc) as ctx:
        sb = lambda n, s, dt=F32: ctx.enter_context(nc.sbuf_tensor(f"{name}s_{n}", s, dt))
        sem = lambda n: ctx.sem(f"{name}s_{n}")
        homing = X.shape[1] > C
        copies = top if homing else 1
        st = [[sb(f"st{b}{k}", [P, G, X.shape[1]]) for k in range(copies)] for b in range(2)]
        home = [sb(f"home{k}", [P, B], I32) for k in range(copies)]
        s_home = sem("home_ready")
        marks = 1 + copies if homing else 1
        idx = [sb(f"idx{b}", [P, top, G], I32) for b in range(2)]
        s_st, s_idx = sem("staged"), sem("idx_ready")
        s_sc = ctx.software(K, 2)
        n_dma = 16 * top * G

        def scatter(pool, i, b):
            g = i * 2 + b
            if not isinstance(i, int) or i > 0:
                pool.wait_ge(s_sc[b], i * n_dma)
            pool.tensor_copy(idx[b][:, :, :], pos_i[:, :, bass.ds(g * G, G)]).then_inc(s_idx, 1)
            if homing:
                for k in range(copies):
                    pool.tensor_copy(st[b][k][:, :, C:C + 1].bitcast(I32), home[k][:, bass.ds(g * G, G)].unsqueeze(2)).then_inc(s_idx, 1)
            pool.wait_ge(s_idx, (g + 1) * marks)
            pool.wait_ge(s_st, (g + 1) * copies)
            pool.sem_inc(s_alone, 1)
            for j in range(G):
                for k in range(top):
                    pool.indirect_dma_start(X, bass.IndirectOffsetOnAxis(idx[b][:, k, j:j + 1].bitcast(U32), 0),
                                            st[b][k % copies][:, j, :], None).then_inc(s_sc[b], 16)

        s_alone = sem("stand_alone")
        with nc.Block() as block:
            @block.scalar
            def _(act):
                def pair(i):
                    for b in range(2):
                        if not isinstance(i, int) or i > 0:
                            act.wait_ge(s_sc[b], i * n_dma)
                            act.sem_inc(s_alone, 1)
                        for t in st[b]:
                            act.copy(t[:, :, 0:C], Z[:, bass.ds(i * (2 * G) + b * G, G), :]).then_inc(s_st, 1)
                pair(0)
                with act.Fori(1, NG // 2) as i:
                    pair(i)

            @block.gpsimd
            def _(pool):
                if homing:
                    for k in range(copies):
                        pool.iota(home[k][:, :], pattern=[[top * P, B]], base=k, channel_multiplier=top).then_inc(s_home, 1)
                    pool.wait_ge(s_home, copies)
                for b in range(2):
                    scatter(pool, 0, b)
                with pool.Fori(1, NG // 2) as i:
                    for b in range(2):
                        scatter(pool, i, b)
                for b in range(2):
                    pool.wait_ge(s_sc[b], NG // 2 * n_dma)


def expert_tiles(nc, name, A, bank, K, NT, ex_i, X, Y):
    with Phase(nc) as ctx:
        sb = lambda n, s, dt=F32: ctx.enter_context(nc.sbuf_tensor(f"{name}t_{n}", s, dt))
        sem = lambda n: ctx.sem(f"{name}t_{n}")
        two = range(2)
        w1a, w1b = [sb(f"w1a{b}", [P, HID]) for b in two], [sb(f"w1b{b}", [CR + 1, HID]) for b in two]
        w2, b2 = [sb(f"w2{b}", [P, HK, C]) for b in two], [sb(f"b2{b}", [P, C]) for b in two]
        homing = X.shape[1] > C
        x = [sb(f"x{b}", [P, G, X.shape[1]]) for b in two]
        home = [sb(f"home{b}", [P, G], I32) for b in two]
        NY = 16 * G if homing else 16
        s_home = sem("home_ready")
        y = [sb(f"y{b}", [P, G, C]) for b in two]
        xTa, xTb = [sb(f"xTa{b}", [P, TOK]) for b in two], [sb(f"xTb{b}", [CR + 1, TOK]) for b in two]
        h = [sb(f"h{b}", [P, HK, TOK]) for b in two]
        s_w, s_x = ([sem(f"{n}{b}") for b in two] for n in ("w_in", "x_in"))
        s_yout = ctx.software(K, 2)
        s_ones, s_xTps, s_xT, s_h, s_gelu, s_yps, s_y = (
            sem(n) for n in ("ones", "xTps_ready", "xT_ready", "hidden_ready", "gelu_ready", "yps_ready", "y_ready"))
        Xv = X.rearrange("(s p j) c -> p s (j c)", p=P, j=G)
        Yv = None if homing else Y.rearrange("(s p j) c -> p s (j c)", p=P, j=G)
        W1, B1, W2, B2 = (A[f"{name}_{n}"] for n in ("w1", "b1", "w2", "b2"))
        YB = (5, 6)

        def tiles(step):
            step(0, 0)
            step(0, 1)
            yield 1, NT // 2
            if NT % 2:
                step(NT // 2, 0)

        def run(eng, step):
            for lo, hi in tiles(step):
                with eng.Fori(lo, hi) as i:
                    step(i, 0)
                    step(i, 1)

        with nc.Block() as block:
            @block.sync
            def _(sp):
                def load(i, b):
                    s = i * 2 + b
                    e = sp.value_load(ex_i[0:1, bass.ds(s, 1)], min_val=0, max_val=A[f"{name}_w1"].shape[0] - 1)
                    if not isinstance(i, int) or i > 0:
                        sp.wait_ge(s_xTps, s * 2 - 2)
                        if homing:
                            stand_alone(sp, K.go)
                            sp.wait_ge(s_home, s - 1)
                    sp.dma_start(x[b][:, :, :].rearrange("p j c -> p (j c)"),
                                 Xv[:, bass.ds(s, 1), :].rearrange("p s n -> p (s n)")).then_inc(s_x[b], 16)
                    if not isinstance(i, int) or i > 0:
                        sp.wait_ge(s_y, (s - 1) * G)
                    sp.dma_start(w1a[b][:, :], W1[bass.ds(e, 1), 0:P, :].rearrange("a k n -> k (a n)")).then_inc(s_w[b], 16)
                    sp.dma_start(w1b[b][0:CR, :], W1[bass.ds(e, 1), P:C, :].rearrange("a k n -> k (a n)")).then_inc(s_w[b], 16)
                    sp.dma_start(w1b[b][CR:CR + 1, :], B1[bass.ds(e, 1), :]).then_inc(s_w[b], 16)
                    sp.dma_start(w2[b][:, :, :], W2[bass.ds(e, 1), :, :].rearrange("a (m p) c -> p (a m) c", p=P)).then_inc(s_w[b], 16)
                    sp.dma_start(b2[b][:, :], B2[bass.ds(e, 1), :].rearrange("a c -> (a c)").partition_broadcast(P)).then_inc(s_w[b], 16)
                run(sp, load)

            @block.gpsimd
            def _(pool):
                def store(i, b):
                    s = i * 2 + b
                    if homing:
                        pool.wait_ge(s_x[b], i * 16 + 16)
                        if not isinstance(i, int) or i > 0:
                            pool.wait_ge(s_yout[b], i * NY)
                        stand_alone(pool, K.go)
                        pool.tensor_copy(home[b][:, :].unsqueeze(2), x[b][:, :, C:C + 1].bitcast(I32)).then_inc(s_home, 1)
                        pool.wait_ge(s_home, s + 1)
                        pool.wait_ge(s_y, s * G + G)
                        stand_alone(pool, K.go)
                        for j in range(G):
                            pool.indirect_dma_start(Y, bass.IndirectOffsetOnAxis(home[b][:, j:j + 1].bitcast(U32), 0),
                                                    y[b][:, j, :], None).then_inc(s_yout[b], 16)
                        return
                    pool.wait_ge(s_y, s * G + G)
                    pool.dma_start(Yv[:, bass.ds(s, 1), :].rearrange("p s n -> p (s n)"),
                                   y[b][:, :, :].rearrange("p j c -> p (j c)")).then_inc(s_yout[b], 16)
                run(pool, store)
                for b in two:
                    pool.wait_ge(s_yout[b], NY * ((NT + 1 - b) // 2))

            @block.vector
            def _(dve):
                def xT(i, b):
                    s = i * 2 + b
                    dve.wait_ge(s_xTps, s * 2 + 1)
                    if not isinstance(i, int) or i > 0:
                        dve.wait_ge(s_h, s * HK - HK)
                    dve.tensor_copy(xTa[b][:, :], bank[:, 0, :]).then_inc(s_xT, 1)
                    dve.wait_ge(s_xTps, s * 2 + 2)
                    dve.tensor_copy(xTb[b][0:CR, :], bank[0:CR, 1, :]).then_inc(s_xT, 1)

                def out(i, b):
                    s = i * 2 + b
                    if not isinstance(i, int) or i > 0:
                        dve.wait_ge(s_yout[b], i * NY)
                    for j in range(G):
                        dve.wait_ge(s_yps, s * G + j + 1)
                        dve.tensor_tensor(y[b][:, j, :], bank[:, YB[j % 2], 0:C], b2[b][:, :], ALU.add).then_inc(s_y, 1)

                for b in two:
                    dve.memset(xTb[b][CR:CR + 1, :], 1.0).then_inc(s_ones, 1)
                xT(0, 0)
                xT(0, 1)
                out(0, 0)
                def pair(i):
                    xT(i, 0)
                    out(i - 1, 1)
                    xT(i, 1)
                    out(i, 0)

                pair(1)
                with dve.Fori(2, NT // 2) as i:
                    pair(i)
                if NT % 2:
                    xT(NT // 2, 0)
                out(NT // 2 - 1, 1)
                if NT % 2:
                    out(NT // 2, 0)

            @block.scalar
            def _(act):
                def gelus(i, b):
                    s = i * 2 + b
                    if not isinstance(i, int) or i > 0:
                        act.wait_ge(s_yps, s * G - G)
                    for m in range(HK):
                        act.wait_ge(s_h, s * HK + m + 1)
                        act.activation(h[b][:, m, :], bank[:, 2 + m % 3, :], ACT.Gelu).then_inc(s_gelu, 1)
                run(act, gelus)

            @block.tensor
            def _(pe):
                def transposes(i, b):
                    s = i * 2 + b
                    pe.wait_ge(s_x[b], i * 16 + 16)
                    if not (isinstance(i, int) and i == 0 and b == 0):
                        pe.wait_ge(s_xT, s * 2)
                    for j in range(G):
                        mm = pe.transpose(bank[:, 0, j * P:(j + 1) * P], x[b][:, j, 0:P], K.ident[:, :])
                    mm.then_inc(s_xTps, 1)
                    for j in range(G):
                        mm = pe.transpose(bank[0:CR, 1, j * P:(j + 1) * P], x[b][:, j, P:C], K.ident[:, :])
                    mm.then_inc(s_xTps, 1)

                def first(i, b):
                    s = i * 2 + b
                    pe.wait_ge(s_w[b], i * 80 + 80)
                    pe.wait_ge(s_xT, s * 2 + 2)
                    for m in range(HK):
                        if m >= 3 or not (isinstance(i, int) and i == 0 and b == 0):
                            pe.wait_ge(s_gelu, s * HK + m - 2)
                        o = bank[:, 2 + m % 3, :]
                        ms = slice(m * P, (m + 1) * P)
                        pe.matmul(o, w1a[b][:, ms], xTa[b][:, :], start=True, stop=False)
                        pe.matmul(o, w1b[b][:, ms], xTb[b][:, :], start=False, stop=True).then_inc(s_h, 1)

                def second(i, b):
                    s = i * 2 + b
                    pe.wait_ge(s_gelu, s * HK + HK)
                    for j in range(G):
                        if j >= 2 or not (isinstance(i, int) and i == 0 and b == 0):
                            pe.wait_ge(s_y, s * G + j - 1)
                        for m in range(HK):
                            mm = pe.matmul(bank[:, YB[j % 2], 0:C], h[b][:, m, j * P:(j + 1) * P], w2[b][:, m, :],
                                           start=(m == 0), stop=(m == HK - 1))
                        mm.then_inc(s_yps, 1)

                pe.wait_ge(s_ones, 2)
                transposes(0, 0)
                first(0, 0)
                transposes(0, 1)
                second(0, 0)
                with pe.Fori(1, NT // 2) as i:
                    first(i - 1, 1)
                    transposes(i, 0)
                    second(i - 1, 1)
                    first(i, 0)
                    transposes(i, 1)
                    second(i, 0)
                first(NT // 2 - 1, 1)
                if NT % 2:
                    transposes(NT // 2, 0)
                second(NT // 2 - 1, 1)
                if NT % 2:
                    first(NT // 2, 0)
                    second(NT // 2, 0)


def combine(nc, name, H, top, wgt, Y, out):
    with Phase(nc) as ctx:
        sb = lambda n, s, dt=F32: ctx.enter_context(nc.sbuf_tensor(f"{name}c_{n}", s, dt))
        sem = lambda n: ctx.sem(f"{name}c_{n}")
        yg = [sb(f"yg{b}", [P, G, top, C]) for b in range(2)]
        s_add, stored = sem("added"), sem("stored")
        s_in = [sem(f"rows_in{b}") for b in range(2)]
        adds = top * G
        rows = out.rearrange("(t p) c -> p t c", p=P)
        Yv = Y[0:top * B * P, :].rearrange("(t p k) c -> p t (k c)", p=P, k=top)

        with nc.Block() as block:
            @block.sync
            def _(sp):
                def load(g, b):
                    sp.dma_start(yg[b][:, :, :, :].rearrange("p j k c -> p j (k c)"), Yv[:, bass.ds(g * G, G), :]).then_inc(s_in[b], 16)

                def groups(i, more):
                    for b in range(2):
                        g = i * 2 + b
                        sp.wait_ge(s_add, g * adds + adds)
                        part = bass.ds(g * G, G)
                        sp.dma_start(rows[:, part, :], H[:, part, :]).then_inc(stored, 16)
                        if more:
                            load(g + 2, b)
                for b in range(2):
                    load(b, b)
                with sp.Fori(0, NG // 2 - 1) as i:
                    groups(i, True)
                groups(NG // 2 - 1, False)
                sp.wait_ge(stored, 16 * NG)

            @block.vector
            def _(dve):
                def add(i, b):
                    g = i * 2 + b
                    dve.wait_ge(s_in[b], i * 16 + 16)
                    for k in range(top):
                        for j in range(G):
                            hs = H[:, bass.ds(g * G + j, 1), :].rearrange("p a c -> p (a c)")
                            if k:
                                dve.wait_ge(s_add, g * adds + j + 1)
                            dve.scalar_tensor_tensor(hs, yg[b][:, j, k, :], wgt[:, k, bass.ds(g * G + j, 1)], hs,
                                                     ALU.mult, ALU.add).then_inc(s_add, 1)
                for b in range(2):
                    add(0, b)
                with dve.Fori(1, NG // 2) as i:
                    for b in range(2):
                        add(i, b)


def mamba_phase(nc, A, H, bank, K, pos_i, Y):
    with Phase(nc) as ctx:
        sb = lambda n, s, dt=F32: ctx.enter_context(nc.sbuf_tensor(f"m_{n}", s, dt))
        sem = lambda n: ctx.sem(f"m_{n}")
        two = range(2)
        DC, NS, TAPS, R = 3, 16, 4, 12
        BC = 2 * NS
        MID, LO, HI, DT = 0, BC, 2 * BC, 3 * BC
        PW = P + 2 * (TAPS - 1)
        L1 = P + 1
        FL = DC * G * L1
        win_a, win_b = sb("win_a", [P, 2 * DC * P]), sb("win_b", [CR, 2 * DC * P])
        cw, cb = sb("cw", [P, DC, TAPS]), sb("cb", [P, DC])
        wx, wdt = sb("wx", [P, DC, DT + R]), sb("wdt", [DT + R, DC * P])
        bdt, Ac, Dp = sb("bdt", [P, DC]), sb("Ac", [P, DC, NS]), sb("Dp", [P, DC])
        wo = sb("wo", [P, DC, C])
        zTa, zTb = sb("zTa", [P, TOK]), sb("zTb", [CR, TOK])
        xp = sb("xp", [P, DC, G, PW])
        dg = sb("dg", [P, DC, TAPS, P])
        E3 = sb("E3", [DT, BC], BF16)
        z = sb("z", [P, G, C])
        idx = sb("idx", [P, G], I32)
        xc = [sb(f"xc{d}", [P, DC, TOK]) for d in two]
        pdt = sb("pdt", [DT + R, TOK])
        rem = pdt[0:HI, :]
        parts = [sb(f"parts{d}", [DT, TOK], BF16) for d in two]
        r = sb("r", [P, DC, TOK])
        dt = [sb(f"dt{d}", [P, DC, TOK]) for d in two]
        u = [sb(f"u{d}", [P, DC, TOK]) for d in two]
        e, w1 = dt, u
        gz = sb("gz", [P, DC, TOK])
        ys = sb("ys", [P, DC, TOK])
        Bs = [sb(f"Bs{b}", [P, TOK]) for b in two]
        dA = [sb(f"dA{b}", [P, FL + 1]) for b in two]
        dBx = [sb(f"dBx{b}", [P, FL + 1]) for b in two]
        h = [sb(f"h{b}", [P, FL + 1]) for b in two]
        NPR = 4
        pr = [sb(f"pr{b}", [P, DC, TOK]) for b in range(NPR)]
        ln = LayerNorm(nc, ctx, "m_ln", 1e-5, K)
        loaded, s_Ac = sem("loaded"), sem("A_ready")
        s_z, s_zTps, s_zT = sem("z_ready"), sem("zTps_ready"), sem("zT_ready")
        s_xps, s_xp, s_zps, s_zc, s_gz = sem("xps_ready"), sem("xp_ready"), sem("zps_ready"), sem("z_copied"), sem("gate_ready")
        s_cvps, s_cv, s_xc, s_pjps, s_part = (sem(n) for n in ("convps_ready", "conv_ready", "xc_ready", "pjps_ready", "part_steps"))
        s_pdt, s_rem, s_lo = sem("pdt_ready"), sem("rem_ready"), sem("lo_ready")
        s_dtps, s_abs, s_e, s_w1, s_ln, s_nc, s_sp = (sem(n) for n in ("dtps_ready", "abs_ready", "e_ready", "e1_ready", "ln_ready", "corr_ready", "dt_ready"))
        s_er, s_dBv, s_dg = sem("r_plus_e_ready"), sem("dBx_by_dve"), sem("E3_steps")
        s_u, s_xs = sem("u_ready"), sem("xs_ready")
        s_idx, s_got, s_added = sem("idx_ready"), *ctx.software(K, 1), sem("rows_added")
        s_Bps, s_B, s_Cps, s_dA, s_dBx, s_h, s_pr, s_red = (
            sem(n) for n in ("Bps_ready", "B_ready", "Cps_ready", "dA_ready", "dBx_ready", "h_ready", "readout_ready", "summed"))
        s_ys, s_gy, s_ops, s_out = sem("y_ready"), sem("gated_ready"), sem("outps_ready"), sem("res_ready")

        def data(t):
            return t[:, 0:FL].rearrange("p (c b t) -> p c b t", c=DC, b=G)[:, :, :, 1:L1]

        def seqs(t):
            return t[:, :, :].rearrange("p c (b t) -> p c b t", b=G)

        with nc.Block() as block:
            @block.sync
            def _(sp):
                for dst, src in (
                    (win_a[:, :], A["m_WinT"][0:P, :]), (win_b[:, :], A["m_WinT"][P:C, :]),
                    (cw[:, :, :], A["m_conv_w"].rearrange("(c p) k -> p c k", p=P)),
                    (cb[:, :], A["m_conv_b"]),
                    *((wx[:, :, o:o + BC], A["m_WxT"][:, R:R + BC].rearrange("(c p) r -> p c r", p=P)) for o in (MID, LO, HI)),
                    (wx[:, :, DT:DT + R], A["m_WxT"][:, 0:R].rearrange("(c p) r -> p c r", p=P)),
                    (wdt[DT:DT + R, :], A["m_WdtT"]), (bdt[:, :], A["m_b_dt"]),
                    (Ac[:, :, :], A["m_A_log"].rearrange("(c p) n -> p c n", p=P)),
                    (Dp[:, :], A["m_D"]),
                    (wo[:, :, :], A["m_WoutT"].rearrange("(c p) n -> p c n", p=P)),
                ):
                    sp.dma_start(dst, src).then_inc(loaded, 16)

            @block.scalar
            def _(act):
                act.wait_ge(loaded, 16 * 13)
                act.activation(Ac[:, :, :], Ac[:, :, :], ACT.Exp).then_inc(s_Ac, 1)

            @block.vector
            def _(dve):
                for b in two:
                    dve.memset(dA[b][:, :], 0.0)
                    dve.memset(dBx[b][:, :], 0.0)
                dve.memset(xp[:, :, :, :], 0.0)
                dve.wait_ge(loaded, 16 * 13)
                for c in range(DC):
                    for k in range(TAPS):
                        dve.tensor_scalar(dg[:, c, k, :], K.ident[:, :], cw[:, c, k:k + 1], None, ALU.mult)
                dve.wait_ge(s_Ac, 1)
                dve.tensor_scalar(Ac[:, :, :], Ac[:, :, :], -1.0, None, ALU.mult)

            @block.gpsimd
            def _(pool):
                pool.memset(E3[:, :], 0.0).then_inc(s_dg, 1)
                for i, o in enumerate((MID, LO, HI)):
                    pool.wait_ge(s_dg, i + 1)
                    pool.affine_select(out=E3[o:o + BC, :], in_=E3[o:o + BC, :], compare_op=ALU.not_equal, fill=1.0,
                                       base=0, pattern=[[-1, BC]], channel_multiplier=1).then_inc(s_dg, 1)

        def chain(g, d, norm=True, first=False):
            q = g * 2 + d
            static = isinstance(g, int)
            gl = g + d
            hh = lambda j: H[:, bass.ds(gl * G + j, 1), :].rearrange("p a c -> p (a c)")

            def pe_conv(pe, c):
                i = q * DC + c
                s_used = s_xp if d == 0 else s_zc
                if c == 0:
                    pe.wait_ge(s_used, g * DC + 2)
                elif c == 1:
                    pe.wait_ge(s_used, g * DC + 3)
                else:
                    pe.wait_ge(s_cv, q * DC + 1)
                for k in range(TAPS):
                    o = k if d == 0 else 2 * (TAPS - 1) - k
                    mm = pe.matmul(bank[:, 7 - c % 2, :], dg[:, c, k, :], xp[:, c, :, o:o + P], start=(k == 0), stop=(k == TAPS - 1))
                mm.then_inc(s_cvps, 1)

            def act_conv(act, c):
                act.wait_ge(s_cvps, q * DC + c + 1)
                if c == 0 and (not static or g > 0):
                    act.wait_ge(s_xs, g)
                    act.wait_ge(s_u, q - 1)
                act.activation(xc[d][:, c, :], bank[:, 7 - c % 2, :], ACT.Identity, bias=cb[:, c:c + 1]).then_inc(s_cv, 1)

            def act_xc(act):
                act.wait_ge(s_cv, q * DC + DC)
                act.activation(xc[d][:, :, :], xc[d][:, :, :], ACT.Silu).then_inc(s_xc, 1)
                if d == 1:
                    act.wait_ge(s_zc, g * DC + DC)
                    act.activation(gz[:, :, :], gz[:, :, :], ACT.Silu).then_inc(s_gz, 1)

            def pe_proj(pe):
                pe.wait_ge(s_xc, q + 1)
                for c in range(DC):
                    mm = pe.matmul(bank[0:DT + R, 6, :], wx[:, c, :], xc[d][:, c, :], start=(c == 0), stop=(c == DC - 1))
                mm.then_inc(s_pjps, 1)

            def act_parts(act):
                act.wait_ge(s_pjps, q + 1)
                if not static or q > 0:
                    act.wait_ge(s_dtps, q * DC)
                act.copy(pdt[DT:DT + R, :], bank[DT:DT + R, 6, :]).then_inc(s_pdt, 1)
                if not static or g > 0:
                    act.wait_ge(s_Cps, (q - 1) * NS)
                act.copy(parts[d][:, :], bank[0:DT, 6, :]).then_inc(s_part, 1)

            def dve_rem(dve):
                dve.wait_ge(s_part, q * 2 + 1)
                dve.tensor_tensor(rem, bank[0:HI, 6, :], parts[d][0:HI, :], ALU.subtract).then_inc(s_rem, 1)

            def act_mid(act):
                act.wait_ge(s_rem, q + 1)
                act.copy(parts[d][0:HI, :], rem).then_inc(s_part, 1)

            def dve_lo(dve):
                dve.wait_ge(s_part, q * 2 + 2)
                v = parts[d][LO:HI, :]
                dve.tensor_tensor(v, pdt[LO:HI, :], v, ALU.subtract).then_inc(s_lo, 1)

            def pe_dt(pe, c):
                if c == 0:
                    pe.wait_ge(s_pdt, q + 1)
                elif c == 1:
                    pe.wait_ge(s_rem, q + 1)
                    pe.wait_ge(s_part, q * 2 + 1)
                else:
                    pe.wait_ge(s_abs, q * 2 * DC + 2)
                pe.matmul(bank[:, 7 - c % 2, :], wdt[DT:DT + R, c * P:(c + 1) * P], pdt[DT:DT + R, :], start=True, stop=True).then_inc(s_dtps, 1)

            def act_abs(act, c):
                act.wait_ge(s_dtps, q * DC + c + 1)
                if c == 0 and (not static or q > 0):
                    act.wait_ge(s_sp, q)
                if c == 0 and (not static or g > 0):
                    act.wait_ge(s_dA, (q - 1) * NS)
                act.activation(e[d][:, c, :], bank[:, 7 - c % 2, :], ACT.Abs, bias=bdt[:, c:c + 1]).then_inc(s_abs, 1)
                act.activation(r[:, c, :], bank[:, 7 - c % 2, :], ACT.Relu, bias=bdt[:, c:c + 1]).then_inc(s_abs, 1)

            def act_e(act):
                act.wait_ge(s_abs, (q + 1) * 2 * DC)
                act.activation(e[d][:, :, :], e[d][:, :, :], ACT.Exp, scale=-1.0).then_inc(s_e, 1)
                act.wait_ge(s_e, q + 1)
                if not static or g > 0:
                    wait_dBx(act, g - 1, d, NS - 1)
                    wait_dBx(act, g - 1, d, BY_DVE[-1])
                act.activation(w1[d][:, :, :], e[d][:, :, :], ACT.Identity, bias=K.ones[:, 0:1]).then_inc(s_w1, 1)

            def act_ln(act):
                act.wait_ge(s_w1, q + 1)
                act.wait_ge(s_er, q + 1)
                act.activation(dt[d][:, :, :], w1[d][:, :, :], ACT.Ln).then_inc(s_ln, 1)

            def pool_er(pool):
                pool.wait_ge(s_e, q + 1)
                pool.tensor_tensor(r[:, :, :], r[:, :, :], e[d][:, :, :], ALU.add).then_inc(s_er, 1)

            def dve_dt(dve):
                dve.wait_ge(s_ln, q + 1)
                dve.scalar_tensor_tensor(w1[d][:, :, :], w1[d][:, :, :], -1.0, dt[d][:, :, :], ALU.add, ALU.subtract).then_inc(s_nc, 1)
                dve.wait_ge(s_nc, q + 1)
                dve.wait_ge(s_er, q + 1)
                dve.tensor_tensor(dt[d][:, :, :], r[:, :, :], w1[d][:, :, :], ALU.subtract).then_inc(s_sp, 1)

            def dve_u(dve):
                dve.wait_ge(s_sp, q + 1)
                dve.tensor_tensor(u[d][:, :, :], dt[d][:, :, :], xc[d][:, :, :], ALU.mult).then_inc(s_u, 1)

            def pool_rows(pool):
                if not first:
                    pool.wait_ge(s_zTps, gl * 2)
                pool.tensor_copy(idx[:, :], pos_i[:, 0, bass.ds(gl * G, G)]).then_inc(s_idx, 1)
                pool.wait_ge(s_idx, gl + 1)
                stand_alone(pool, K.go)
                for j in range(G):
                    pool.indirect_dma_start(z[:, j, :], None, Y,
                                            bass.IndirectOffsetOnAxis(idx[:, j:j + 1].bitcast(U32), 0)).then_inc(s_got, 16)

            def dve_rows(dve):
                hs = H[:, bass.ds(gl * G, G), :]
                dve.wait_ge(s_got, (gl + 1) * 16 * G)
                dve.tensor_tensor(hs, hs, z[:, :, :], ALU.add).then_inc(s_added, 1)

            def dve_stats(dve):
                dve.wait_ge(s_added, gl + 1)
                stand_alone(dve, K.go)
                ln.stats(dve, gl, hh)

            def dve_norm(dve):
                ln.normalise(dve, gl, hh, lambda j: z[:, j, :], s_z)

            def pe_zT(pe):
                pe.wait_ge(s_z, gl * G + G)
                if not first:
                    pe.wait_ge(s_abs, (q + 1) * 2 * DC)
                for j in range(G):
                    mm = pe.transpose(bank[:, 6, j * P:(j + 1) * P], z[:, j, 0:P], K.ident[:, :])
                mm.then_inc(s_zTps, 1)
                for j in range(G):
                    mm = pe.transpose(bank[0:CR, 7, j * P:(j + 1) * P], z[:, j, P:C], K.ident[:, :])
                mm.then_inc(s_zTps, 1)

            def act_zT(act):
                if not first:
                    act.wait_ge(s_zps, gl * DC)
                act.wait_ge(s_zTps, gl * 2 + 1)
                act.copy(zTa[:, :], bank[:, 6, :]).then_inc(s_zT, 1)
                act.wait_ge(s_zTps, gl * 2 + 2)
                act.copy(zTb[:, :], bank[0:CR, 7, :]).then_inc(s_zT, 1)

            def pe_in(pe, c):
                s_ps, s_used = (s_xps, s_xp) if d == 0 else (s_zps, s_zc)
                if c == 0:
                    pe.wait_ge(s_zT, g * 2 + 2)
                    if d == 1:
                        pe.wait_ge(s_abs, q * 2 * DC)
                if c == 2:
                    pe.wait_ge(s_used, g * DC + 1)
                m = slice((d * DC + c) * P, (d * DC + c + 1) * P)
                o = bank[:, 6 + c % 2, :]
                pe.matmul(o, win_a[:, m], zTa[:, :], start=True, stop=False)
                pe.matmul(o, win_b[:, m], zTb[:, :], start=False, stop=True).then_inc(s_ps, 1)

            def act_in(act, c):
                v = bank[:, 6 + c % 2, :]
                if d == 0:
                    act.wait_ge(s_xps, g * DC + c + 1)
                    if c == 0 and (not static or g > 0):
                        act.wait_ge(s_cvps, g * 2 * DC)
                    act.copy(xp[:, c, :, TAPS - 1:TAPS - 1 + P], v.rearrange("p (b t) -> p b t", b=G)).then_inc(s_xp, 1)
                else:
                    act.wait_ge(s_zps, g * DC + c + 1)
                    if c == 0 and (not static or g > 0):
                        act.wait_ge(s_gy, g)
                    act.copy(gz[:, c, :], v).then_inc(s_zc, 1)

            def pool_xs(pool):
                pool.wait_ge(s_xc, q + 1)
                if not static or g > 0:
                    pool.wait_ge(s_ops, g * 2)
                pool.tensor_tensor(ys[:, :, :], xc[0][:, :, :], xc[1][:, :, :], ALU.add).then_inc(s_xs, 1)

            W = {"pe": [], "act": [], "dve": [], "pool": []}
            def put(eng, unit, f, *a):
                W[eng].append((unit, f, a))

            if norm and (d == 1 or first):
                at = -8 if first else 8
                put("pool", -10 if first else 1, pool_rows)
                put("dve", at - 1, dve_rows)
                put("dve", at, dve_stats)
                put("pool", at + 1, lambda pool: ln.rstd(pool, gl))
                put("dve", at + 2, dve_norm)
                put("pe", at + 6, pe_zT)
            if d == 0:
                put("act", 0, act_zT)
            put("pe", 0, pe_in, 0); put("pe", 0, pe_in, 1)
            put("act", 2, act_in, 0); put("act", 2, act_in, 1)
            put("pe", 2, pe_in, 2); put("pe", 3, pe_conv, 0)
            put("act", 4, act_in, 2); put("act", 5, act_conv, 0)
            put("pe", 4, pe_conv, 1); put("pe", 5, pe_conv, 2)
            put("act", 6, act_conv, 1); put("act", 7, act_conv, 2); put("act", 7, act_xc)
            put("pe", 7, pe_proj)
            put("act", 9, act_parts)
            put("dve", 9, dve_rem)
            put("pe", 9, pe_dt, 0)
            put("act", 11, act_mid); put("act", 11, act_abs, 0)
            put("dve", 11, dve_lo)
            put("pe", 11, pe_dt, 1); put("pe", 11, pe_dt, 2)
            put("act", 13, act_abs, 1); put("act", 13, act_abs, 2); put("act", 13, act_e)
            put("act", 14, act_ln)
            put("pool", 13, pool_er)
            put("dve", 14, dve_dt)
            put("dve", 14, dve_u)
            if d == 1:
                put("pool", 8, pool_xs)
            return W

        BY_DVE = (0, 14)
        by_dve = lambda n: sum(k <= n for k in BY_DVE)

        def ahead(g, d, n, k):
            n, d = (n + k) % NS, d + (n + k) // NS
            return g + d // 2, d % 2, n

        def first_two(g, d, n):
            return isinstance(g, int) and g == 0 and d == 0 and n < 2

        def wait_dBx(eng, g, d, n):
            q = g * 2 + d
            if n in BY_DVE:
                eng.wait_ge(s_dBv, q * len(BY_DVE) + by_dve(n))
            else:
                eng.wait_ge(s_dBx, q * (NS - len(BY_DVE)) + n + 1 - by_dve(n))

        def wait_dBx_before(eng, g, d, n, k):
            wait_dBx(eng, *ahead(g, d, n, -k))

        def pe_B(pe, g, d, n):
            N = (g * 2 + d) * NS + n
            if n == 0:
                pe.wait_ge(s_lo, g * 2 + d + 1)
            if not first_two(g, d, n) or n > 0:
                pe.wait_ge(s_B, N)
            pe.matmul(bank[:, 5, :], E3[:, n:n + 1].to_broadcast([DT, P]), parts[d][:, :], start=True, stop=True).then_inc(s_Bps, 1)

        def pe_C(pe, g, d, n):
            N = (g * 2 + d) * NS + n
            if not first_two(g, d, n):
                pe.wait_ge(s_pr, N - 1)
            pe.matmul(bank[:, 3 + n % 2, :], E3[:, NS + n:NS + n + 1].to_broadcast([DT, P]), parts[d][:, :],
                      start=True, stop=True).then_inc(s_Cps, 1)

        def pe_sum(pe, g, d, n):
            N = (g * 2 + d) * NS + n
            pe.wait_ge(s_pr, N + 1)
            if d == 0 and n == 0 and (not isinstance(g, int) or g > 0):
                pe.wait_ge(s_out, g * 2)
            for c in range(DC):
                mm = pe.matmul(bank[:, c, :], K.ident[:, :], pr[n % NPR][:, c, :], start=(d == 0 and n == 0),
                               stop=(d == 1 and n == NS - 1))
            mm.then_inc(s_red, 1)

        def act_B(act, g, d, n):
            act.wait_ge(s_Bps, (g * 2 + d) * NS + n + 1)
            if not first_two(g, d, n):
                wait_dBx_before(act, g, d, n, 2)
            act.copy(Bs[n % 2][:, :], bank[:, 5, :]).then_inc(s_B, 1)

        def act_decay(act, g, d, n):
            N = (g * 2 + d) * NS + n
            if n == 0:
                act.wait_ge(s_sp, g * 2 + d + 1)
            if not first_two(g, d, n):
                act.wait_ge(s_h, N - 1)
            for c in range(DC):
                ins = act.activation(data(dA[n % 2])[:, c, :, :], seqs(dt[d])[:, c, :, :], ACT.Exp, scale=Ac[:, c, n:n + 1])
            ins.then_inc(s_dA, 1)

        def make_dBx(eng, g, d, n, done):
            N = (g * 2 + d) * NS + n
            if n < 2:
                eng.wait_ge(s_u, g * 2 + d + 1)
            eng.wait_ge(s_B, N + 1)
            if not first_two(g, d, n):
                eng.wait_ge(s_h, N - 1)
            bb = Bs[n % 2][:, :].rearrange("p (b t) -> p b t", b=G).unsqueeze(1).to_broadcast([P, DC, G, P])
            eng.tensor_tensor(data(dBx[n % 2]), seqs(u[d]), bb, ALU.mult).then_inc(done, 1)

        def dve_scan(dve, g, d, n):
            N = (g * 2 + d) * NS + n
            dve.wait_ge(s_dA, N + 1)
            wait_dBx(dve, g, d, n)
            if not first_two(g, d, n):
                dve.wait_ge(s_pr, N - 1)
            b = n % 2
            v = (lambda t: t[:, 0:FL]) if d == 0 else (lambda t: t[:, FL:0:-1])
            dve.tensor_tensor_scan(v(h[b]), v(dA[b]), v(dBx[b]), 0.0, ALU.mult, ALU.add).then_inc(s_h, 1)

        def dve_read(dve, g, d, n):
            N = (g * 2 + d) * NS + n
            early = isinstance(g, int) and g == 0 and d == 0 and n < NPR
            dve.wait_ge(s_h, N + 1)
            dve.wait_ge(s_Cps, N + 1)
            if not early:
                dve.wait_ge(s_red, N - NPR + 1)
            cc = bank[:, 3 + n % 2, :].rearrange("p (b t) -> p b t", b=G).unsqueeze(1).to_broadcast([P, DC, G, P])
            dve.tensor_tensor(seqs(pr[n % NPR]), data(h[n % 2]), cc, ALU.mult).then_inc(s_pr, 1)

        def dve_y(dve, g):
            dve.wait_ge(s_xs, g + 1)
            dve.wait_ge(s_red, (g + 1) * 2 * NS)
            for c in range(DC):
                dve.scalar_tensor_tensor(ys[:, c, :], ys[:, c, :], Dp[:, c:c + 1], bank[:, c, :], ALU.mult,
                                         ALU.add).then_inc(s_ys, 1)
            dve.wait_ge(s_ys, g * DC + DC)
            dve.wait_ge(s_gz, g + 1)
            dve.tensor_tensor(ys[:, :, :], ys[:, :, :], gz[:, :, :], ALU.mult).then_inc(s_gy, 1)

        def pe_out(pe, g):
            pe.wait_ge(s_gy, g + 1)
            for j in range(G):
                for c in range(DC):
                    mm = pe.matmul(bank[:, j // 2, (j % 2) * C:(j % 2 + 1) * C], ys[:, c, j * P:(j + 1) * P],
                                   wo[:, c, :], start=(c == 0), stop=(c == DC - 1))
                if j % 2:
                    mm.then_inc(s_ops, 1)

        def dve_out(dve, g):
            for b in two:
                dve.wait_ge(s_ops, g * 2 + b + 1)
                hs = H[:, bass.ds(g * G + 2 * b, 2), :]
                dve.scalar_tensor_tensor(hs, bank[:, b, 0:2 * C].rearrange("p (j c) -> p j c", j=2), 0.5, hs,
                                         ALU.mult, ALU.add).then_inc(s_out, 1)

        def in_order(steps):
            return sorted(steps, key=lambda s: s[0])

        def slot(eng, name, g, d, steps, main, last):
            pend = in_order(steps)
            for n in range(NS):
                now = [s for s in pend if s[0] == n]
                pend = pend[len(now):]
                main(eng, g, d, n, last and d == 1, lambda: [f(eng, *a) for _, f, a in now])
            assert not pend

        def program(eng, name, main, before, after):
            for _, f, a in in_order(chain(0, 0, first=True)[name]):
                f(eng, *a)
            before(eng)

            def group(g, last):
                slot(eng, name, g, 0, chain(g, 1, norm=not last)[name], main, last)
                slot(eng, name, g, 1, [] if last else chain(g + 1, 0)[name], main, last)

            group(0, False)
            with eng.Fori(1, NG - 1) as g:
                group(g, False)
            group(NG - 1, True)
            after(eng)

        def nothing(*a):
            pass

        def very_first(g, d, n):
            return isinstance(g, int) and (g, d, n) == (0, 0, 0)

        def after_group(g, d):
            return d == 0 and (not isinstance(g, int) or g > 0)

        LAST = (NG - 1, 1, NS - 1)
        SUMS = {3: (), 4: (), 5: (2,), 6: (3, 4), 7: (5,), 8: (6, 7)}
        AFTER = {**SUMS, 2: (0,), 3: (1,)}
        with nc.Block() as block:
            @block.tensor
            def _(pe):
                def main(pe, g, d, n, end, prepare):
                    if not (end and n >= NS - 3):
                        pe_B(pe, *ahead(g, d, n, 3))
                    prepare()
                    if not (end and n >= NS - 1):
                        pe_C(pe, *ahead(g, d, n, 1))
                    if after_group(g, d) and n == 1:
                        pe_out(pe, g - 1)
                    elif not very_first(g, d, n):
                        for k in (AFTER if after_group(g, d) else SUMS).get(n, (n - 1,)):
                            pe_sum(pe, *ahead(g, d, k, 0))

                def before(pe):
                    for n in range(3):
                        pe_B(pe, 0, 0, n)
                    pe_C(pe, 0, 0, 0)

                def after(pe):
                    pe_sum(pe, *LAST)
                    pe_out(pe, NG - 1)
                program(pe, "pe", main, before, after)

            @block.scalar
            def _(act):
                def main(act, g, d, n, end, prepare):
                    act_decay(act, g, d, n)
                    if not (end and n >= NS - 1):
                        act_B(act, *ahead(g, d, n, 1))
                    prepare()
                program(act, "act", main, lambda act: act_B(act, 0, 0, 0), nothing)

            @block.gpsimd
            def _(pool):
                def main(pool, g, d, n, end, prepare):
                    if n not in BY_DVE:
                        make_dBx(pool, g, d, n, s_dBx)
                    prepare()
                program(pool, "pool", main, nothing, nothing)

            @block.vector
            def _(dve):
                def main(dve, g, d, n, end, prepare):
                    dve_scan(dve, g, d, n)
                    if not very_first(g, d, n):
                        dve_read(dve, *ahead(g, d, n, -1))
                    if after_group(g, d) and n == 1:
                        dve_y(dve, g - 1)
                    if (n + 1) % NS in BY_DVE and not (end and n == NS - 1):
                        make_dBx(dve, *ahead(g, d, n, 1), s_dBv)
                    if after_group(g, d) and n == 2:
                        dve_out(dve, g - 1)
                    prepare()

                def before(dve):
                    make_dBx(dve, 0, 0, 0, s_dBv)

                def after(dve):
                    dve_read(dve, *LAST)
                    dve_y(dve, NG - 1)
                    dve_out(dve, NG - 1)
                program(dve, "dve", main, before, after)


def tower(nc, A, out):
    with Phase(nc) as ctx:
        H = ctx.enter_context(nc.sbuf_tensor("H", [P, B, C], F32))
        bank = ctx.enter_context(nc.psum_tensor("bank", [P, 8, 512], F32))
        K = constants(nc, ctx, A)
        n0, n1 = expert_tiles_of(E0, 1) * TOK, expert_tiles_of(E1, 2) * TOK
        X0 = nc.dram_tensor("slots_x0", (n0, C), F32).ap()
        Y0 = nc.dram_tensor("slots_y0", (n0, C), F32).ap()
        X1 = nc.dram_tensor("slots_x1", (n1, C + 1), F32).ap()
        Y1 = nc.dram_tensor("rows_y1", (2 * B * P + SPARE, C), F32).ap()
        attention_phase(nc, A, H, bank, K, X0, X1)
        with Phase(nc) as first:
            pos_i = first.enter_context(nc.sbuf_tensor("f0_pos_i", [P, 1, B], I32))
            expert_phase(nc, "f0", A, H, bank, K, E0, 1, "f0_center", X0, Y0, pos_i)
            mamba_phase(nc, A, H, bank, K, pos_i, Y0)
        expert_phase(nc, "f1", A, H, bank, K, E1, 2, None, X1, Y1, None, out)


def layout(inputs):
    import numpy as np
    g = lambda n: np.asarray(inputs[n])
    c = np.ascontiguousarray
    return {
        "ids_wordT": c(g("x").T), "ids_posi": c(g("itok_BS_0_511").reshape(-1)),
        "ids_demo": c(g("itok_BS_0_255").reshape(-1)), "ids_seg": c(g("mask_BS_i1_0").reshape(-1)),
        "word_table": c(g("L0_tok_word_table")), "demo_table": c(g("L0_tok_demo_table")),
        "posi_table": c(g("L0_tok_posi_table")), "seg_table": c(g("L0_tok_seg_table")),
        "ln_gamma": c(g("L0_tok_ln_gamma")), "ln_beta": c(g("L0_tok_ln_beta")),
        "WqkvT": c(g("L0_attn_Wqkv_w").T), "bqkv": c(g("L0_attn_Wqkv_b").reshape(1, -1)),
        "WprojT": c(g("L0_attn_Wproj_w").T), "bproj": c(g("L0_attn_Wproj_b").reshape(1, -1)),
        "f0_gate": c(g("L0_ffn_gate_w")), "f0_gate_b": c(g("L0_ffn_gate_b").reshape(1, -1)),
        "f0_center": c(g("L0_ffn_gate_center")),
        "f0_w1": c(g("L0_ffn_w1")), "f0_b1": c(g("L0_ffn_b1")), "f0_w2": c(g("L0_ffn_w2")), "f0_b2": c(g("L0_ffn_b2")),
        "m_WinT": c(g("L1_attn_W_in").T), "m_conv_w": c(g("L1_attn_conv_w")), "m_conv_b": c(g("L1_attn_conv_b").reshape(-1, P).T),
        "m_WxT": c(g("L1_attn_W_xproj").T), "m_WdtT": c(g("L1_attn_W_dt").T), "m_b_dt": c(g("L1_attn_b_dt").reshape(-1, P).T),
        "m_A_log": c(g("L1_attn_A_log")), "m_D": c(g("L1_attn_D_param").reshape(-1, P).T), "m_WoutT": c(g("L1_attn_W_out").T),
        "f1_gate": c(g("L1_ffn_router_w")), "f1_gate_b": c(g("L1_ffn_router_b").reshape(1, -1)),
        "f1_w1": c(g("L1_ffn_w1")), "f1_b1": c(g("L1_ffn_b1")), "f1_w2": c(g("L1_ffn_w2")), "f1_b2": c(g("L1_ffn_b2")),
    }


def kernel(**inputs):
    import numpy as np
    import concourse.bacc as bacc
    from concourse.bass_utils import run_bass_kernel_spmd

    nc = bacc.Bacc("TRN2", target_bir_lowering=False, num_devices=1)
    arrays = layout(inputs)
    A = {n: nc.dram_tensor(n, a.shape, mybir.dt.from_np(a.dtype), kind="ExternalInput").ap() for n, a in arrays.items()}
    out = nc.dram_tensor("out", (B * P, C), F32, kind="ExternalOutput").ap()
    tower(nc, A, out)
    r = run_bass_kernel_spmd(nc, [arrays], core_ids=[0])
    return r.results[0]["out"].reshape(B, P, C)
```
